# Optimizing a Trainium2 kernel written in Bass

```python
import numpy as np
import jax
import jax.numpy as jnp

def _softmax(x, axis=-1):
    return jax.nn.softmax(x, axis=axis)

def _gelu(x):
    return jax.nn.gelu(x, approximate=True)

def _silu(x):
    return jax.nn.silu(x)

def _sigmoid(x):
    return jax.nn.sigmoid(x)

def _layernorm(x, axis=-1, eps=1e-05):
    m = jnp.mean(x, axis=axis, keepdims=True)
    v = jnp.var(x, axis=axis, keepdims=True)
    return (x - m) / jnp.sqrt(v + eps)

def _scatter_add(tgt, idx, src, axis=0):
    return tgt.at[idx].add(src)

def _segment_sum(src, seg, n):
    return jax.ops.segment_sum(src, seg, n)
kernel_name = 'mk_adaln_attn_ffn_d2_seqx_r8_2f8465'

def setup_inputs(seed: int=0):
    np.random.seed(seed)
    _w = jnp.asarray

    def _rec_inputs():
        import jax
        import jax.numpy as jnp
        _rk = jax.random.key(seed)
        x = -0.0003929 + 0.9999 * jax.random.normal(jax.random.fold_in(_rk, 1), (16, 128, 128), jnp.float32)
        _lenS = 128 - jax.random.randint(jax.random.fold_in(_rk, 7), (16,), 0, max(1, 128 // 4) + 1, jnp.int32)
        _lenS2 = 128 - jax.random.randint(jax.random.fold_in(_rk, 8), (16,), 0, max(1, 128 // 4) + 1, jnp.int32)
        itok_B_0_7 = jax.random.randint(jax.random.fold_in(_rk, 11), (16,), 0, 8, jnp.int32)
        fside_Bx2_0 = -2.90419 + 8.51931 * jax.random.normal(jax.random.fold_in(_rk, 12), (16, 2), jnp.float32)
        condB_angle = 0.0111926 + 0.196324 * jax.random.normal(jax.random.fold_in(_rk, 13), (16,), jnp.float32)
        condB_zX = jax.random.uniform(jax.random.fold_in(_rk, 14), (16,), jnp.float32, 0.0, 0.983423)
        condB_zY = jax.random.uniform(jax.random.fold_in(_rk, 15), (16,), jnp.float32, 0.0, 0.979075)
        condB_zR = jax.random.uniform(jax.random.fold_in(_rk, 16), (16,), jnp.float32, 0.0, 0.9968)
        itok_B_0_2 = jax.random.randint(jax.random.fold_in(_rk, 17), (16,), 0, 3, jnp.int32)
        return (x, itok_B_0_7, fside_Bx2_0, condB_angle, condB_zX, condB_zY, condB_zR, itok_B_0_2)
    x, itok_B_0_7, fside_Bx2_0, condB_angle, condB_zX, condB_zY, condB_zR, itok_B_0_2 = _rec_inputs()

    def _L0_cond_setup():
        import jax, jax.numpy as jnp
        import numpy as np
        S, O, H = (8, 128, 128)
        B, N = (32, 64)
        key = jax.random.key(seed)
        k1, k2, k3, k4 = jax.random.split(key, 4)
        x = jax.random.normal(k1, (B, N, H), dtype=jnp.float32)
        subject_id = jax.random.randint(k2, (B,), 0, S)
        wbound = jnp.sqrt(2.0 / 6.0) * jnp.sqrt(3.0 / H)
        weight = jax.random.uniform(k3, (S, O, H), minval=-wbound, maxval=wbound, dtype=jnp.float32)
        bbound = 1.0 / jnp.sqrt(H)
        bias = jax.random.uniform(k4, (S, O), minval=-bbound, maxval=bbound, dtype=jnp.float32)
        return {'x': x, 'subject_id': subject_id, 'weight': weight, 'bias': bias}
    _L0_cond_all = _L0_cond_setup()
    _L0_cond_in = {k: v for k, v in _L0_cond_all.items() if k in ('weight', 'bias')}
    del _L0_cond_all

    def _L0_attn_setup():
        import jax, jax.numpy as jnp
        import numpy as np
        EPS = 1e-10

        def scores_dtype(x):
            return x.dtype
        key = jax.random.key(seed)
        ks = jax.random.split(key, 5)
        B, S, D, N, H = (2, 256, 128, 16, 64)
        init_range = 0.02
        residual = jax.random.normal(ks[0], (B, S, D), dtype=jnp.float32)
        W_key = jax.random.normal(ks[1], (N, D, H), dtype=jnp.float32) * init_range
        W_query = jax.random.normal(ks[2], (N, D, H), dtype=jnp.float32) * init_range
        W_values = jax.random.normal(ks[3], (N, D, H), dtype=jnp.float32) * init_range
        W_output = jax.random.normal(ks[4], (N, H, D), dtype=jnp.float32) * init_range
        return {'residual': residual, 'W_key': W_key, 'W_query': W_query, 'W_values': W_values, 'W_output': W_output, 'Bias_key': jnp.zeros((N, H), jnp.float32), 'Bias_query': jnp.zeros((N, H), jnp.float32), 'Bias_values': jnp.zeros((N, H), jnp.float32), 'Bias_output': jnp.zeros((D,), jnp.float32)}
    _L0_attn_all = _L0_attn_setup()
    _L0_attn_in = {k: v for k, v in _L0_attn_all.items() if k in ('W_key', 'W_query', 'W_values', 'W_output', 'Bias_key', 'Bias_query', 'Bias_values', 'Bias_output')}
    del _L0_attn_all

    def _L0_cond2_setup():
        import jax, jax.numpy as jnp
        import numpy as np
        B, H, W = (32, 128, 128)
        SCALE_DX = 1.0
        SCALE_ANGLE = 1.0

        def _rigid_transform(X, dx, angle):
            b, h, w = X.shape
            gx = jnp.arange(w, dtype=jnp.float32)[None, :] - w / 2.0
            gy = jnp.arange(h, dtype=jnp.float32)[:, None] - h / 2.0
            theta = angle * SCALE_ANGLE
            c = jnp.cos(theta)[:, None, None]
            s = jnp.sin(theta)[:, None, None]
            xp = c * gx - s * gy + dx[:, 0, None, None] * SCALE_DX
            yp = s * gx + c * gy + dx[:, 1, None, None] * SCALE_DX
            gx_n = yp / h * 2.0
            gy_n = xp / w * 2.0
            ix = (gx_n + 1.0) * 0.5 * (w - 1)
            iy = (gy_n + 1.0) * 0.5 * (h - 1)
            ix0 = jnp.floor(ix)
            iy0 = jnp.floor(iy)
            wx1 = ix - ix0
            wy1 = iy - iy0
            wx0 = 1.0 - wx1
            wy0 = 1.0 - wy1
            ix0i = ix0.astype(jnp.int32)
            iy0i = iy0.astype(jnp.int32)
            ix1i = ix0i + 1
            iy1i = iy0i + 1
            bidx = jnp.arange(b, dtype=jnp.int32)[:, None, None]

            def gather(yi, xi):
                valid = (xi >= 0) & (xi <= w - 1) & (yi >= 0) & (yi <= h - 1)
                xc = jnp.clip(xi, 0, w - 1)
                yc = jnp.clip(yi, 0, h - 1)
                return X[bidx, yc, xc] * valid.astype(X.dtype)
            out = gather(iy0i, ix0i) * (wy0 * wx0) + gather(iy0i, ix1i) * (wy0 * wx1) + gather(iy1i, ix0i) * (wy1 * wx0) + gather(iy1i, ix1i) * (wy1 * wx1)
            return out
        key = jax.random.key(seed)
        k1, k2, k3 = jax.random.split(key, 3)
        X = jax.random.normal(k1, (B, H, W), dtype=jnp.float32)
        dx = jax.random.normal(k2, (B, 2), dtype=jnp.float32) * 8.0
        angle = jax.random.normal(k3, (B,), dtype=jnp.float32) * 0.2
        return {'X': X, 'dx': dx, 'angle': angle}
    _L0_cond2_all = _L0_cond2_setup()
    _L0_cond2_in = {k: v for k, v in _L0_cond2_all.items() if k in ()}
    del _L0_cond2_all

    def _L0_ffn_setup():
        import jax, jax.numpy as jnp
        import numpy as np
        DIM = 128
        DEPTH = 6
        HEADS = 16
        DIM_HEAD = 64
        WINDOW = 32
        INNER = HEADS * DIM_HEAD
        DIM_INNER = int(DIM * 4 * 2 / 3)
        QK_SCALE = 8.0

        def shift_tokens(t):
            a, s = jnp.split(t, 2, -1)
            s = jnp.pad(s, ((0, 0), (1, 0), (0, 0)))[:, :-1]
            return jnp.concatenate([a, s], -1)

        def l2norm(t):
            return t / jnp.maximum(jnp.linalg.norm(t, axis=-1, keepdims=True), 1e-12)

        def rotate_half(x):
            x1, x2 = jnp.split(x, 2, -1)
            return jnp.concatenate([-x2, x1], -1)

        def rotary_tables(n):
            half = jnp.arange(0, DIM_HEAD, 2, dtype=jnp.float32)
            inv_freq = 1.0 / 10000.0 ** (half / DIM_HEAD)
            t = jnp.arange(n, dtype=jnp.float32)
            freqs = t[:, None] * inv_freq[None, :]
            freqs = jnp.concatenate([freqs, freqs], -1)
            base_scale = (half + 0.4 * DIM_HEAD) / (1.4 * DIM_HEAD)
            power = (t - n // 2) / (WINDOW // 2)
            scale = base_scale[None, :] ** power[:, None]
            scale = jnp.concatenate([scale, scale], -1)
            return (freqs, scale)

        def local_attention(q, k, v):
            b, h, n, d = q.shape
            w = WINDOW
            nw = n // w
            bq = q.reshape(b, h, nw, w, d)
            bk = k.reshape(b, h, nw, w, d)
            bv = v.reshape(b, h, nw, w, d)

            def look(t):
                p = jnp.pad(t, ((0, 0), (0, 0), (1, 0), (0, 0), (0, 0)))
                return jnp.concatenate([p[:, :, :nw], p[:, :, 1:]], axis=3)
            bk2, bv2 = (look(bk), look(bv))
            seq = jnp.arange(n).reshape(nw, w)
            seq_p = jnp.pad(seq, ((1, 0), (0, 0)), constant_values=-1)
            jt = jnp.concatenate([seq_p[:nw], seq_p[1:]], axis=1)
            it = seq[:, :, None]
            jb = jt[:, None, :]
            mask = (it < jb) | (it > jb + w) | (jb == -1)
            sim = jnp.einsum('bhwie,bhwje->bhwij', bq, bk2) * QK_SCALE
            sim = jnp.where(mask, -jnp.finfo(sim.dtype).max, sim)
            attn = jax.nn.softmax(sim, -1)
            out = jnp.einsum('bhwij,bhwje->bhwie', attn, bv2)
            return out.reshape(b, h, n, d)

        def attn_layer(x, Wqkv, qs, ksc, Wo):
            b, n, _ = x.shape
            qkv = x @ Wqkv
            q, k, v = jnp.split(qkv, 3, -1)
            sh = lambda t: t.reshape(b, n, HEADS, DIM_HEAD).transpose(0, 2, 1, 3)
            q, k, v = (sh(q), sh(k), sh(v))
            q = l2norm(q) * qs
            k = l2norm(k) * ksc
            freqs, scale = rotary_tables(n)
            cos, sin = (jnp.cos(freqs), jnp.sin(freqs))
            q = q * cos * scale + rotate_half(q) * sin * scale
            inv = 1.0 / scale
            k = k * cos * inv + rotate_half(k) * sin * inv
            out = local_attention(q, k, v)
            out = out.transpose(0, 2, 1, 3).reshape(b, n, INNER)
            return out @ Wo

        def ffn_layer(x, g, bln, W1, b1, W2, b2):
            mu = x.mean(-1, keepdims=True)
            var = ((x - mu) ** 2).mean(-1, keepdims=True)
            xn = (x - mu) / jnp.sqrt(var + 1e-05) * g + bln
            hg = xn @ W1 + b1
            a, gate = jnp.split(hg, 2, -1)
            return a * jax.nn.gelu(gate, approximate=False) @ W2 + b2
        key = jax.random.key(seed)
        ks = jax.random.split(key, 8)
        B, N = (2, 256)
        init = lambda k, shape: jax.random.normal(k, shape, jnp.float32) * 0.02
        return {'x': jax.random.normal(ks[0], (B, N, DIM), jnp.float32), 'Wqkv': init(ks[1], (DEPTH, DIM, 3 * INNER)), 'q_scale': jnp.ones((DEPTH, DIM_HEAD), jnp.float32), 'k_scale': jnp.ones((DEPTH, DIM_HEAD), jnp.float32), 'Wo': init(ks[2], (DEPTH, INNER, DIM)), 'ln_g': jnp.ones((DEPTH, DIM), jnp.float32), 'ln_b': jnp.zeros((DEPTH, DIM), jnp.float32), 'W1': init(ks[3], (DEPTH, DIM, 2 * DIM_INNER)), 'b1': jnp.zeros((DEPTH, 2 * DIM_INNER), jnp.float32), 'W2': init(ks[4], (DEPTH, DIM_INNER, DIM)), 'b2': jnp.zeros((DEPTH, DIM), jnp.float32)}
    _L0_ffn_all = _L0_ffn_setup()
    _L0_ffn_in = {k: v for k, v in _L0_ffn_all.items() if k in ('Wqkv', 'q_scale', 'k_scale', 'Wo', 'ln_g', 'ln_b', 'W1', 'b1', 'W2', 'b2')}
    del _L0_ffn_all

    def _L1_cond_setup():
        import jax, jax.numpy as jnp
        import numpy as np
        key = jax.random.key(seed)
        k1, k2, k3, k4 = jax.random.split(key, 4)
        B, H, W = (64, 128, 128)
        return {'y': jax.random.uniform(k1, (B, H, W), dtype=jnp.float32), 'zX': jax.random.uniform(k2, (B, 1), dtype=jnp.float32), 'zY': jax.random.uniform(k3, (B, 1), dtype=jnp.float32), 'zR': jax.random.uniform(k4, (B, 1), dtype=jnp.float32), 'dx': 1, 'dy': 1}
    _L1_cond_all = _L1_cond_setup()
    _L1_cond_in = {k: v for k, v in _L1_cond_all.items() if k in ()}
    del _L1_cond_all

    def _L1_attn_setup():
        import jax, jax.numpy as jnp
        import numpy as np
        D_MODEL = 128
        HEADS = 4
        DK = 128
        DV = 256
        HDK = DK // HEADS
        HDV = DV // HEADS
        LOW_RANK = 16
        CHUNK = 64
        GATE_NORM = 16.0
        EPS = 1e-05

        def _gla_chunked(q, k, v, g):
            B, H, T, _ = q.shape
            NC = T // CHUNK
            scale = HDK ** (-0.5)

            def to_chunks(t, d):
                return t.reshape(B, H, NC, CHUNK, d).transpose(2, 0, 1, 3, 4)
            qc = to_chunks(q, HDK)
            kc = to_chunks(k, HDK)
            vc = to_chunks(v, HDV)
            bc = jnp.cumsum(to_chunks(g, HDK), axis=-2)
            mask = jnp.tril(jnp.ones((CHUNK, CHUNK), bool))

            def step(S, inp):
                qb, kb, vb, bb = inp
                qg = qb * jnp.exp(bb) * scale
                kd = kb * jnp.exp(-bb)
                A = jnp.einsum('bhtd,bhsd->bhts', qg, kd)
                A = jnp.where(mask, A, 0.0)
                o = jnp.einsum('bhts,bhsv->bhtv', A, vb) + jnp.einsum('bhtd,bhdv->bhtv', qg, S)
                b_last = bb[:, :, -1:, :]
                kg = kb * jnp.exp(b_last - bb)
                S = S * jnp.exp(b_last[:, :, 0, :])[..., None] + jnp.einsum('bhtd,bhtv->bhdv', kg, vb)
                return (S, o)
            S0 = jnp.zeros((B, H, HDK, HDV), q.dtype)
            _, o = jax.lax.scan(step, S0, (qc, kc, vc, bc))
            return o.transpose(1, 2, 0, 3, 4).reshape(B, H, T, HDV)
        key = jax.random.key(seed)
        ks = jax.random.split(key, 10)
        gain = 2.0 ** (-2.5)

        def xavier(k, shape):
            lim = gain * np.sqrt(6.0 / (shape[0] + shape[1]))
            return jax.random.uniform(k, shape, jnp.float32, -lim, lim)
        return {'x': jax.random.normal(ks[0], (2, 256, D_MODEL), jnp.float32), 'Wq': xavier(ks[1], (D_MODEL, DK)), 'Wk': xavier(ks[2], (D_MODEL, DK)), 'Wv': xavier(ks[3], (D_MODEL, DV)), 'Wg': xavier(ks[4], (D_MODEL, DV)), 'Wgk1': xavier(ks[5], (D_MODEL, LOW_RANK)), 'Wgk2': xavier(ks[6], (LOW_RANK, DK)), 'bgk2': jnp.zeros((DK,), jnp.float32), 'Wo': xavier(ks[7], (DV, D_MODEL)), 'rms_w': jnp.ones((HDV,), jnp.float32)}
    _L1_attn_all = _L1_attn_setup()
    _L1_attn_in = {k: v for k, v in _L1_attn_all.items() if k in ('Wq', 'Wk', 'Wv', 'Wg', 'Wgk1', 'Wgk2', 'bgk2', 'Wo', 'rms_w')}
    del _L1_attn_all

    def _L1_cond2_setup():
        import jax, jax.numpy as jnp
        import numpy as np
        B, S, D, F, E = (8, 128, 128, 512, 4)

        def _dense(x, wi, wo):
            return jax.nn.relu(x @ wi) @ wo
        key = jax.random.key(seed)
        ks = jax.random.split(key, 10)
        scale = 0.02
        return {'hidden_states': jax.random.normal(ks[0], (B, S, D), jnp.float32), 'type_idx': jax.random.randint(ks[1], (B,), 0, 3, jnp.int32), 'expert_wi': jax.random.normal(ks[2], (E, D, F), jnp.float32) * scale, 'expert_wo': jax.random.normal(ks[3], (E, F, D), jnp.float32) * scale, 'share_wi': jax.random.normal(ks[4], (3, D, F), jnp.float32) * scale, 'share_wo': jax.random.normal(ks[5], (3, F, D), jnp.float32) * scale, 'gate_vecs': jnp.array([[0.22, 0.22, 0.2, 0.2], [0.2, 0.22, 0.22, 0.2], [0.2, 0.2, 0.22, 0.22]], jnp.float32), 'gate_w1': jax.random.normal(ks[6], (4 * D, D), jnp.float32) * scale, 'gate_w2': jax.random.normal(ks[7], (D, 4), jnp.float32) * scale}
    _L1_cond2_all = _L1_cond2_setup()
    _L1_cond2_in = {k: v for k, v in _L1_cond2_all.items() if k in ('expert_wi', 'expert_wo', 'share_wi', 'share_wo', 'gate_vecs', 'gate_w1', 'gate_w2')}
    del _L1_cond2_all

    def _L1_ffn_setup():
        import jax, jax.numpy as jnp
        import numpy as np
        H = 128
        I = 128
        E = 8
        key = jax.random.key(seed)
        ks = jax.random.split(key, 8)
        s = 0.02
        x = jax.random.normal(ks[0], (4, 256, H), dtype=jnp.float32)
        Wg = jax.random.normal(ks[1], (H, E), dtype=jnp.float32) * s
        bg = jnp.zeros((E,), dtype=jnp.float32)
        W1 = jax.random.normal(ks[2], (E, H, I), dtype=jnp.float32) * s
        b1 = jnp.zeros((E, I), dtype=jnp.float32)
        W2 = jax.random.normal(ks[3], (E, I, H), dtype=jnp.float32) * s
        b2 = jnp.zeros((E, H), dtype=jnp.float32)
        return {'x': x, 'Wg': Wg, 'bg': bg, 'W1': W1, 'b1': b1, 'W2': W2, 'b2': b2}
    _L1_ffn_all = _L1_ffn_setup()
    _L1_ffn_in = {k: v for k, v in _L1_ffn_all.items() if k in ('Wg', 'bg', 'W1', 'b1', 'W2', 'b2')}
    del _L1_ffn_all
    return {'x': x, 'itok_B_0_7': itok_B_0_7, 'fside_Bx2_0': fside_Bx2_0, 'condB_angle': condB_angle, 'condB_zX': condB_zX, 'condB_zY': condB_zY, 'condB_zR': condB_zR, 'itok_B_0_2': itok_B_0_2, 'L0_cond_weight': _L0_cond_in['weight'], 'L0_cond_bias': _L0_cond_in['bias'], 'L0_attn_W_key': _L0_attn_in['W_key'], 'L0_attn_W_query': _L0_attn_in['W_query'], 'L0_attn_W_values': _L0_attn_in['W_values'], 'L0_attn_W_output': _L0_attn_in['W_output'], 'L0_attn_Bias_key': _L0_attn_in['Bias_key'], 'L0_attn_Bias_query': _L0_attn_in['Bias_query'], 'L0_attn_Bias_values': _L0_attn_in['Bias_values'], 'L0_attn_Bias_output': _L0_attn_in['Bias_output'], 'L0_ffn_Wqkv': _L0_ffn_in['Wqkv'], 'L0_ffn_q_scale': _L0_ffn_in['q_scale'], 'L0_ffn_k_scale': _L0_ffn_in['k_scale'], 'L0_ffn_Wo': _L0_ffn_in['Wo'], 'L0_ffn_ln_g': _L0_ffn_in['ln_g'], 'L0_ffn_ln_b': _L0_ffn_in['ln_b'], 'L0_ffn_W1': _L0_ffn_in['W1'], 'L0_ffn_b1': _L0_ffn_in['b1'], 'L0_ffn_W2': _L0_ffn_in['W2'], 'L0_ffn_b2': _L0_ffn_in['b2'], 'L1_attn_Wq': _L1_attn_in['Wq'], 'L1_attn_Wk': _L1_attn_in['Wk'], 'L1_attn_Wv': _L1_attn_in['Wv'], 'L1_attn_Wg': _L1_attn_in['Wg'], 'L1_attn_Wgk1': _L1_attn_in['Wgk1'], 'L1_attn_Wgk2': _L1_attn_in['Wgk2'], 'L1_attn_bgk2': _L1_attn_in['bgk2'], 'L1_attn_Wo': _L1_attn_in['Wo'], 'L1_attn_rms_w': _L1_attn_in['rms_w'], 'L1_cond2_expert_wi': _L1_cond2_in['expert_wi'], 'L1_cond2_expert_wo': _L1_cond2_in['expert_wo'], 'L1_cond2_share_wi': _L1_cond2_in['share_wi'], 'L1_cond2_share_wo': _L1_cond2_in['share_wo'], 'L1_cond2_gate_vecs': _L1_cond2_in['gate_vecs'], 'L1_cond2_gate_w1': _L1_cond2_in['gate_w1'], 'L1_cond2_gate_w2': _L1_cond2_in['gate_w2'], 'L1_ffn_Wg': _L1_ffn_in['Wg'], 'L1_ffn_bg': _L1_ffn_in['bg'], 'L1_ffn_W1': _L1_ffn_in['W1'], 'L1_ffn_b1': _L1_ffn_in['b1'], 'L1_ffn_W2': _L1_ffn_in['W2'], 'L1_ffn_b2': _L1_ffn_in['b2']}

def reference(x, itok_B_0_7, fside_Bx2_0, condB_angle, condB_zX, condB_zY, condB_zR, itok_B_0_2, L0_cond_weight, L0_cond_bias, L0_attn_W_key, L0_attn_W_query, L0_attn_W_values, L0_attn_W_output, L0_attn_Bias_key, L0_attn_Bias_query, L0_attn_Bias_values, L0_attn_Bias_output, L0_ffn_Wqkv, L0_ffn_q_scale, L0_ffn_k_scale, L0_ffn_Wo, L0_ffn_ln_g, L0_ffn_ln_b, L0_ffn_W1, L0_ffn_b1, L0_ffn_W2, L0_ffn_b2, L1_attn_Wq, L1_attn_Wk, L1_attn_Wv, L1_attn_Wg, L1_attn_Wgk1, L1_attn_Wgk2, L1_attn_bgk2, L1_attn_Wo, L1_attn_rms_w, L1_cond2_expert_wi, L1_cond2_expert_wo, L1_cond2_share_wi, L1_cond2_share_wo, L1_cond2_gate_vecs, L1_cond2_gate_w1, L1_cond2_gate_w2, L1_ffn_Wg, L1_ffn_bg, L1_ffn_W1, L1_ffn_b1, L1_ffn_W2, L1_ffn_b2):
    import jax
    import jax.numpy as jnp

    def _L0_cond_ref(x, subject_id, weight, bias):
        import jax, jax.numpy as jnp
        import numpy as np
        S, O, H = (8, 128, 128)
        B, N = (32, 64)
        W = weight[subject_id]
        b = bias[subject_id]
        y = jnp.einsum('bnh,boh->bno', x, W) + b[:, None, :]
        return y

    def _L0_attn_ref(residual, W_key, W_query, W_values, W_output, Bias_key, Bias_query, Bias_values, Bias_output):
        import jax, jax.numpy as jnp
        import numpy as np
        EPS = 1e-10

        def scores_dtype(x):
            return x.dtype
        B, S, D = residual.shape
        N, _, H = W_key.shape
        keys = jnp.einsum('bse,neh->bsnh', residual, W_key) + Bias_key
        queries = jnp.einsum('bse,neh->bsnh', residual, W_query) + Bias_query
        values = jnp.einsum('bse,neh->bsnh', residual, W_values) + Bias_values
        scores = jnp.einsum('bknh,bqnh->bnqk', keys, queries) / jnp.sqrt(jnp.asarray(H, scores_dtype(residual)))
        q_idx = jnp.arange(S)[:, None]
        k_idx = jnp.arange(S)[None, :]
        causal_mask = q_idx < k_idx
        scores = jnp.where(causal_mask[None, None, :, :], jnp.asarray(EPS, scores.dtype), scores)
        probs = jax.nn.softmax(scores, axis=3)
        weighted = jnp.einsum('bnqk,bknh->bqnh', probs, values)
        out = jnp.einsum('bqnh,nhe->bqe', weighted, W_output) + Bias_output
        return out

    def _L0_cond2_ref(X, dx, angle):
        import jax, jax.numpy as jnp
        import numpy as np
        B, H, W = (32, 128, 128)
        SCALE_DX = 1.0
        SCALE_ANGLE = 1.0

        def _rigid_transform(X, dx, angle):
            b, h, w = X.shape
            gx = jnp.arange(w, dtype=jnp.float32)[None, :] - w / 2.0
            gy = jnp.arange(h, dtype=jnp.float32)[:, None] - h / 2.0
            theta = angle * SCALE_ANGLE
            c = jnp.cos(theta)[:, None, None]
            s = jnp.sin(theta)[:, None, None]
            xp = c * gx - s * gy + dx[:, 0, None, None] * SCALE_DX
            yp = s * gx + c * gy + dx[:, 1, None, None] * SCALE_DX
            gx_n = yp / h * 2.0
            gy_n = xp / w * 2.0
            ix = (gx_n + 1.0) * 0.5 * (w - 1)
            iy = (gy_n + 1.0) * 0.5 * (h - 1)
            ix0 = jnp.floor(ix)
            iy0 = jnp.floor(iy)
            wx1 = ix - ix0
            wy1 = iy - iy0
            wx0 = 1.0 - wx1
            wy0 = 1.0 - wy1
            ix0i = ix0.astype(jnp.int32)
            iy0i = iy0.astype(jnp.int32)
            ix1i = ix0i + 1
            iy1i = iy0i + 1
            bidx = jnp.arange(b, dtype=jnp.int32)[:, None, None]

            def gather(yi, xi):
                valid = (xi >= 0) & (xi <= w - 1) & (yi >= 0) & (yi <= h - 1)
                xc = jnp.clip(xi, 0, w - 1)
                yc = jnp.clip(yi, 0, h - 1)
                return X[bidx, yc, xc] * valid.astype(X.dtype)
            out = gather(iy0i, ix0i) * (wy0 * wx0) + gather(iy0i, ix1i) * (wy0 * wx1) + gather(iy1i, ix0i) * (wy1 * wx0) + gather(iy1i, ix1i) * (wy1 * wx1)
            return out
        return _rigid_transform(X, dx, angle)

    def _L0_ffn_ref(x, Wqkv, q_scale, k_scale, Wo, ln_g, ln_b, W1, b1, W2, b2):
        import jax, jax.numpy as jnp
        import numpy as np
        DIM = 128
        DEPTH = 6
        HEADS = 16
        DIM_HEAD = 64
        WINDOW = 32
        INNER = HEADS * DIM_HEAD
        DIM_INNER = int(DIM * 4 * 2 / 3)
        QK_SCALE = 8.0

        def shift_tokens(t):
            a, s = jnp.split(t, 2, -1)
            s = jnp.pad(s, ((0, 0), (1, 0), (0, 0)))[:, :-1]
            return jnp.concatenate([a, s], -1)

        def l2norm(t):
            return t / jnp.maximum(jnp.linalg.norm(t, axis=-1, keepdims=True), 1e-12)

        def rotate_half(x):
            x1, x2 = jnp.split(x, 2, -1)
            return jnp.concatenate([-x2, x1], -1)

        def rotary_tables(n):
            half = jnp.arange(0, DIM_HEAD, 2, dtype=jnp.float32)
            inv_freq = 1.0 / 10000.0 ** (half / DIM_HEAD)
            t = jnp.arange(n, dtype=jnp.float32)
            freqs = t[:, None] * inv_freq[None, :]
            freqs = jnp.concatenate([freqs, freqs], -1)
            base_scale = (half + 0.4 * DIM_HEAD) / (1.4 * DIM_HEAD)
            power = (t - n // 2) / (WINDOW // 2)
            scale = base_scale[None, :] ** power[:, None]
            scale = jnp.concatenate([scale, scale], -1)
            return (freqs, scale)

        def local_attention(q, k, v):
            b, h, n, d = q.shape
            w = WINDOW
            nw = n // w
            bq = q.reshape(b, h, nw, w, d)
            bk = k.reshape(b, h, nw, w, d)
            bv = v.reshape(b, h, nw, w, d)

            def look(t):
                p = jnp.pad(t, ((0, 0), (0, 0), (1, 0), (0, 0), (0, 0)))
                return jnp.concatenate([p[:, :, :nw], p[:, :, 1:]], axis=3)
            bk2, bv2 = (look(bk), look(bv))
            seq = jnp.arange(n).reshape(nw, w)
            seq_p = jnp.pad(seq, ((1, 0), (0, 0)), constant_values=-1)
            jt = jnp.concatenate([seq_p[:nw], seq_p[1:]], axis=1)
            it = seq[:, :, None]
            jb = jt[:, None, :]
            mask = (it < jb) | (it > jb + w) | (jb == -1)
            sim = jnp.einsum('bhwie,bhwje->bhwij', bq, bk2) * QK_SCALE
            sim = jnp.where(mask, -jnp.finfo(sim.dtype).max, sim)
            attn = jax.nn.softmax(sim, -1)
            out = jnp.einsum('bhwij,bhwje->bhwie', attn, bv2)
            return out.reshape(b, h, n, d)

        def attn_layer(x, Wqkv, qs, ksc, Wo):
            b, n, _ = x.shape
            qkv = x @ Wqkv
            q, k, v = jnp.split(qkv, 3, -1)
            sh = lambda t: t.reshape(b, n, HEADS, DIM_HEAD).transpose(0, 2, 1, 3)
            q, k, v = (sh(q), sh(k), sh(v))
            q = l2norm(q) * qs
            k = l2norm(k) * ksc
            freqs, scale = rotary_tables(n)
            cos, sin = (jnp.cos(freqs), jnp.sin(freqs))
            q = q * cos * scale + rotate_half(q) * sin * scale
            inv = 1.0 / scale
            k = k * cos * inv + rotate_half(k) * sin * inv
            out = local_attention(q, k, v)
            out = out.transpose(0, 2, 1, 3).reshape(b, n, INNER)
            return out @ Wo

        def ffn_layer(x, g, bln, W1, b1, W2, b2):
            mu = x.mean(-1, keepdims=True)
            var = ((x - mu) ** 2).mean(-1, keepdims=True)
            xn = (x - mu) / jnp.sqrt(var + 1e-05) * g + bln
            hg = xn @ W1 + b1
            a, gate = jnp.split(hg, 2, -1)
            return a * jax.nn.gelu(gate, approximate=False) @ W2 + b2
        for i in range(DEPTH):
            x = attn_layer(shift_tokens(x), Wqkv[i], q_scale[i], k_scale[i], Wo[i]) + x
            x = ffn_layer(shift_tokens(x), ln_g[i], ln_b[i], W1[i], b1[i], W2[i], b2[i]) + x
        return x

    def _L1_cond_ref(y, zX, zY, zR, dx, dy):
        import jax, jax.numpy as jnp
        import numpy as np
        yp_x = jnp.pad(y, ((0, 0), (0, 0), (1, 1)), mode='reflect')
        lap_x = (yp_x[:, :, :-2] - 2.0 * y + yp_x[:, :, 2:]) / (dx * dx)
        yp_y = jnp.pad(y, ((0, 0), (1, 1), (0, 0)), mode='reflect')
        lap_y = (yp_y[:, :-2, :] - 2.0 * y + yp_y[:, 2:, :]) / (dy * dy)
        du_dt = zX[:, :, None] * lap_x + zY[:, :, None] * lap_y + zR[:, :, None] * y * (1.0 - y)
        return du_dt

    def _L1_attn_ref(x, Wq, Wk, Wv, Wg, Wgk1, Wgk2, bgk2, Wo, rms_w):
        import jax, jax.numpy as jnp
        import numpy as np
        D_MODEL = 128
        HEADS = 4
        DK = 128
        DV = 256
        HDK = DK // HEADS
        HDV = DV // HEADS
        LOW_RANK = 16
        CHUNK = 64
        GATE_NORM = 16.0
        EPS = 1e-05

        def _gla_chunked(q, k, v, g):
            B, H, T, _ = q.shape
            NC = T // CHUNK
            scale = HDK ** (-0.5)

            def to_chunks(t, d):
                return t.reshape(B, H, NC, CHUNK, d).transpose(2, 0, 1, 3, 4)
            qc = to_chunks(q, HDK)
            kc = to_chunks(k, HDK)
            vc = to_chunks(v, HDV)
            bc = jnp.cumsum(to_chunks(g, HDK), axis=-2)
            mask = jnp.tril(jnp.ones((CHUNK, CHUNK), bool))

            def step(S, inp):
                qb, kb, vb, bb = inp
                qg = qb * jnp.exp(bb) * scale
                kd = kb * jnp.exp(-bb)
                A = jnp.einsum('bhtd,bhsd->bhts', qg, kd)
                A = jnp.where(mask, A, 0.0)
                o = jnp.einsum('bhts,bhsv->bhtv', A, vb) + jnp.einsum('bhtd,bhdv->bhtv', qg, S)
                b_last = bb[:, :, -1:, :]
                kg = kb * jnp.exp(b_last - bb)
                S = S * jnp.exp(b_last[:, :, 0, :])[..., None] + jnp.einsum('bhtd,bhtv->bhdv', kg, vb)
                return (S, o)
            S0 = jnp.zeros((B, H, HDK, HDV), q.dtype)
            _, o = jax.lax.scan(step, S0, (qc, kc, vc, bc))
            return o.transpose(1, 2, 0, 3, 4).reshape(B, H, T, HDV)
        B, T, _ = x.shape
        q = (x @ Wq).reshape(B, T, HEADS, HDK).transpose(0, 2, 1, 3)
        k = (x @ Wk).reshape(B, T, HEADS, HDK).transpose(0, 2, 1, 3)
        v = (x @ Wv).reshape(B, T, HEADS, HDV).transpose(0, 2, 1, 3)
        gk = x @ Wgk1 @ Wgk2 + bgk2
        g = jax.nn.log_sigmoid(gk.astype(jnp.float32)) / GATE_NORM
        g = g.reshape(B, T, HEADS, HDK).transpose(0, 2, 1, 3)
        o = _gla_chunked(q, k, v, g)
        o = o.transpose(0, 2, 1, 3)
        o = o * jax.lax.rsqrt(jnp.mean(o * o, axis=-1, keepdims=True) + EPS) * rms_w
        o = o.reshape(B, T, HEADS * HDV)
        o = o * jax.nn.silu(x @ Wg)
        return o @ Wo

    def _L1_cond2_ref(hidden_states, type_idx, expert_wi, expert_wo, share_wi, share_wo, gate_vecs, gate_w1, gate_w2):
        import jax, jax.numpy as jnp
        import numpy as np
        B, S, D, F, E = (8, 128, 128, 512, 4)

        def _dense(x, wi, wo):
            return jax.nn.relu(x @ wi) @ wo
        s0 = _dense(hidden_states, share_wi[0], share_wo[0])
        s1 = _dense(hidden_states, share_wi[1], share_wo[1])
        s2 = _dense(hidden_states, share_wi[2], share_wo[2])
        idx_a = type_idx
        idx_b = type_idx + 1
        out_a = jnp.einsum('bsf,bfd->bsd', jax.nn.relu(jnp.einsum('bsd,bdf->bsf', hidden_states, expert_wi[idx_a])), expert_wo[idx_a])
        out_b = jnp.einsum('bsf,bfd->bsd', jax.nn.relu(jnp.einsum('bsd,bdf->bsf', hidden_states, expert_wi[idx_b])), expert_wo[idx_b])
        p = jax.nn.softmax(gate_vecs / 0.1, axis=-1)
        wa = p[type_idx, idx_a][:, None, None]
        wb = p[type_idx, idx_b][:, None, None]
        expert_out = out_a * wa + out_b * wb
        gi = jnp.concatenate([expert_out[:, 0], s0[:, 0], s1[:, 0], s2[:, 0]], axis=-1)
        g = jax.nn.softmax(jax.nn.relu(gi @ gate_w1) @ gate_w2, axis=-1)
        out = expert_out * g[:, 0, None, None] + s0 * g[:, 1, None, None] + s1 * g[:, 2, None, None] + s2 * g[:, 3, None, None]
        return out

    def _L1_ffn_ref(x, Wg, bg, W1, b1, W2, b2):
        import jax, jax.numpy as jnp
        import numpy as np
        H = 128
        I = 128
        E = 8
        B, S, Hd = x.shape
        xf = x.reshape(-1, Hd)
        logits = xf @ Wg + bg
        gates = jax.nn.softmax(logits, axis=-1)
        idx = jnp.argmax(gates, axis=-1)
        h = jax.nn.gelu(jnp.einsum('th,ehi->tei', xf, W1) + b1, approximate=False)
        y = jnp.einsum('tei,eih->teh', h, W2) + b2
        out = jnp.take_along_axis(y, idx[:, None, None], axis=1)[:, 0, :]
        return out.reshape(B, S, Hd)
    x = x + _L0_attn_ref(_L0_cond_ref(x, itok_B_0_7, L0_cond_weight, L0_cond_bias), L0_attn_W_key, L0_attn_W_query, L0_attn_W_values, L0_attn_W_output, L0_attn_Bias_key, L0_attn_Bias_query, L0_attn_Bias_values, L0_attn_Bias_output)
    x = x + _L0_ffn_ref(_L0_cond2_ref(x, fside_Bx2_0, condB_angle), L0_ffn_Wqkv, L0_ffn_q_scale, L0_ffn_k_scale, L0_ffn_Wo, L0_ffn_ln_g, L0_ffn_ln_b, L0_ffn_W1, L0_ffn_b1, L0_ffn_W2, L0_ffn_b2)
    x = x + _L1_attn_ref(_L1_cond_ref(x, condB_zX[:, None], condB_zY[:, None], condB_zR[:, None], 1, 1), L1_attn_Wq, L1_attn_Wk, L1_attn_Wv, L1_attn_Wg, L1_attn_Wgk1, L1_attn_Wgk2, L1_attn_bgk2, L1_attn_Wo, L1_attn_rms_w)
    x = x + _L1_ffn_ref(_L1_cond2_ref(x, itok_B_0_2, L1_cond2_expert_wi, L1_cond2_expert_wo, L1_cond2_share_wi, L1_cond2_share_wo, L1_cond2_gate_vecs, L1_cond2_gate_w1, L1_cond2_gate_w2), L1_ffn_Wg, L1_ffn_bg, L1_ffn_W1, L1_ffn_b1, L1_ffn_W2, L1_ffn_b2)
    return x

_drawn_inputs = setup_inputs


def setup_inputs(seed=0):
    import zlib

    import numpy as np

    out = dict(_drawn_inputs(seed))
    spreads = {'L0_attn_Bias_key': (0.0, 0.1),
     'L0_attn_Bias_query': (0.0, 0.1),
     'L0_attn_Bias_values': (0.0, 0.1),
     'L0_attn_Bias_output': (0.0, 0.1),
     'L0_ffn_q_scale': (1.0, 0.2),
     'L0_ffn_k_scale': (1.0, 0.2),
     'L0_ffn_ln_g': (1.0, 0.2),
     'L0_ffn_ln_b': (0.0, 0.1),
     'L0_ffn_b1': (0.0, 0.1),
     'L0_ffn_b2': (0.0, 0.1),
     'L1_attn_bgk2': (0.0, 0.1),
     'L1_attn_rms_w': (1.0, 0.2),
     'L1_ffn_bg': (0.0, 0.1),
     'L1_ffn_b1': (0.0, 0.1),
     'L1_ffn_b2': (0.0, 0.1)}
    factors = {}
    for name, (base, spread) in spreads.items():
        noise = np.random.default_rng([zlib.crc32(name.encode()), seed]).standard_normal(out[name].shape)
        drawn = base * np.exp(spread * noise) if base else spread * noise
        out[name] = jnp.asarray(drawn.astype(out[name].dtype))
    for name, factor in factors.items():
        out[name] = (out[name] * factor).astype(out[name].dtype)
    return out
```

```python
from contextlib import ExitStack

import numpy as np

import concourse.bass as bass
from concourse import mybir

F32 = mybir.dt.float32
BF16 = mybir.dt.bfloat16
I32 = mybir.dt.int32
ALU = mybir.AluOpType
ACT = mybir.ActivationFunctionType
AX = mybir.AxisListType

B = 16
P = 128
N = B * P
HALF = P // 2
CH = 4
CW = CH * P
NCH = B // CH
HEADS, HD = 16, 64
GROUPS = 4
GH = HEADS // GROUPS
GV = GH * HD
TICKS = B * GROUPS
BODY = 2 * GROUPS
DEPTH = 6
WINDOW = 32
INNER = int(P * 4 * 2 / 3)
FCH = [(0, P), (P, P), (2 * P, INNER - 2 * P)]
SUBJ = 8
MASKED = -1e30
L2_EPS = 1e-12 ** 2
LN_EPS = 1e-5
FILL = 1e-10

RG_ROWS = 4
RG_CHUNKS = P // RG_ROWS
RG_BODY = 4
RG_BODIES = RG_CHUNKS // RG_BODY
RG_HAT, RG_X, RG_PROD, RG_RED = 1, 1, 2, 3
GRID = (P - 1) / P
CENTRE = (P - 1) / 2
ROUND = 1.5 * 2.0 ** 23
TWO_PI = (6.28125, 0.0019350051879882812, 3.0199159795074593e-07)
PI_BELOW = 3.1415925

GLH, GLK, GLV, RANK = 4, 32, 64, 16
GATE_NORM = 16.0
GLA_STEPS = 6 + 3 + 1 + 2 * CH

TYPES, F, FJ, NEXP = 3, 512, 4, 7
E_FREE, E_DOWN = 2, 10
ME = 8

D_PREP, D_QKV, D_ROPE, D_SCORE, D_PROB, D_OUT, D_PROJ = 0, 2, 3, 4, 5, 6, 7

R_CB, R_LNG, R_LNB, R_B2, R_MB1, R_GK, R_BO = 0, 8, 14, 20, 26, 34, 35
R_B1 = 36
ROWS = R_B1 + 6 * DEPTH


def runs(kind, u, delay):
    t = u - delay
    return kind == "steady" or (kind == "first" and t >= 0) or (kind == "last" and t < 0)


def reused(kind, t, back):
    return kind != "first" or t >= back


def attention_pass(eng, tick, ticks, seqs):
    for u in range(BODY):
        tick("first", u, ticks, seqs, 0)
    with eng.Fori(1, TICKS // BODY) as i:
        for u in range(BODY):
            tick("steady", u, ticks + i * BODY, seqs + i * 2, i)
    for u in range(D_PROJ):
        tick("last", u, ticks + TICKS, seqs + B, TICKS // BODY)


class Semaphores:
    def __init__(self, sem):
        self.const_loaded = sem("const_loaded")
        self.x_loaded = sem("x_loaded")
        self.small_loaded = sem("small_loaded")
        self.rows_zeroed = sem("rows_zeroed")
        self.x_turned = sem("x_turned")
        self.x_state = sem("x_state")
        self.cond_turned = sem("cond_turned")
        self.cond_state = sem("cond_state")
        self.l0bias_loaded = sem("l0bias_loaded")
        self.consts_set = sem("consts_set")
        self.wqkv_loaded = sem("wqkv_loaded")
        self.wo_loaded = sem("wo_loaded")
        self.ids_loaded = sem("ids_loaded")
        self.wsel_ready = sem("wsel_ready")
        self.cond_ready = sem("cond_ready")
        self.ys_ready = sem("ys_ready")
        self.wffn_loaded = sem("wffn_loaded")
        self.tables_ready = sem("tables_ready")
        self.xs_ready = sem("xs_ready")
        self.out_ready = sem("out_ready")
        self.out_stored = sem("out_stored")
        self.out_turned = sem("out_turned")
        self.lf_shifted = sem("lf_shifted")
        self.lf_mean = sem("lf_mean")
        self.lf_centred = sem("lf_centred")
        self.lf_squared = sem("lf_squared")
        self.lf_var = sem("lf_var")
        self.lf_vareps = sem("lf_vareps")
        self.lf_rstd = sem("lf_rstd")
        self.lf_spread = sem("lf_spread")
        self.lf_normed = sem("lf_normed")
        self.lf_xn = sem("lf_xn")
        self.rg_image = sem("rg_image")
        self.rg_xarg = sem("rg_xarg")
        self.rg_yarg = sem("rg_yarg")
        self.rg_xabs = sem("rg_xabs")
        self.rg_yabs = sem("rg_yabs")
        self.rg_hat = sem("rg_hat")
        self.rg_xb = sem("rg_xb")
        self.rg_prod = sem("rg_prod")
        self.rg_red = sem("rg_red")
        self.rg_moved = sem("rg_moved")
        self.rg_consts = sem("rg_consts")
        self.rg_params = sem("rg_params")
        self.rg_wave = sem("rg_wave")
        self.rg_steps = sem("rg_steps")
        self.rg_ycolbles = sem("rg_ycolbles")
        self.lf_bias = sem("lf_bias")
        self.lf_h = sem("lf_h")
        self.lf_gelu = sem("lf_gelu")
        self.lf_gated = sem("lf_gated")
        self.lf_y = sem("lf_y")
        self.lf_state = sem("lf_state")
        self.g_loaded = sem("g_loaded")
        self.g_lapx = sem("g_lapx")
        self.g_src = sem("g_src")
        self.g_qk = sem("g_qk")
        self.g_low = sem("g_low")
        self.g_low_moved = sem("g_low_moved")
        self.g_decay = sem("g_decay")
        self.g_keys = sem("g_keys")
        self.g_vg = sem("g_vg")
        self.g_vg_used = sem("g_vg_used")
        self.g_headed = sem("g_headed")
        self.g_masked = sem("g_masked")
        self.g_a = sem("g_a")
        self.g_o = sem("g_o")
        self.g_o_read = sem("g_o_read")
        self.g_gated = sem("g_gated")
        self.g_oT = sem("g_oT")
        self.g_oT_moved = sem("g_oT_moved")
        self.g_y = sem("g_y")
        self.g_added = sem("g_added")
        self.g_steps = sem("g_steps")
        self.g_edges = sem("g_edges")
        self.g_edge2 = sem("g_edge2")
        self.g_abs = sem("g_abs")
        self.g_soft = sem("g_soft")
        self.g_log = sem("g_log")
        self.g_sum = sem("g_sum")
        self.g_exp = sem("g_exp")
        self.g_sq = sem("g_sq")
        self.g_mean = sem("g_mean")
        self.g_rms = sem("g_rms")
        self.g_sg = sem("g_sg")
        self.g_v_moved = sem("g_v_moved")
        self.x_final = sem("x_final")
        self.e_loaded = sem("e_loaded")
        self.e_first = sem("e_first")
        self.e_gate_h = sem("e_gate_h")
        self.e_gate_relu = sem("e_gate_relu")
        self.e_gate_o = sem("e_gate_o")
        self.e_gate_in = sem("e_gate_in")
        self.e_gate_hid = sem("e_gate_hid")
        self.e_gate_hid_relu = sem("e_gate_hid_relu")
        self.e_gate_logit = sem("e_gate_logit")
        self.e_gate_diag = sem("e_gate_diag")
        self.e_gate_all = sem("e_gate_all")
        self.e_steps = sem("e_steps")
        self.e_type_arg = sem("e_type_arg")
        self.e_type_exp = sem("e_type_exp")
        self.e_gate_arg = sem("e_gate_arg")
        self.e_gate_exp = sem("e_gate_exp")
        self.e_scales = sem("e_scales")
        self.e_chosen = sem("e_chosen")
        self.e_up = sem("e_up")
        self.e_relu = sem("e_relu")
        self.e_moved = sem("e_moved")
        self.e_down = sem("e_down")
        self.e_scaled = sem("e_scaled")
        self.m_loaded = sem("m_loaded")
        self.m_copied = sem("m_copied")
        self.m_logit = sem("m_logit")
        self.m_onehot = sem("m_onehot")
        self.m_turned = sem("m_turned")
        self.m_hot = sem("m_hot")
        self.m_up = sem("m_up")
        self.m_masked = sem("m_masked")
        self.m_y = sem("m_y")
        self.m_steps = sem("m_steps")
        self.m_equal = sem("m_equal")
        self.m_first = sem("m_first")
        self.m_gelu = sem("m_gelu")
        self.m_added = sem("m_added")


class AttentionSemaphores:
    def __init__(self, sem):
        self.qk_ready = sem("attn_qk_ready")
        self.v_ready = sem("attn_v_ready")
        self.squared = sem("attn_squared")
        self.summed = sem("attn_summed")
        self.clamped = sem("attn_clamped")
        self.rs_ready = sem("attn_rs_ready")
        self.normed = sem("attn_normed")
        self.roped_c = sem("attn_roped_c")
        self.roped_s = sem("attn_roped_s")
        self.qr_ready = sem("attn_qr_ready")
        self.qkT_ready = sem("attn_qkT_ready")
        self.qkT_moved = sem("attn_qkT_moved")
        self.sc_ready = sem("attn_sc_ready")
        self.kept = sem("attn_kept")
        self.filled = sem("attn_filled")
        self.maxed = sem("attn_maxed")
        self.negmax_ready = sem("attn_negmax_ready")
        self.exp_ready = sem("attn_exp_ready")
        self.rec_ready = sem("attn_rec_ready")
        self.pT_ready = sem("attn_pT_ready")
        self.pT_moved = sem("attn_pT_moved")
        self.v_moved = sem("attn_v_moved")
        self.o_ready = sem("attn_o_ready")
        self.on_ready = sem("attn_on_ready")
        self.oT_ready = sem("attn_oT_ready")
        self.oT_moved = sem("attn_oT_moved")
        self.y_ready = sem("attn_y_ready")
        self.added = sem("attn_added")


def build(nc, d, out):
    with ExitStack() as ctx:
        def sb(name, shape, dt=F32):
            return ctx.enter_context(nc.sbuf_tensor(name, shape, dt))

        def sem(name):
            return ctx.enter_context(nc.semaphore(name))

        bank = [ctx.enter_context(nc.psum_tensor(f"bank{i}", [P, 512], F32)) for i in range(6)]
        scores = ctx.enter_context(nc.psum_tensor("scores", [P, 2, 512], F32))
        qk_ps = bank[0:2]
        qkT_ps = bank[2]
        sc_ps = scores[:, :, 0:2 * P]
        cond_ps = scores[:, 0, 2 * P:3 * P]
        pT_ps = bank[3]
        v_ps, oT_ps = bank[4][:, 0:GV], bank[4][:, GV:2 * GV]
        o_ps, y_ps = bank[5][:, 0:GV], bank[5][:, GV:GV + P]

        XT = sb("XT", [P, N])
        ZT = sb("ZT", [P, N])
        ident = sb("ident", [P, P])
        ident16 = sb("ident16", [P, P], BF16)
        local_mask = sb("local_mask", [P, P], BF16)
        keep = sb("keep", [P, P])
        fill = sb("fill", [P, P])
        ropec = sb("ropec", [P, 2, HD])
        ropes = sb("ropes", [P, 2, HD])
        ones = sb("ones", [P, P])
        mean_w = sb("mean_w", [P, P])
        neg_half = sb("neg_half", [P, 8])
        rows = sb("rows", [ROWS, P])
        cols = sb("cols", [P, ROWS])
        wqk = sb("wqk", [P, GROUPS, 2, GV])
        wv = sb("wv", [P, HEADS * HD])
        wo = sb("wo", [P, HEADS * HD // P, P])
        w1 = sb("w1", [P, 2 * INNER])
        w2 = sb("w2", [P, 3, P])
        condT = sb("condT", [P, SUBJ, P + 1])
        wsel = sb("wsel", [P, 2, P + 1])
        subject = sb("subject", [1, B], I32)
        bqk = sb("bqk", [P, GROUPS, 2, GV])
        bv = sb("bv", [P, HEADS * HD])
        qkscale = sb("qkscale", [P, DEPTH, 2, HD])
        tabc = sb("tabc", [P, 2, HD])
        tabs = sb("tabs", [P, 2, HD])
        xs = [sb(f"xs{i}", [P, P]) for i in range(2)]
        ys = [sb(f"ys{i}", [P, P]) for i in range(2)]
        sq = [sb(f"sq{i}", [P, 512]) for i in range(2)]
        ss = [sb(f"ss{i}", [P, 8]) for i in range(2)]
        ssc = [sb(f"ssc{i}", [P, 8]) for i in range(2)]
        rs = [sb(f"rs{i}", [P, 8]) for i in range(2)]
        qn_pair = sb("qn_pair", [P, 2, 512])
        qn = [qn_pair[:, i, :] for i in range(2)]
        t1_pair = sb("t1_pair", [P, 2, 512])
        t1 = [t1_pair[:, i, :] for i in range(2)]
        t2_pair = sb("t2_pair", [P, 2, 512])
        t2 = [t2_pair[:, i, :] for i in range(2)]
        qr_pair = sb("qr_pair", [P, 2, 512])
        qr = [qr_pair[:, i, :] for i in range(2)]
        qkT = [sb(f"qkT{i}", [P, 512]) for i in range(2)]
        vt = [sb(f"vt{i}", [P, GV]) for i in range(GROUPS)]
        negmax = [sb(f"negmax{i}", [P, GH]) for i in range(2)]
        rowmax = [sb(f"rowmax{i}", [P, GH]) for i in range(2)]
        pr = [sb(f"pr{i}", [P, 512]) for i in range(2)]
        sums = [sb(f"sums{i}", [P, GH]) for i in range(2)]
        rec = [sb(f"rec{i}", [P, GH]) for i in range(2)]
        pT = [sb(f"pT{i}", [P, 512]) for i in range(2)]
        on = [sb(f"on{i}", [P, GV]) for i in range(2)]
        oT = [sb(f"oT{i}", [P, HEADS * HD]) for i in range(2)]
        angle = sb("angle", [P, B])
        offset = sb("offset", [P, B, 2])
        phase = sb("phase", [P, 2, B])
        turns = sb("turns", [P, 2, B])
        wave = sb("wave", [P, 2, B])
        step = sb("step", [P, 3, B])
        shift = sb("shift", [P, B, 2])
        grid = sb("grid", [P, P])
        negpart = sb("negpart", [P, 1])
        rg_ycol = sb("rg_ycol", [P, N])
        rg_xcol = sb("rg_xcol", [P, N])
        rg_yrow = sb("rg_yrow", [P, N])
        rg_xrow = sb("rg_xrow", [P, N])
        rg_x = sb("rg_x", [P, P])
        rg_u = [sb(f"rg_u{i}", [P, 2, CW]) for i in range(2)] + [t1_pair, t2_pair]
        rg_w = [sb(f"rg_w{i}", [P, 2, CW]) for i in range(2)] + [qn_pair, qr_pair]
        rg_ux, rg_uy = [u[:, 0, :] for u in rg_u], [u[:, 1, :] for u in rg_u]
        rg_wx, rg_wy = [w[:, 0, :] for w in rg_w], [w[:, 1, :] for w in rg_w]
        rg_p = pr
        gate_b = sb("gate_b", [P, 3])
        xf = [sb(f"xf{i}", [P, CW]) for i in range(2)]
        xc, xq, xn = t1, t2, qr
        xv, xr = ssc[0][:, 0:CH], ssc[1][:, 0:CH]
        gl = qn
        hg = [[sb(f"hg{i}{j}", [P, CW]) for j in range(3)] for i in range(2)]
        xin = ZT[:, :].rearrange("p (b f) -> p b f", b=B)
        cond_in = oT[0][:, :].rearrange("p (s h) -> p s h", s=SUBJ)

        mask_wide, pick_wide = t1[0][:, 0:P], oT[1][0:ME, 0:ME * P]
        diffuse = sb("diffuse", [P, 3, B])
        lap = sb("lap", [P, P])
        gwq, gwk = sb("gwq", [P, P]), sb("gwk", [P, P])
        gwl1, gwl2 = sb("gwl1", [P, RANK]), sb("gwl2", [RANK, P])
        gwvg = sb("gwvg", [P, 2 * GLH * GLV])
        gwo = sb("gwo", [P, 2, P])
        rmsw = sb("rmsw", [P, GLV])
        restart = sb("restart", [P, CW])
        gmask = sb("gmask", [P, P])
        headmask = sb("headmask", [P, GLH])
        gsrc, glow = sq[0], sq[1][0:RANK, :]
        gsum, gep, gen_, gq1 = qn[0], qn[1], qr[0], qr[1]
        gka, gkb, ga, goT = t2[0], t2[1], pr[0], qkT
        gv, gsg, gsq, gon, gout = vt[0], vt[1], vt[2], vt[3], on[0]
        gss, grs = negmax[0], rowmax[0]
        gq4 = wqk[:, :, :, :].rearrange("p g i n -> p (g i n)")

        e_up_w, e_down_w, e_sel = rg_ycol, rg_xcol, (rg_yrow, rg_xrow)
        l0_biases = bqk[:, :, :, :].rearrange("p g i n -> p (g i n)")
        share_up = l0_biases[:, 0:3 * F]
        share_down = sb("share_down", [P, 3, FJ, P])
        gw1, gw2 = l0_biases[:, 3 * F:].rearrange("p (k f) -> p k f", k=4), sb("gw2", [P, 4])
        first = sb("first", [P, B])
        gate_h = xf[0][:, 0:NEXP * FJ * B]
        gate_in, gate_hid = sb("gate_in", [P, 4 * B]), sb("gate_hid", [P, B])
        gate_p, gate_max, gate_diag = sb("gate_p", [B, 4]), sb("gate_max", [B, 1]), sb("gate_diag", [B, 4 * B])
        typew, typem = sb("typew", [P, TYPES * 4]), sb("typem", [P, TYPES])
        typei, etype = sb("typei", [P, B], I32), sb("etype", [1, B], I32)
        typef, is_type = sb("typef", [P, B]), sb("is_type", [P, B, TYPES])
        pick, expw = sb("pick", [P, 4 * B]), sb("expw", [P, 4 * B])
        scale5 = sb("scale5", [P, B, 5])
        e_scale = [sb(f"e_scale{i}", [P, 5]) for i in range(2)]
        e_h = t1
        m_w1, m_w2 = wv, wo[:, :, :].rearrange("p c e -> p (c e)")
        m_pick = sb("m_pick", [ME, ME * P], BF16)
        m_b2 = sb("m_b2", [ME, P])
        m_hotT, m_hot16 = qkT[0][0:ME, :], sb("m_hot16", [ME, CW], BF16)
        m_gate, m_gate_b, m_rank = sb("m_gate", [P, ME]), sb("m_gate_b", [P, ME]), sb("m_rank", [P, ME])
        m_logits, m_hot, m_max = sb("m_logits", [P, CH * ME]), sb("m_hot", [P, CH * ME]), sb("m_max", [P, CH])
        m_src, m_g, m_h = sq[0], t2, qn

        def up_of(e):
            return e_up_w[:, e * F:(e + 1) * F] if e < 4 else share_up[:, (e - 4) * F:(e - 3) * F]

        def down_of(e):
            return e_down_w[:, e * F:(e + 1) * F].rearrange("p (j e) -> p j e", j=FJ) if e < 4 \
                else share_down[:, e - 4, :, :]

        s = Semaphores(sem)

        a = AttentionSemaphores(sem)

        block = ctx.enter_context(nc.Block())

        def heads(ap):
            return ap.rearrange("p (h e) -> p h e", e=HD)

        def over(ap, shape, axis):
            return ap.unsqueeze(axis).to_broadcast(shape)

        @block.sync
        def _(sp):
            sp.dma_start(xin, d["x"].rearrange("b t f -> t b f")).then_inc(s.x_loaded, 16)
            sp.dma_start(ident[:, :], d["c_ident"]).then_inc(s.const_loaded, 16)
            sp.dma_start(cond_in, d["L0_cond_weight"].rearrange("s o h -> o s h")).then_inc(s.x_loaded, 16)
            sp.dma_start(mask_wide, d["c_local_mask"]).then_inc(s.const_loaded, 16)
            sp.dma_start(pick_wide, d["c_pick"]).then_inc(s.const_loaded, 16)
            sp.dma_start(keep[:, :], d["c_keep"]).then_inc(s.const_loaded, 16)
            sp.dma_start(fill[:, :], d["c_fill"]).then_inc(s.const_loaded, 16)
            sp.dma_start(ropec[:, :, :], d["c_ropec"]).then_inc(s.const_loaded, 16)
            sp.dma_start(ropes[:, :, :], d["c_ropes"]).then_inc(s.const_loaded, 16)
            sp.wait_ge(s.rows_zeroed, 1)
            small = [(R_CB, "L0_cond_bias"), (R_LNG, "L0_ffn_ln_g"), (R_LNB, "L0_ffn_ln_b"), (R_B2, "L0_ffn_b2"),
                     (R_MB1, "L1_ffn_b1")]
            for r, name in small:
                sp.dma_start(rows[r:r + d[name].shape[0], :], d[name]).then_inc(s.small_loaded, 16)
            sp.dma_start(rows[R_GK:R_GK + 1, :], d["L1_attn_bgk2"].unsqueeze(0)).then_inc(s.small_loaded, 16)
            sp.dma_start(rows[R_BO:R_BO + 1, :], d["L0_attn_Bias_output"].unsqueeze(0)).then_inc(s.small_loaded, 16)
            for half in range(2):
                for j, (o, w) in enumerate(FCH):
                    r = R_B1 + DEPTH * (3 * half + j)
                    sp.dma_start(rows[r:r + DEPTH, 0:w], d["L0_ffn_b1"][:, half * INNER + o:half * INNER + o + w])\
                        .then_inc(s.small_loaded, 16)
            sp.dma_start(subject[:, :], d["itok_B_0_7"].unsqueeze(0)).then_inc(s.ids_loaded, 16)
            for i, w in enumerate(("L0_attn_W_query", "L0_attn_W_key")):
                for g in range(GROUPS):
                    sp.dma_start(heads(wqk[:, g, i, :]), d[w][g * GH:(g + 1) * GH].rearrange("n e h -> e n h"))\
                        .then_inc(s.wqkv_loaded, 16)
            sp.dma_start(heads(wv[:, :]), d["L0_attn_W_values"].rearrange("n e h -> e n h"))\
                .then_inc(s.wqkv_loaded, 16)
            sp.dma_start(wo[:, :, :], d["L0_attn_W_output"].rearrange("n h e -> (n h) e")
                         .rearrange("(c p) e -> p c e", p=P)).then_inc(s.wo_loaded, 16)
            for i, w in enumerate(("L0_attn_Bias_query", "L0_attn_Bias_key")):
                sp.dma_start(bqk[:, :, i, :], d[w].rearrange("(g n) h -> g (n h)", g=GROUPS)
                             .partition_broadcast(P)).then_inc(s.l0bias_loaded, 16)
            sp.dma_start(bv[:, :], d["L0_attn_Bias_values"].rearrange("n h -> (n h)").partition_broadcast(P))\
                .then_inc(s.l0bias_loaded, 16)
            for i, w in enumerate(("L0_ffn_q_scale", "L0_ffn_k_scale")):
                sp.dma_start(qkscale[:, :, i, :], d[w].partition_broadcast(P)).then_inc(s.l0bias_loaded, 16)
            for i, w in enumerate(("condB_angle", "fside_Bx2_0")):
                sp.dma_start((angle, offset)[i][tuple([slice(None)] * (2 + i))], d[w].partition_broadcast(P))\
                    .then_inc(s.rg_params, 16)
            sp.dma_start(grid[:, :], d["c_grid"]).then_inc(s.rg_params, 16)
            sp.dma_start(negpart[:, :], d["c_negpart"]).then_inc(s.rg_params, 16)

            for z, name in enumerate(("condB_zX", "condB_zY", "condB_zR")):
                sp.dma_start(diffuse[:, z, :], d[name].partition_broadcast(P)).then_inc(s.g_loaded, 16)
            for to, name in ((lap, "c_lap"), (gwq, "L1_attn_Wq"), (gwk, "L1_attn_Wk"), (gwl1, "L1_attn_Wgk1"),
                             (gwl2, "L1_attn_Wgk2"), (restart, "c_restart"), (gmask, "c_gmask"),
                             (headmask, "c_headmask")):
                sp.dma_start(to[:, :], d[name]).then_inc(s.g_loaded, 16)
            for i, name in enumerate(("L1_attn_Wv", "L1_attn_Wg")):
                sp.dma_start(gwvg[:, i * GLH * GLV:(i + 1) * GLH * GLV], d[name]).then_inc(s.g_loaded, 16)
            sp.dma_start(gwo[:, :, :], d["L1_attn_Wo"].rearrange("(h p) e -> p h e", p=P)).then_inc(s.g_loaded, 16)
            sp.dma_start(rmsw[:, :], d["L1_attn_rms_w"].partition_broadcast(P)).then_inc(s.g_loaded, 16)

            def load_attention(src_qkv):
                for i in range(2):
                    sp.dma_start(wqk[:, :, i, :], src_qkv[:, i * HEADS * HD:(i + 1) * HEADS * HD]
                                 .rearrange("e (g n) -> e g n", g=GROUPS)).then_inc(s.wqkv_loaded, 16)
                sp.dma_start(wv[:, :], src_qkv[:, 2 * HEADS * HD:3 * HEADS * HD]).then_inc(s.wqkv_loaded, 16)

            def load_wo(src):
                sp.dma_start(wo[:, :, :], src.rearrange("(c p) e -> p c e", p=P)).then_inc(s.wo_loaded, 16)

            def load_ffn(up, dn):
                sp.dma_start(w1[:, :], up).then_inc(s.wffn_loaded, 16)
                sp.dma_start(w2[:, 0:2, :], dn[0:2 * P, :].rearrange("(j p) e -> p j e", p=P))\
                    .then_inc(s.wffn_loaded, 16)
                sp.dma_start(w2[0:FCH[2][1], 2, :], dn[2 * P:INNER, :]).then_inc(s.wffn_loaded, 16)

            load_ffn(d["L0_ffn_W1"][0], d["L0_ffn_W2"][0])
            sp.wait_ge(a.v_ready, TICKS)
            load_attention(d["L0_ffn_Wqkv"][0])
            sp.wait_ge(a.y_ready, B)
            load_wo(d["L0_ffn_Wo"][0])
            sp.wait_ge(s.rg_moved, B)
            sp.dma_start(e_up_w[:, :].rearrange("p (e f) -> p e f", e=4),
                         d["L1_cond2_expert_wi"].rearrange("e p f -> p e f")).then_inc(s.e_loaded, 16)
            sp.dma_start(e_down_w[:, :].rearrange("p (e j f) -> p e j f", e=4, j=FJ),
                         d["L1_cond2_expert_wo"].rearrange("e (j p) f -> p e j f", p=P)).then_inc(s.e_loaded, 16)
            sp.dma_start(share_up[:, :].rearrange("p (e f) -> p e f", e=3),
                         d["L1_cond2_share_wi"].rearrange("e p f -> p e f")).then_inc(s.e_loaded, 16)
            sp.dma_start(share_down[:, :, :, :],
                         d["L1_cond2_share_wo"].rearrange("e (j p) f -> p e j f", p=P)).then_inc(s.e_loaded, 16)
            sp.dma_start(gw1[:, :, :], d["L1_cond2_gate_w1"].rearrange("(k p) f -> p k f", p=P))\
                .then_inc(s.e_loaded, 16)
            sp.dma_start(gw2[:, :], d["L1_cond2_gate_w2"]).then_inc(s.e_loaded, 16)
            sp.dma_start(typew[:, :], d["L1_cond2_gate_vecs"].rearrange("t e -> (t e)").partition_broadcast(P))\
                .then_inc(s.e_loaded, 16)
            sp.dma_start(typei[:, :], d["itok_B_0_2"].partition_broadcast(P)).then_inc(s.e_loaded, 16)
            sp.dma_start(etype[:, :], d["itok_B_0_2"].unsqueeze(0)).then_inc(s.e_loaded, 16)
            sp.dma_start(m_b2[:, :], d["L1_ffn_b2"]).then_inc(s.m_loaded, 16)
            sp.dma_start(m_gate[:, :], d["L1_ffn_Wg"]).then_inc(s.m_loaded, 16)
            sp.dma_start(m_gate_b[:, :], d["L1_ffn_bg"].partition_broadcast(P)).then_inc(s.m_loaded, 16)
            sp.dma_start(m_rank[:, :], d["c_rank"]).then_inc(s.m_loaded, 16)
            with sp.Fori(1, DEPTH) as l:
                def of_layer(name):
                    return d[name][bass.ds(l, 1)].rearrange("l e n -> (l e) n")
                sp.wait_ge(a.v_ready, (l + 1) * TICKS)
                load_attention(of_layer("L0_ffn_Wqkv"))
                sp.wait_ge(a.y_ready, (l + 1) * B)
                load_wo(of_layer("L0_ffn_Wo"))
                sp.wait_ge(s.lf_y, l * NCH)
                load_ffn(of_layer("L0_ffn_W1"), of_layer("L0_ffn_W2"))
            sp.wait_ge(a.y_ready, (DEPTH + 1) * B)
            sp.dma_start(m_w1[:, :].rearrange("p (e i) -> p e i", e=ME), d["L1_ffn_W1"].rearrange("e p i -> p e i"))\
                .then_inc(s.m_loaded, 16)
            sp.dma_start(m_w2.rearrange("p (e i) -> p e i", e=ME), d["L1_ffn_W2"].rearrange("e p i -> p e i"))\
                .then_inc(s.m_loaded, 16)
            sp.wait_ge(s.out_ready, 4)
            sp.dma_start(out.rearrange("b t f -> t b f"), ZT[:, :].rearrange("p (b f) -> p b f", b=B))\
                .then_inc(s.out_stored, 16)
            sp.wait_ge(s.out_stored, 16)


        def pe_tick(pe, local):
            src = xs if local else ys

            def tick(kind, u, n, q, i):
                t = u - D_PROJ
                if runs(kind, u, D_PROJ) and t % GROUPS == GROUPS - 1:
                    pe.wait_ge(a.oT_moved, n + t + 1)
                    if runs(kind, u - 1, D_PROB):
                        pe.wait_ge(a.on_ready, n + u - D_PROB)
                    for c in range(8):
                        mm = pe.matmul(y_ps, wo[:, c, :], oT[(t // GROUPS) % 2][:, c * P:(c + 1) * P],
                                       start=(c == 0), stop=(c == 7))
                    mm.then_inc(a.y_ready, 1)
                if runs(kind, u, D_PREP) and u % GROUPS == 0 and not local:
                    b = u // GROUPS
                    pe.wait_ge(s.wsel_ready, q + b + 1)
                    if runs(kind, u - 1, D_SCORE):
                        pe.wait_ge(a.exp_ready, n + u - D_SCORE)
                    if kind != "first" or b >= 1:
                        pe.wait_ge(s.ys_ready, q + b)
                    pe.matmul(cond_ps, wsel[:, b % 2, 0:P], XT[:, bass.ds((2 * i + b) * P, P)],
                              start=True, stop=True).then_inc(s.cond_ready, 1)
                t = u - D_QKV
                if runs(kind, u, D_QKV):
                    g = t % GROUPS
                    if g == 0:
                        if local:
                            pe.wait_ge(s.xs_ready, (q - B) * 2 + 2 * (t // GROUPS) + 2)
                        else:
                            pe.wait_ge(s.ys_ready, q + t // GROUPS + 1)
                    if reused(kind, t, 2):
                        pe.wait_ge(a.normed if local else a.qr_ready, n + t - 1)
                    pe.matmul(qk_ps[t % 2][:, :], src[(t // GROUPS) % 2][:, :],
                              wqk[:, g, :, :].rearrange("p i n -> p (i n)"),
                              start=True, stop=True).then_inc(a.qk_ready, 1)
                t = u - D_SCORE
                if runs(kind, u, D_SCORE):
                    pe.wait_ge(a.qkT_moved, n + t + 1)
                    if reused(kind, t, 1):
                        pe.wait_ge(a.exp_ready, n + t)
                    if not local:
                        if kind == "steady" and u % GROUPS == 1:
                            pe.wait_ge(s.ys_ready, q + u // GROUPS + 1)
                        if kind == "first" and t == 1:
                            pe.wait_ge(s.ys_ready, q + 2)
                    st = qkT[t % 2]
                    if local:
                        for r in range(2):
                            pe.matmul(sc_ps[:, r, :].rearrange("p (a k) -> p a k", a=2), ident16[:, :],
                                      over(local_mask[:, :], [P, 2, P], 1), start=True, stop=False,
                                      skip_group_check=True)
                    for pair in range(2):
                        for r in range(2):
                            mm = pe.matmul(sc_ps[:, r, pair * P:(pair + 1) * P],
                                           st[r * HD:(r + 1) * HD, pair * P:(pair + 1) * P],
                                           st[r * HD:(r + 1) * HD, (2 + pair) * P:(3 + pair) * P],
                                           start=not local, stop=True, skip_group_check=True)
                    mm.then_inc(a.sc_ready, 1)
                t = u - D_PROB
                if runs(kind, u, D_PROB):
                    pe.wait_ge(a.exp_ready, n + t + 1)
                    if reused(kind, t, 1):
                        pe.wait_ge(a.pT_moved, n + t)
                    for h in range(GH):
                        mm = pe.transpose(pT_ps[:, h * P:(h + 1) * P], pr[t % 2][:, h * P:(h + 1) * P], ident[:, :])
                    mm.then_inc(a.pT_ready, 1)
                if runs(kind, u - 1, D_QKV):
                    pe.wait_ge(a.v_moved, n + u - D_QKV)
                if runs(kind, u - 1, D_OUT):
                    pe.wait_ge(a.oT_moved, n + u - D_OUT)
                t = u - D_QKV
                if runs(kind, u, D_QKV):
                    g = t % GROUPS
                    pe.matmul(v_ps, src[(t // GROUPS) % 2][:, :], wv[:, g * GV:(g + 1) * GV],
                              start=True, stop=True).then_inc(a.v_ready, 1)
                t = u - D_OUT
                if runs(kind, u, D_OUT):
                    pe.wait_ge(a.on_ready, n + t + 1)
                    for c in range(2):
                        mm = pe.transpose(oT_ps[:, c * P:(c + 1) * P], on[t % 2][:, c * P:(c + 1) * P], ident[:, :])
                    mm.then_inc(a.oT_ready, 1)
                t = u - D_ROPE
                if runs(kind, u, D_ROPE):
                    pe.wait_ge(a.qr_ready, n + t + 1)
                    if reused(kind, t, 1):
                        pe.wait_ge(a.qkT_moved, n + t)
                    for c in range(4):
                        mm = pe.transpose(qkT_ps[:, c * P:(c + 1) * P], qr[t % 2][:, c * P:(c + 1) * P], ident[:, :])
                    mm.then_inc(a.qkT_ready, 1)
                t = u - D_PROB
                if runs(kind, u, D_PROB):
                    pe.wait_ge(a.pT_moved, n + t + 1)
                    pe.wait_ge(a.v_moved, n + t + 1)
                    if reused(kind, t, 1):
                        pe.wait_ge(a.on_ready, n + t)
                    t2_ = u - D_PROJ
                    if runs(kind, u, D_PROJ) and t2_ % GROUPS == GROUPS - 1:
                        pe.wait_ge(a.added, q + t2_ // GROUPS + 1)
                    for h in range(GH):
                        at = (h % 2 * 2 + h // 2) * P
                        mm = pe.matmul(o_ps[:, h * HD:(h + 1) * HD], pT[t % 2][:, at:at + P],
                                       vt[t % GROUPS][:, h * HD:(h + 1) * HD], start=True, stop=True)
                    mm.then_inc(a.o_ready, 1)
            return tick

        def dve_tick(dve, local):
            def tick(kind, u, n, q, i):
                t = u - D_PROJ
                if runs(kind, u, D_PROJ) and t % GROUPS == GROUPS - 1:
                    dve.wait_ge(a.y_ready, q + t // GROUPS + 1)
                    at = bass.ds((2 * i + t // GROUPS) * P, P)
                    if local:
                        dve.tensor_tensor(ZT[:, at], y_ps, ZT[:, at], ALU.add).then_inc(a.added, 1)
                    else:
                        dve.scalar_tensor_tensor(XT[:, at], y_ps, cols[:, R_BO:R_BO + 1], XT[:, at],
                                                 ALU.add, ALU.add).then_inc(a.added, 1)
                t = u - D_ROPE
                if runs(kind, u, D_ROPE):
                    if local:
                        dve.wait_ge(a.rs_ready, n + t + 1)
                        if reused(kind, t, 2):
                            dve.wait_ge(a.roped_s, n + t - 1)
                        dve.tensor_tensor(heads(qn[t % 2][:, :]), heads(qk_ps[t % 2][:, :]),
                                          over(rs[t % 2][:, :], [P, 8, HD], 2), ALU.mult).then_inc(a.normed, 1)
                    else:
                        dve.wait_ge(a.qk_ready, n + t + 1)
                        if reused(kind, t, 2):
                            dve.wait_ge(a.qkT_ready, n + t - 1)
                        dve.tensor_tensor(qr[t % 2][:, :], qk_ps[t % 2][:, :],
                                          bqk[:, t % GROUPS, :, :].rearrange("p i n -> p (i n)"),
                                          ALU.add).then_inc(a.qr_ready, 1)
                t = u - D_SCORE
                if runs(kind, u, D_SCORE):
                    dve.wait_ge(a.sc_ready, n + t + 1)
                    sc = sc_ps.rearrange("p r (a k) -> p r a k", a=2)
                    if reused(kind, t, 2):
                        dve.wait_ge(a.exp_ready, n + t - 1)
                    if local:
                        dve.tensor_reduce(negmax[t % 2][:, :].rearrange("p (r a) -> p r a", r=2), sc, AX.X, ALU.max, negate=True)\
                            .then_inc(a.negmax_ready, 1)
                    else:
                        dve.tensor_tensor(sc, sc, keep[:, :].unsqueeze(1).unsqueeze(1).to_broadcast([P, 2, 2, P]), ALU.mult).then_inc(a.kept, 1)
                        dve.wait_ge(a.kept, n + t + 1)
                        dve.tensor_tensor(sc, sc, fill[:, :].unsqueeze(1).unsqueeze(1).to_broadcast([P, 2, 2, P]), ALU.add).then_inc(a.filled, 1)
                        dve.wait_ge(a.filled, n + t + 1)
                        dve.tensor_reduce(rowmax[t % 2][:, :].rearrange("p (r a) -> p r a", r=2), sc, AX.X, ALU.max).then_inc(a.maxed, 1)
                        dve.wait_ge(a.maxed, n + t + 1)
                        dve.tensor_scalar(negmax[t % 2][:, :], rowmax[t % 2][:, :], -HD ** -0.5, None, ALU.mult)\
                            .then_inc(a.negmax_ready, 1)
                t = u - D_ROPE
                if runs(kind, u, D_ROPE) and local:
                    dve.wait_ge(a.normed, n + t + 1)
                    dve.tensor_tensor(t1[t % 2][:, :].rearrange("p (i h e) -> p i h e", i=2, h=GH),
                                      qn[t % 2][:, :].rearrange("p (i h e) -> p i h e", i=2, h=GH),
                                      over(tabc[:, :, :], [P, 2, GH, HD], 2), ALU.mult).then_inc(a.roped_c, 1)
                t = u - D_PROB
                if runs(kind, u, D_PROB):
                    dve.wait_ge(a.pT_ready, n + t + 1)
                    if reused(kind, t, 2):
                        dve.wait_ge(a.o_ready, n + t - 1)
                    dve.tensor_copy(pT[t % 2][:, :], pT_ps[:, :]).then_inc(a.pT_moved, 1)
                t = u - D_ROPE
                if runs(kind, u, D_ROPE) and local:
                    dve.wait_ge(a.roped_c, n + t + 1)
                    dve.wait_ge(a.roped_s, n + t + 1)
                    if reused(kind, t, 2):
                        dve.wait_ge(a.qkT_ready, n + t - 1)
                    dve.tensor_tensor(qr[t % 2][:, :], t1[t % 2][:, :], t2[t % 2][:, :], ALU.add)\
                        .then_inc(a.qr_ready, 1)
                t = u - D_QKV
                if runs(kind, u, D_QKV):
                    if local:
                        dve.wait_ge(a.squared, n + t + 1)
                        if reused(kind, t, 2):
                            dve.wait_ge(a.rs_ready, n + t - 1)
                        dve.tensor_reduce(ss[t % 2][:, :], heads(sq[t % 2][:, :]), AX.X, ALU.add)\
                            .then_inc(a.summed, 1)
                        dve.wait_ge(a.summed, n + t + 1)
                        dve.tensor_scalar(ssc[t % 2][:, :], ss[t % 2][:, :], L2_EPS, None, ALU.max)\
                            .then_inc(a.clamped, 1)
                    else:
                        dve.wait_ge(a.v_ready, n + t + 1)
                        if runs(kind, u, D_OUT):
                            dve.wait_ge(a.oT_ready, n + u - D_OUT + 1)
                        if reused(kind, t, GROUPS):
                            dve.wait_ge(a.o_ready, n + t - GROUPS + 1)
                        g = t % GROUPS
                        dve.tensor_tensor(vt[g][:, :], v_ps, bv[:, g * GV:(g + 1) * GV], ALU.add)\
                            .then_inc(a.v_moved, 1)
                t = u - D_PROB
                if runs(kind, u, D_PROB):
                    dve.wait_ge(a.exp_ready, n + t + 1)
                    dve.reciprocal(rec[t % 2][:, :], sums[t % 2][:, :]).then_inc(a.rec_ready, 1)
                    dve.wait_ge(a.o_ready, n + t + 1)
                    dve.wait_ge(a.rec_ready, n + t + 1)
                    if reused(kind, t, 2):
                        dve.wait_ge(a.oT_ready, n + t - 1)
                    dve.tensor_tensor(on[t % 2][:, :].rearrange("p (a r e) -> p a r e", a=2, r=2),
                                      o_ps.rearrange("p (a r e) -> p a r e", a=2, r=2),
                                      over(rec[t % 2][:, :].rearrange("p (r a) -> p a r", r=2), [P, 2, 2, HD], 3),
                                      ALU.mult).then_inc(a.on_ready, 1)
            return tick

        def act_tick(act, local):
            def tick(kind, u, n, q, i):
                if runs(kind, u, D_PREP) and u % GROUPS == 0 and local:
                    b = u // GROUPS
                    if kind != "first":
                        act.wait_ge(a.v_ready, n + u - GROUPS)
                    at = (2 * i + b) * P
                    act.copy(xs[b % 2][0:HALF, :], ZT[0:HALF, bass.ds(at, P)]).then_inc(s.xs_ready, 1)
                    act.copy(xs[b % 2][HALF:P, 1:P], ZT[HALF:P, bass.ds(at, P - 1)])\
                        .then_inc(s.xs_ready, 1)
                t = u - D_QKV
                if runs(kind, u, D_QKV) and local:
                    act.wait_ge(a.qk_ready, n + t + 1)
                    if reused(kind, t, 2):
                        act.wait_ge(a.summed, n + t - 1)
                    act.activation(sq[t % 2][:, :], qk_ps[t % 2][:, :], ACT.Square).then_inc(a.squared, 1)
                t = u - D_SCORE
                if runs(kind, u, D_SCORE):
                    act.wait_ge(a.negmax_ready, n + t + 1)
                if runs(kind, u, D_PREP) and u % GROUPS == 0 and not local:
                    b = u // GROUPS
                    act.wait_ge(s.cond_ready, q + b + 1)
                    if kind != "first":
                        act.wait_ge(a.v_ready, n + u - GROUPS - D_QKV + 1)
                    act.activation(ys[b % 2][:, :], cond_ps, ACT.Identity, bias=wsel[:, b % 2, P:P + 1])\
                        .then_inc(s.ys_ready, 1)
                t = u - D_SCORE
                if runs(kind, u, D_SCORE):
                    if reused(kind, t, 2):
                        act.wait_ge(a.pT_ready, n + t - 1)
                        act.wait_ge(a.rec_ready, n + t - 1)
                    for h in range(GH):
                        ex = act.activation(pr[t % 2][:, h * P:(h + 1) * P], sc_ps[:, h // 2, h % 2 * P:(h % 2 + 1) * P],
                                            ACT.Exp, bias=negmax[t % 2][:, h:h + 1],
                                            scale=1.0 if local else HD ** -0.5, accum_out=sums[t % 2][:, h:h + 1])
                    ex.then_inc(a.exp_ready, 1)
                if runs(kind, u, D_QKV):
                    act.wait_ge(a.v_ready, n + u - D_QKV + 1)
                if runs(kind, u, D_OUT):
                    act.wait_ge(a.oT_ready, n + u - D_OUT + 1)
                t = u - D_QKV
                if runs(kind, u, D_QKV) and local:
                    if reused(kind, t, GROUPS):
                        act.wait_ge(a.o_ready, n + t - GROUPS + 1)
                    act.copy(vt[t % GROUPS][:, :], v_ps).then_inc(a.v_moved, 1)
                elif runs(kind, u, D_QKV):
                    act.wait_ge(a.v_moved, n + t + 1)
                t = u - D_OUT
                if runs(kind, u, D_OUT):
                    if t % GROUPS == 0 and reused(kind, t, BODY):
                        act.wait_ge(a.y_ready, q + t // GROUPS - 1)
                    g = t % GROUPS
                    act.copy(oT[(t // GROUPS) % 2][:, g * GV:(g + 1) * GV], oT_ps).then_inc(a.oT_moved, 1)
                t = u - D_ROPE
                if runs(kind, u, D_ROPE):
                    act.wait_ge(a.qkT_ready, n + t + 1)
                    if reused(kind, t, 2):
                        act.wait_ge(a.sc_ready, n + t - 1)
                    act.copy(qkT[t % 2][:, :], qkT_ps[:, :]).then_inc(a.qkT_moved, 1)
            return tick

        def pool_tick(pool, local, l=None):
            def tick(kind, u, n, q, i):
                if runs(kind, u, D_PREP) and u % GROUPS == 0 and not local:
                    b = u // GROUPS
                    if kind != "first":
                        pool.wait_ge(s.ys_ready, q + b - 1)
                    who = pool.value_load(subject[0:1, bass.ds(2 * i + b, 1)], min_val=0, max_val=SUBJ - 1)
                    pool.tensor_copy(wsel[:, b % 2, :], condT[:, bass.ds(who, 1), :])\
                        .then_inc(s.wsel_ready, 1)
                t = u - D_ROPE
                if runs(kind, u, D_ROPE) and local:
                    if kind == "first" and t == 0:
                        pool.wait_ge(s.tables_ready, l * 3 + 3)
                    pool.wait_ge(a.normed, n + t + 1)
                    if reused(kind, t, 2):
                        pool.wait_ge(a.qr_ready, n + t - 1)
                    pool.tensor_tensor(t2[t % 2][:, :].rearrange("p (i h f e) -> p i h f e", i=2, h=GH, f=2),
                                       qn[t % 2][:, :].rearrange("p (i h f e) -> p i h f e", i=2, h=GH, f=2)
                                       [:, :, :, ::-1, :],
                                       over(tabs[:, :, :].rearrange("p i (f e) -> p i f e", f=2),
                                            [P, 2, GH, 2, HD // 2], 2), ALU.mult).then_inc(a.roped_s, 1)
                t = u - D_QKV
                if runs(kind, u, D_QKV) and local:
                    pool.wait_ge(a.clamped, n + t + 1)
                    if reused(kind, t, 2):
                        pool.wait_ge(a.normed, n + t - 1)
                    pool.tensor_tensor(rs[t % 2][:, :], ssc[t % 2][:, :], neg_half[:, 0:8], ALU.pow)\
                        .then_inc(a.rs_ready, 1)
            return tick


        def images(eng, tick):
            def chunks_of(b):
                with eng.Fori(1, RG_BODIES) as i:
                    for u in range(RG_BODY):
                        tick("steady", u, b * RG_CHUNKS + i * RG_BODY, b, i * RG_BODY)
            for u in range(RG_BODY):
                tick("first", u, 0, 0, 0)
            chunks_of(0)
            with eng.Fori(1, B) as b:
                for u in range(RG_BODY):
                    tick("turn", u, b * RG_CHUNKS, b, 0)
                chunks_of(b)
            for u in range(RG_RED):
                tick("last", u, B * RG_CHUNKS, B, 0)

        def in_turn(kind, u, delay):
            return kind in ("steady", "turn") or runs(kind, u, delay)

        def pe_image(pe):
            def tick(kind, u, n, b, c):
                t = u - RG_X
                if in_turn(kind, u, RG_X):
                    if kind in ("first", "turn") and t == 0:
                        pe.wait_ge(s.rg_image, b + 1)
                    pe.wait_ge(s.rg_hat, n + t + 1)
                    if kind != "first" or t >= 2:
                        pe.wait_ge(s.rg_prod, n + t - 1)
                    pe.matmul(qk_ps[t % 2][:, :], rg_x[:, :], rg_wx[t % RG_BODY][:, :], start=True, stop=True)\
                        .then_inc(s.rg_xb, 1)
                t = u - RG_RED
                if in_turn(kind, u, RG_RED):
                    pe.wait_ge(s.rg_prod, n + t + 1)
                    if kind == "turn" and t == 0:
                        pe.wait_ge(s.rg_moved, b)
                    row = (c + t) * RG_ROWS if t >= 0 or kind == "steady" else (RG_CHUNKS + t) * RG_ROWS
                    for r in range(RG_ROWS):
                        mm = pe.matmul(qkT_ps[:, bass.ds(row + r, 1)], rg_p[t % 2][:, r * P:(r + 1) * P],
                                       ones[:, 0:1], start=True, stop=True)
                    mm.then_inc(s.rg_red, 1)
            return tick

        def dve_image(dve):
            def tick(kind, u, n, b, c):
                t = u
                if kind != "last":
                    if kind != "first":
                        dve.wait_ge(s.rg_hat, n + t - RG_BODY + 1)
                    row = (n + t) * RG_ROWS
                    dve.tensor_tensor(rg_ux[t][:, :].rearrange("p (r w) -> p r w", r=RG_ROWS),
                                      over(rg_xcol[:, bass.ds(b * P, P)], [P, RG_ROWS, P], 1),
                                      over(rg_xrow[:, bass.ds(row, RG_ROWS)], [P, RG_ROWS, P], 2), ALU.add)\
                        .then_inc(s.rg_xarg, 1)
                t = u - RG_PROD
                if in_turn(kind, u, RG_PROD):
                    dve.wait_ge(s.rg_xb, n + t + 1)
                    dve.wait_ge(s.rg_hat, n + t + 1)
                    if kind != "first" or t >= 2:
                        dve.wait_ge(s.rg_red, n + t - 1)
                    dve.tensor_tensor(rg_p[t % 2][:, :], qk_ps[t % 2][:, :], rg_wy[t % RG_BODY][:, :], ALU.mult)\
                        .then_inc(s.rg_prod, 1)
                t = u
                if kind != "last":
                    dve.wait_ge(s.rg_xarg, n + t + 1)
                    bits = rg_ux[t][:, :].bitcast(I32)
                    dve.tensor_scalar(bits, bits, 0x7FFFFFFF, None, ALU.bitwise_and).then_inc(s.rg_xabs, 1)
                if kind in ("first", "turn") and u == 0:
                    if kind == "turn":
                        dve.wait_ge(s.rg_xb, n)
                    dve.tensor_copy(rg_x[:, :], XT[:, bass.ds(b * P, P)]).then_inc(s.rg_image, 1)
            return tick

        def act_image(act):
            def tick(kind, u, n, b, c):
                t = u
                if kind != "last":
                    act.wait_ge(s.rg_yarg, n + t + 1)
                    act.activation(rg_uy[t][:, :], rg_uy[t][:, :], ACT.Abs).then_inc(s.rg_yabs, 1)
                t = u - RG_HAT
                if in_turn(kind, u, RG_HAT):
                    act.wait_ge(s.rg_xabs, n + t + 1)
                    act.wait_ge(s.rg_yabs, n + t + 1)
                    if kind != "first" or t >= RG_BODY:
                        act.wait_ge(s.rg_xb, n + t - RG_BODY + 1)
                        act.wait_ge(s.rg_prod, n + t - RG_BODY + 1)
                    act.activation(rg_w[t % RG_BODY][:, :, :], rg_u[t % RG_BODY][:, :, :], ACT.Relu, bias=1.0, scale=-1.0)\
                        .then_inc(s.rg_hat, 1)
                if u == RG_RED - 1 and kind in ("turn", "last"):
                    act.wait_ge(s.rg_red, n)
                    act.copy(ZT[:, bass.ds(b * P - P, P)], qkT_ps[:, 0:P]).then_inc(s.rg_moved, 1)
            return tick

        def pool_image(pool):
            def tick(kind, u, n, b, c):
                if kind != "last":
                    if kind != "first":
                        pool.wait_ge(s.rg_hat, n + u - RG_BODY + 1)
                    row = (n + u) * RG_ROWS
                    pool.tensor_tensor(rg_uy[u][:, :].rearrange("p (r w) -> p r w", r=RG_ROWS),
                                       over(rg_ycol[:, bass.ds(b * P, P)], [P, RG_ROWS, P], 1),
                                       over(rg_yrow[:, bass.ds(row, RG_ROWS)], [P, RG_ROWS, P], 2), ALU.add)\
                        .then_inc(s.rg_yarg, 1)
            return tick

        def shift_in(act, c, l):
            act.wait_ge(a.added, l * B + B + CH * (c + 1))
            lo = ZT[0:HALF, c * CW:(c + 1) * CW]
            hi = ZT[HALF:P, c * CW:(c + 1) * CW].rearrange("p (b t) -> p b t", b=CH)
            if c >= 2:
                act.wait_ge(s.lf_centred, l * NCH + c - 1)
            act.copy(xf[c % 2][0:HALF, :], lo).then_inc(s.lf_shifted, 1)
            act.copy(xf[c % 2][HALF:P, :].rearrange("p (b t) -> p b t", b=CH)[:, :, 1:P], hi[:, :, 0:P - 1])\
                .then_inc(s.lf_shifted, 1)

        def ffn_pe(pe, l):
            pe.wait_ge(s.wffn_loaded, l * 48 + 48)

            def mean(c):
                pe.wait_ge(s.lf_shifted, l * (2 * NCH) + 2 * (c + 1))
                if c >= 1:
                    pe.wait_ge(s.lf_centred, l * NCH + c)
                pe.matmul(qk_ps[0][:, :], mean_w[:, :], xf[c % 2][:, :], start=True, stop=True)\
                    .then_inc(s.lf_mean, 1)

            def var(c):
                pe.wait_ge(s.lf_squared, l * NCH + c + 1)
                if c >= 1:
                    pe.wait_ge(s.lf_normed, l * NCH + c)
                for j in range(CH):
                    mm = pe.matmul(qk_ps[1][:, j:j + 1], xq[c % 2][:, j * P:(j + 1) * P], mean_w[:, 0:1],
                                   start=True, stop=True)
                mm.then_inc(s.lf_var, 1)

            def spread(c):
                pe.wait_ge(s.lf_rstd, l * NCH + c + 1)
                for j in range(CH):
                    mm = pe.transpose(qk_ps[1][:, j * P:(j + 1) * P], xr[:, j:j + 1].to_broadcast([P, P]), ident[:, :])
                mm.then_inc(s.lf_spread, 1)

            def hidden(c, j):
                k = 3 * c + j
                o, w = FCH[j]
                if j == 0:
                    pe.wait_ge(s.lf_xn, l * NCH + c + 1)
                if k >= 2:
                    pe.wait_ge(s.lf_gated, l * 12 + k - 1)
                pe.matmul(bank[2 + k % 2][0:w, :], w1[:, o:o + w], xn[c % 2][:, :], start=True, stop=True)
                pe.matmul(bank[4 + k % 2][0:w, :], w1[:, INNER + o:INNER + o + w], xn[c % 2][:, :],
                          start=True, stop=True).then_inc(s.lf_h, 1)

            def down(c):
                if c >= 1:
                    pe.wait_ge(s.lf_state, l * NCH + c)
                for j, (o, w) in enumerate(FCH):
                    pe.wait_ge(s.lf_gated, l * 12 + 3 * c + j + 1)
                    mm = pe.matmul(scores[:, 0, :], w2[0:w, j, :], hg[c % 2][j][0:w, :], start=(j == 0), stop=(j == 2))
                mm.then_inc(s.lf_y, 1)

            mean(0)
            var(0)
            spread(0)
            for c in range(NCH):
                if c + 1 < NCH:
                    mean(c + 1)
                hidden(c, 0)
                hidden(c, 1)
                if c + 1 < NCH:
                    var(c + 1)
                hidden(c, 2)
                if c + 1 < NCH:
                    spread(c + 1)
                down(c)

        def ffn_dve(dve, l):
            def centre(c):
                dve.wait_ge(s.lf_mean, l * NCH + c + 1)
                if c >= 2:
                    dve.wait_ge(s.lf_squared, l * NCH + c - 1)
                    dve.wait_ge(s.lf_normed, l * NCH + c - 1)
                dve.tensor_tensor(xc[c % 2][:, :], xf[c % 2][:, :], qk_ps[0][:, :], ALU.subtract)\
                    .then_inc(s.lf_centred, 1)

            def vareps(c):
                dve.wait_ge(s.lf_var, l * NCH + c + 1)
                if c >= 1:
                    dve.wait_ge(s.lf_rstd, l * NCH + c)
                dve.tensor_scalar(xv, qk_ps[1][:, 0:CH], LN_EPS, None, ALU.add).then_inc(s.lf_vareps, 1)

            def norm(c):
                dve.wait_ge(s.lf_spread, l * NCH + c + 1)
                dve.wait_ge(s.lf_centred, l * NCH + c + 1)
                dve.tensor_tensor(xc[c % 2][:, :], xc[c % 2][:, :], qk_ps[1][:, :], ALU.mult).then_inc(s.lf_normed, 1)
                dve.wait_ge(s.lf_normed, l * NCH + c + 1)
                if c >= 2:
                    dve.wait_ge(s.lf_h, l * 12 + 3 * (c - 1))
                dve.tensor_scalar(xn[c % 2][:, :], xc[c % 2][:, :], cols[:, bass.ds(l + R_LNG, 1)],
                                  cols[:, bass.ds(l + R_LNB, 1)], ALU.mult, ALU.add).then_inc(s.lf_xn, 1)

            def gate(c, j):
                k = 3 * c + j
                w = FCH[j][1]
                dve.wait_ge(s.lf_gelu, l * 12 + k + 1)
                if c >= 2 and j == 0:
                    dve.wait_ge(s.lf_y, l * NCH + c - 1)
                dve.scalar_tensor_tensor(hg[c % 2][j][0:w, :], bank[2 + k % 2][0:w, :],
                                         cols[0:w, bass.ds(l + R_B1 + DEPTH * j, 1)], gl[k % 2][0:w, :],
                                         ALU.add, ALU.mult).then_inc(s.lf_gated, 1)

            def state(c):
                dve.wait_ge(s.lf_y, l * NCH + c + 1)
                dve.scalar_tensor_tensor(ZT[:, c * CW:(c + 1) * CW], scores[:, 0, :], cols[:, bass.ds(l + R_B2, 1)],
                                         ZT[:, c * CW:(c + 1) * CW], ALU.add, ALU.add).then_inc(s.lf_state, 1)

            centre(0)
            vareps(0)
            norm(0)
            for c in range(NCH):
                if c + 1 < NCH:
                    centre(c + 1)
                gate(c, 0)
                gate(c, 1)
                if c + 1 < NCH:
                    vareps(c + 1)
                gate(c, 2)
                if c + 1 < NCH:
                    norm(c + 1)
                state(c)

        def ffn_act(act, l):
            def square(c):
                act.wait_ge(s.lf_centred, l * NCH + c + 1)
                if c >= 2:
                    act.wait_ge(s.lf_var, l * NCH + c - 1)
                act.activation(xq[c % 2][:, :], xc[c % 2][:, :], ACT.Square).then_inc(s.lf_squared, 1)

            def gelu(c, j):
                k = 3 * c + j
                w = FCH[j][1]
                act.wait_ge(s.lf_h, l * 12 + k + 1)
                if k >= 2:
                    act.wait_ge(s.lf_gated, l * 12 + k - 1)
                act.activation(gl[k % 2][0:w, :], bank[4 + k % 2][0:w, :], ACT.Gelu,
                               bias=gate_b[0:w, j:j + 1]).then_inc(s.lf_gelu, 1)

            shift_in(act, 0, l)
            square(0)
            act.wait_ge(s.lf_bias, l + 1)
            for c in range(NCH):
                if c + 1 < NCH:
                    shift_in(act, c + 1, l)
                gelu(c, 0)
                if c + 1 < NCH:
                    square(c + 1)
                gelu(c, 1)
                gelu(c, 2)

        def ffn_pool(pool, l):
            for c in range(NCH):
                pool.wait_ge(s.lf_vareps, l * NCH + c + 1)
                if c >= 1:
                    pool.wait_ge(s.lf_spread, l * NCH + c)
                pool.tensor_tensor(xr, xv, neg_half[:, 0:CH], ALU.pow).then_inc(s.lf_rstd, 1)



        def sections(ap):
            return ap.rearrange("p (b c t) -> p b c t", b=CH, c=2)

        def seqs_of(ap):
            return ap.rearrange("p (b t) -> p b t", b=CH)

        def gla_pe(pe, c):
            at = bass.ds(c * CW, CW)
            pe.matmul(bank[0][:, :], lap[:, :], XT[:, at], start=True, stop=True).then_inc(s.g_lapx, 1)
            pe.wait_ge(s.g_src, c + 1)
            pe.matmul(bank[1][:, :], gwq[:, :], gsrc[:, :], start=True, stop=True).then_inc(s.g_qk, 1)
            pe.matmul(bank[2][:, :], gwk[:, :], gsrc[:, :], start=True, stop=True).then_inc(s.g_qk, 1)
            pe.matmul(bank[3][0:RANK, :], gwl1[:, :], gsrc[:, :], start=True, stop=True).then_inc(s.g_low, 1)
            pe.wait_ge(s.g_low_moved, c + 1)
            pe.matmul(bank[0][:, :], gwl2[:, :], glow[:, :], start=True, stop=True).then_inc(s.g_decay, 1)
            for j in range(CH):
                k = c * CH + j
                pe.wait_ge(s.g_vg_used, k) if j else pe.wait_ge(s.g_keys, 3 * c + 3)
                pe.matmul(bank[4][:, :], gsrc[:, j * P:(j + 1) * P], gwvg[:, :], start=True, stop=True)\
                    .then_inc(s.g_vg, 1)
                if j == 0:
                    pe.wait_ge(s.g_headed, c * GLH + GLH)
                else:
                    pe.wait_ge(s.g_masked, k)
                for h, keys in enumerate((gka, gkb)):
                    mm = pe.matmul(scores[:, 0, h * 2 * P:(h + 1) * 2 * P], keys[:, j * P:(j + 1) * P],
                                   gq4[:, j * 4 * P + h * 2 * P:j * 4 * P + (h + 1) * 2 * P], start=True, stop=True)
                mm.then_inc(s.g_a, 1)
                pe.wait_ge(s.g_masked, k + 1)
                pe.wait_ge(s.g_v_moved, k + 1)
                if j:
                    pe.wait_ge(s.g_o_read, k)
                for h in range(GLH):
                    mm = pe.matmul(bank[5][:, h * GLV:(h + 1) * GLV], ga[:, h * P:(h + 1) * P],
                                   gv[:, h * GLV:(h + 1) * GLV], start=True, stop=True)
                mm.then_inc(s.g_o, 1)
                pe.wait_ge(s.g_gated, k + 1)
                if j:
                    pe.wait_ge(s.g_oT_moved, k)
                for h in range(2):
                    mm = pe.transpose(bank[3][:, h * P:(h + 1) * P], gout[:, h * P:(h + 1) * P], ident[:, :])
                mm.then_inc(s.g_oT, 1)
            pe.wait_ge(s.g_oT_moved, c * CH + CH)
            for h in range(2):
                mm = pe.matmul(bank[1][:, :], gwo[:, h, :], goT[h][:, :], start=(h == 0), stop=(h == 1))
            mm.then_inc(s.g_y, 1)
            pe.wait_ge(s.g_added, c + 1)

        def gla_dve(dve, c):
            at = bass.ds(c * CW, CW)
            seqs = bass.ds(c * CH, CH)
            step_no = [0]

            def ordered(ins):
                step_no[0] += 1
                ins.then_inc(s.g_steps, 1)
                dve.wait_ge(s.g_steps, c * GLA_STEPS + step_no[0])
            x = XT[:, at]
            ge, gn, gl_, gy = xf[0], xf[1], t1[0], t1[1]
            dve.tensor_tensor(seqs_of(ge[:, :])[:, :, 1:P - 1], seqs_of(x)[:, :, 0:P - 2], seqs_of(x)[:, :, 2:P],
                              ALU.add).then_inc(s.g_edges, 1)
            dve.tensor_scalar(seqs_of(ge[:, :])[:, :, 0::P - 1], seqs_of(x)[:, :, 1::P - 3], 2.0, None, ALU.mult)\
                .then_inc(s.g_edges, 1)
            dve.tensor_scalar(gn[:, :], x, -1.0, 1.0, ALU.mult, ALU.add).then_inc(s.g_edges, 1)
            dve.wait_ge(s.g_edges, c * 3 + 3)
            ordered(dve.scalar_tensor_tensor(ge[:, :], x, -2.0, ge[:, :], ALU.mult, ALU.add))
            ordered(dve.tensor_tensor(seqs_of(gy[:, :]), seqs_of(x), over(diffuse[:, 2, seqs], [P, CH, P], 2), ALU.mult))
            ordered(dve.tensor_tensor(gy[:, :], gy[:, :], gn[:, :], ALU.mult))
            ordered(dve.tensor_tensor(seqs_of(ge[:, :]), seqs_of(ge[:, :]), over(diffuse[:, 1, seqs], [P, CH, P], 2),
                                      ALU.mult))
            dve.wait_ge(s.g_lapx, c + 1)
            ordered(dve.tensor_tensor(seqs_of(gl_[:, :]), seqs_of(bank[0][:, :]), over(diffuse[:, 0, seqs], [P, CH, P], 2),
                                      ALU.mult))
            ordered(dve.tensor_tensor(gl_[:, :], gl_[:, :], ge[:, :], ALU.add))
            dve.tensor_tensor(gsrc[:, :], gl_[:, :], gy[:, :], ALU.add).then_inc(s.g_src, 1)
            pre, low = gn, gy
            dve.wait_ge(s.g_src, c + 1)
            dve.wait_ge(s.g_decay, c + 1)
            ordered(dve.tensor_scalar(pre[:, :], bank[0][:, :], cols[:, R_GK:R_GK + 1], None, ALU.add))
            dve.tensor_scalar(low[:, :], pre[:, :], 0.0, None, ALU.min).then_inc(s.g_edge2, 1)
            dve.tensor_scalar(gl_[:, :].bitcast(I32), pre[:, :].bitcast(I32), 0x7FFFFFFF, None, ALU.bitwise_and)\
                .then_inc(s.g_abs, 1)
            dve.wait_ge(s.g_log, c + 1)
            dve.wait_ge(s.g_edge2, c + 1)
            ordered(dve.tensor_tensor(low[:, :], low[:, :], ge[:, :], ALU.subtract))
            ordered(dve.tensor_tensor_scan(gsum[:, :], restart[:, :], low[:, :], 0.0, ALU.mult, ALU.add))
            dve.tensor_tensor(seqs_of(gn[:, :])[:, :, 0:HALF],
                              sections(gsum[:, :])[:, :, 0, HALF - 1:HALF].to_broadcast([P, CH, HALF]),
                              sections(gsum[:, :])[:, :, 0, :], ALU.subtract).then_inc(s.g_sum, 1)
            dve.wait_ge(s.g_exp, c * 3 + 3)
            dve.wait_ge(s.g_qk, c * 2 + 2)
            dve.tensor_tensor(gka[:, :], bank[2][:, :], gen_[:, :], ALU.mult).then_inc(s.g_keys, 1)
            dve.tensor_tensor(sections(gkb[:, :])[:, :, 0, :], sections(bank[2][:, :])[:, :, 0, :],
                              seqs_of(ge[:, :])[:, :, 0:HALF], ALU.mult).then_inc(s.g_keys, 1)
            dve.tensor_tensor(sections(gkb[:, :])[:, :, 1, :], sections(bank[2][:, :])[:, :, 1, :],
                              sections(gen_[:, :])[:, :, 1, :], ALU.mult).then_inc(s.g_keys, 1)
            ordered(dve.scalar_tensor_tensor(gq1[:, :], gep[:, :], GLK ** -0.5, bank[1][:, :], ALU.mult, ALU.mult))
            for h in range(GLH):
                dve.tensor_scalar(gq4[:, :].rearrange("p (b c h t) -> p b c h t", b=CH, c=2, h=GLH)[:, :, :, h, :],
                                  sections(gq1[:, :]), headmask[:, h:h + 1], None, ALU.mult).then_inc(s.g_headed, 1)
            for j in range(CH):
                k = c * CH + j
                dve.wait_ge(s.g_a, k + 1)
                if j:
                    dve.wait_ge(s.g_o, k)
                dve.tensor_tensor(ga[:, :].rearrange("p (h c t) -> p h c t", h=GLH, c=2),
                                  scores[:, 0, :].rearrange("p (c h t) -> p h c t", h=GLH, c=2),
                                  over(gmask[:, :].rearrange("p (c t) -> p c t", c=2), [P, GLH, 2, HALF], 1),
                                  ALU.mult).then_inc(s.g_masked, 1)
                dve.wait_ge(s.g_sq, k + 1)
                ordered(dve.tensor_reduce(gss[:, :], gsq[:, :].rearrange("p (h e) -> p h e", h=GLH), AX.X, ALU.add))
                dve.tensor_scalar(gss[:, :], gss[:, :], 1.0 / GLV, LN_EPS, ALU.mult, ALU.add).then_inc(s.g_mean, 1)
                dve.wait_ge(s.g_rms, k + 1)
                dve.wait_ge(s.g_sg, k + 1)
                dve.tensor_tensor(gon[:, :].rearrange("p (h e) -> p h e", h=GLH),
                                  bank[5][:, 0:4 * GLV].rearrange("p (h e) -> p h e", h=GLH),
                                  over(grs[:, :], [P, GLH, GLV], 2), ALU.mult).then_inc(s.g_o_read, 1)
                dve.wait_ge(s.g_o_read, k + 1)
                ordered(dve.tensor_tensor(gon[:, :], gon[:, :], gsg[:, :], ALU.mult))
                if j:
                    dve.wait_ge(s.g_oT, k)
                dve.tensor_tensor(gout[:, :].rearrange("p (h e) -> p h e", h=GLH),
                                  gon[:, :].rearrange("p (h e) -> p h e", h=GLH),
                                  over(rmsw[:, :], [P, GLH, GLV], 1), ALU.mult).then_inc(s.g_gated, 1)
            dve.wait_ge(s.g_y, c + 1)
            dve.tensor_tensor(XT[:, at], bank[1][:, :], XT[:, at], ALU.add).then_inc(s.g_added, 1)
            dve.wait_ge(s.g_added, c + 1)

        def gla_act(act, c):
            ge, gn, gl_ = xf[0], xf[1], t1[0]
            act.wait_ge(s.g_low, c + 1)
            act.copy(glow[:, :], bank[3][0:RANK, :]).then_inc(s.g_low_moved, 1)
            act.wait_ge(s.g_abs, c + 1)
            act.activation(ge[:, :], gl_[:, :], ACT.Exp, scale=-1.0).then_inc(s.g_soft, 1)
            act.wait_ge(s.g_soft, c + 1)
            act.activation(ge[:, :], ge[:, :], ACT.Ln, bias=1.0).then_inc(s.g_log, 1)
            act.wait_ge(s.g_sum, c + 1)
            act.activation(gep[:, :], gsum[:, :], ACT.Exp, scale=1.0 / GATE_NORM).then_inc(s.g_exp, 1)
            act.activation(gen_[:, :], gsum[:, :], ACT.Exp, scale=-1.0 / GATE_NORM).then_inc(s.g_exp, 1)
            act.activation(seqs_of(ge[:, :])[:, :, 0:HALF], seqs_of(gn[:, :])[:, :, 0:HALF], ACT.Exp,
                           scale=1.0 / GATE_NORM).then_inc(s.g_exp, 1)
            for j in range(CH):
                k = c * CH + j
                act.wait_ge(s.g_vg, k + 1)
                if j:
                    act.wait_ge(s.g_gated, k)
                    act.wait_ge(s.g_o, k)
                act.copy(gv[:, :], bank[4][:, 0:GLH * GLV]).then_inc(s.g_v_moved, 1)
                act.activation(gsg[:, :], bank[4][:, GLH * GLV:2 * GLH * GLV], ACT.Silu).then_inc(s.g_sg, 1)
                act.wait_ge(s.g_sg, k + 1)
                act.wait_ge(s.g_v_moved, k + 1)
                act.sem_inc(s.g_vg_used, 1)
                act.wait_ge(s.g_o, k + 1)
                act.activation(gsq[:, :], bank[5][:, 0:4 * GLV], ACT.Square).then_inc(s.g_sq, 1)
                act.wait_ge(s.g_oT, k + 1)
                for h in range(2):
                    cp = act.copy(goT[h][:, j * P:(j + 1) * P], bank[3][:, h * P:(h + 1) * P])
                cp.then_inc(s.g_oT_moved, 1)
            act.wait_ge(s.g_y, c + 1)

        def gla_pool(pool, c):
            for j in range(CH):
                k = c * CH + j
                pool.wait_ge(s.g_mean, k + 1)
                pool.tensor_tensor(grs[:, :], gss[:, :], neg_half[:, 0:GLH], ALU.pow).then_inc(s.g_rms, 1)


        def gate_pe(pe):
            pe.wait_ge(s.e_loaded, 16 * 9)
            pe.wait_ge(s.e_first, 1)
            for e in range(NEXP):
                for j in range(FJ):
                    at = (e * FJ + j) * B
                    mm = pe.matmul(bank[0][:, at:at + B], up_of(e)[:, j * P:(j + 1) * P], first[:, :],
                                   start=True, stop=True)
            mm.then_inc(s.e_gate_h, 1)
            pe.wait_ge(s.e_gate_relu, 1)
            for e in range(NEXP):
                for j in range(FJ):
                    at = (e * FJ + j) * B
                    mm = pe.matmul(bank[1][:, e * B:(e + 1) * B], down_of(e)[:, j, :], gate_h[:, at:at + B],
                                   start=(j == 0), stop=(j == FJ - 1))
            mm.then_inc(s.e_gate_o, 1)
            pe.wait_ge(s.e_gate_in, 2)
            for k in range(4):
                mm = pe.matmul(bank[2][:, 0:B], gw1[:, k, :], gate_in[:, k * B:(k + 1) * B], start=(k == 0),
                               stop=(k == 3))
            mm.then_inc(s.e_gate_hid, 1)
            pe.wait_ge(s.e_gate_hid_relu, 1)
            pe.matmul(bank[3][0:B, 0:4], gate_hid[:, :], gw2[:, :], start=True, stop=True).then_inc(s.e_gate_logit, 1)
            pe.wait_ge(s.e_gate_diag, 1)
            pe.matmul(bank[4][:, 0:4 * B], ones[0:B, :], gate_diag[:, :], start=True, stop=True)\
                .then_inc(s.e_gate_all, 1)

        def gate_dve(dve):
            step_no = [0]

            def ordered(ins):
                step_no[0] += 1
                ins.then_inc(s.e_steps, 1)
                dve.wait_ge(s.e_steps, step_no[0])
            dve.wait_ge(s.g_added, NCH)
            dve.tensor_copy(first[:, :].unsqueeze(2), XT[:, :].rearrange("p (b t) -> p b t", b=B)[:, :, 0:1])\
                .then_inc(s.e_first, 1)
            dve.wait_ge(s.e_loaded, 16 * 9)
            tw = typew[:, :].rearrange("p (t e) -> p t e", t=TYPES)
            ordered(dve.tensor_reduce(typem[:, :], tw, AX.X, ALU.max))
            ordered(dve.tensor_tensor(tw, tw, over(typem[:, :], [P, TYPES, 4], 2), ALU.subtract))
            ordered(dve.tensor_scalar(typew[:, :], typew[:, :], 10.0, None, ALU.mult))
            dve.sem_inc(s.e_type_arg, 1)
            dve.wait_ge(s.e_type_exp, 1)
            ordered(dve.tensor_reduce(typem[:, :], tw, AX.X, ALU.add))
            ordered(dve.reciprocal(typem[:, :], typem[:, :]))
            ordered(dve.tensor_tensor(tw, tw, over(typem[:, :], [P, TYPES, 4], 2), ALU.mult))
            ordered(dve.tensor_copy(typef[:, :], typei[:, :]))
            for t in range(TYPES):
                ins = dve.tensor_scalar(is_type[:, :, t], typef[:, :], float(t), None, ALU.is_equal)
                ordered(ins)
            for i in range(2):
                ordered(dve.tensor_tensor(pick[:, 0:B * TYPES].rearrange("p (b t) -> p b t", b=B), is_type[:, :, :],
                                          over(typew[:, i:i + 11:5], [P, B, TYPES], 1), ALU.mult))
                ordered(dve.tensor_reduce(scale5[:, :, i], pick[:, 0:B * TYPES].rearrange("p (b t) -> p b t", b=B),
                                          AX.X, ALU.add))
            ordered(dve.memset(expw[:, :], 0.0))
            ew = expw[:, :].rearrange("p (e b) -> p e b", e=4)
            for t in range(TYPES):
                for i in range(2):
                    ordered(dve.scalar_tensor_tensor(ew[:, t + i, :], is_type[:, :, t], typew[:, 5 * t + i:5 * t + i + 1],
                                                     ew[:, t + i, :], ALU.mult, ALU.add))
            dve.wait_ge(s.e_gate_h, 1)
            dve.tensor_scalar(gate_h[:, :], bank[0][:, 0:NEXP * FJ * B], 0.0, None, ALU.max).then_inc(s.e_gate_relu, 1)
            dve.wait_ge(s.e_gate_o, 1)
            ordered(dve.tensor_tensor(pick[:, 0:4 * B], bank[1][:, 0:4 * B], expw[:, :], ALU.mult))
            dve.tensor_reduce(gate_in[:, 0:B], pick[:, 0:4 * B].rearrange("p (e b) -> p b e", e=4), AX.X, ALU.add)\
                .then_inc(s.e_gate_in, 1)
            dve.tensor_copy(gate_in[:, B:4 * B], bank[1][:, 4 * B:7 * B]).then_inc(s.e_gate_in, 1)
            dve.wait_ge(s.e_gate_hid, 1)
            dve.tensor_scalar(gate_hid[:, :], bank[2][:, 0:B], 0.0, None, ALU.max).then_inc(s.e_gate_hid_relu, 1)
            dve.wait_ge(s.e_gate_logit, 1)
            ordered(dve.tensor_reduce(gate_max[:, :], bank[3][0:B, 0:4], AX.X, ALU.max))
            ordered(dve.tensor_scalar(gate_p[:, :], bank[3][0:B, 0:4], gate_max[:, :], None, ALU.subtract))
            dve.sem_inc(s.e_gate_arg, 1)
            dve.wait_ge(s.e_gate_exp, 1)
            ordered(dve.tensor_reduce(gate_max[:, :], gate_p[:, :], AX.X, ALU.add))
            ordered(dve.reciprocal(gate_max[:, :], gate_max[:, :]))
            ordered(dve.tensor_scalar(gate_p[:, :], gate_p[:, :], gate_max[:, :], None, ALU.mult))
            dve.tensor_tensor(gate_diag[:, :].rearrange("p (b k) -> p b k", b=B), over(gate_p[:, :], [B, B, 4], 1),
                              over(ident[0:B, 0:B], [B, B, 4], 2), ALU.mult).then_inc(s.e_gate_diag, 1)
            dve.wait_ge(s.e_gate_all, 1)
            ga_ = bank[4][:, 0:4 * B].rearrange("p (b k) -> p b k", b=B)
            ordered(dve.tensor_copy(scale5[:, :, 2:5], ga_[:, :, 1:4]))
            dve.tensor_tensor(scale5[:, :, 0:2], scale5[:, :, 0:2], ga_[:, :, 0:1].to_broadcast([P, B, 2]), ALU.mult)\
                .then_inc(s.e_scales, 1)

        def gate_act(act):
            act.wait_ge(s.e_type_arg, 1)
            act.activation(typew[:, :], typew[:, :], ACT.Exp).then_inc(s.e_type_exp, 1)
            act.wait_ge(s.e_gate_arg, 1)
            act.activation(gate_p[:, :], gate_p[:, :], ACT.Exp).then_inc(s.e_gate_exp, 1)


        def experts_pe(pe, i):
            def up(u, x):
                job = i * 10 + u * 5 + x
                parity = (u * 5 + x) % 2
                if x == 0:
                    pe.wait_ge(s.e_chosen, i * 4 + u * 2 + 2)
                pe.wait_ge(s.e_relu, job - 1 + E_FREE)
                w = e_sel[u][:, x * F:(x + 1) * F] if x < 2 else up_of(2 + x)
                for j in range(FJ):
                    mm = pe.matmul(bank[parity][:, j * P:(j + 1) * P], w[:, j * P:(j + 1) * P],
                                   XT[:, bass.ds((i * 2 + u) * P, P)], start=True, stop=True)
                mm.then_inc(s.e_up, 1)

            def down(u, x):
                job = i * 10 + u * 5 + x
                parity = (u * 5 + x) % 2
                pe.wait_ge(s.e_relu, job + 1 + E_FREE)
                if x == 0:
                    pe.wait_ge(s.e_moved, i * 2 + u - 1 + E_FREE)
                w = e_sel[u][:, (2 + x) * F:(3 + x) * F].rearrange("p (j e) -> p j e", j=FJ) if x < 2 else down_of(2 + x)
                for j in range(FJ):
                    mm = pe.matmul(bank[2 + u][:, 0:P], w[:, j, :], e_h[parity][:, j * P:(j + 1) * P],
                                   start=(x == 0 and j == 0), stop=(x == 4 and j == FJ - 1))
                mm.then_inc(s.e_down, 1)
            jobs = [(u, x) for u in range(2) for x in range(5)]
            up(*jobs[0])
            for n, job in enumerate(jobs):
                if n + 1 < len(jobs):
                    up(*jobs[n + 1])
                down(*job)

        def experts_relu(eng, i, mine):
            for u in range(2):
                for x in range(5):
                    job, parity = i * 10 + u * 5 + x, (u * 5 + x) % 2
                    if parity != mine:
                        continue
                    eng.wait_ge(s.e_up, job + 1)
                    eng.wait_ge(s.e_relu, job + E_FREE)
                    eng.wait_ge(s.e_down, job - 1 + E_DOWN)
                    if x <= 1:
                        eng.wait_ge(s.e_scaled, i * 2 + u + 1)
                    if mine:
                        eng.tensor_scalar(e_h[parity][:, :], bank[parity][:, :], e_scale[u][:, x:x + 1], 0.0,
                                          ALU.mult, ALU.max).then_inc(s.e_relu, 1)
                    else:
                        eng.activation(e_h[parity][:, :], bank[parity][:, :], ACT.Relu,
                                       scale=e_scale[u][:, x:x + 1]).then_inc(s.e_relu, 1)
                if mine:
                    eng.wait_ge(s.e_down, i * 10 + u * 5 + 5 + E_DOWN)
                    eng.tensor_copy(ZT[:, bass.ds((i * 2 + u) * P, P)], bank[2 + u][:, 0:P]).then_inc(s.e_moved, 1)

        def experts_scale(dve, i):
            for u in range(2):
                dve.tensor_copy(e_scale[u][:, :].unsqueeze(1), scale5[:, bass.ds(i * 2 + u, 1), :])\
                    .then_inc(s.e_scaled, 1)

        def experts_pool(pool, i):
            for u in range(2):
                b = i * 2 + u
                pool.wait_ge(s.e_down, b * 5 - 8 + E_DOWN)
                who = pool.value_load(etype[0:1, bass.ds(b, 1)], min_val=0, max_val=TYPES - 1)
                pool.tensor_copy(e_sel[u][:, 0:2 * F], e_up_w[:, bass.ds(who * F, 2 * F)]).then_inc(s.e_chosen, 1)
                pool.tensor_copy(e_sel[u][:, 2 * F:4 * F], e_down_w[:, bass.ds(who * F, 2 * F)]).then_inc(s.e_chosen, 1)


        def moe_pe(pe, c):
            pe.wait_ge(s.m_copied, c + 1)
            for j in range(CH):
                mm = pe.matmul(bank[0][:, j * ME:(j + 1) * ME], m_src[:, j * P:(j + 1) * P], m_gate[:, :],
                               start=True, stop=True)
            mm.then_inc(s.m_logit, 1)
            pe.wait_ge(s.m_onehot, c + 1)
            for j in range(CH):
                mm = pe.transpose(bank[1][0:ME, j * P:(j + 1) * P], m_hot[:, j * ME:(j + 1) * ME], ident[:, :])
            mm.then_inc(s.m_turned, 1)
            pe.wait_ge(s.m_hot, 2 * c + 2)
            y = scores[:, 0, :]
            pe.matmul(y, m_b2[:, :], m_hotT[:, :], start=True, stop=False)

            def up(e):
                if e >= 2:
                    pe.wait_ge(s.m_masked, c * ME + e - 1)
                pe.matmul(bank[2 + e % 2][:, :], m_w1[:, e * P:(e + 1) * P], m_src[:, :], start=True, stop=True)
                pe.matmul(bank[4 + e % 2][:, :], m_pick[:, e * P:(e + 1) * P], m_hot16[:, :], start=True, stop=True)\
                    .then_inc(s.m_up, 1)
            up(0)
            for e in range(ME):
                if e + 1 < ME:
                    up(e + 1)
                pe.wait_ge(s.m_masked, c * ME + e + 1)
                mm = pe.matmul(y, m_w2[:, e * P:(e + 1) * P], m_h[e % 2][:, :], start=False, stop=(e == ME - 1))
            mm.then_inc(s.m_y, 1)

        def moe_dve(dve, c):
            at = bass.ds(c * CW, CW)
            step_no = [0]

            def ordered(ins):
                step_no[0] += 1
                ins.then_inc(s.m_steps, 1)
                dve.wait_ge(s.m_steps, c * 3 + step_no[0])
            by_seq = lambda ap: ap.rearrange("p (b e) -> p b e", b=CH)
            dve.tensor_copy(m_src[:, :], ZT[:, at]).then_inc(s.m_copied, 1)
            dve.wait_ge(s.m_logit, c + 1)
            ordered(dve.tensor_tensor(by_seq(m_logits[:, :]), by_seq(bank[0][:, 0:CH * ME]),
                                      over(m_gate_b[:, :], [P, CH, ME], 1), ALU.add))
            ordered(dve.tensor_reduce(m_max[:, :], by_seq(m_logits[:, :]), AX.X, ALU.max))
            dve.tensor_tensor(by_seq(m_logits[:, :]), by_seq(m_logits[:, :]), over(m_max[:, :], [P, CH, ME], 2),
                              ALU.is_equal).then_inc(s.m_equal, 1)
            dve.wait_ge(s.m_equal, c + 1)
            ordered(dve.tensor_tensor(by_seq(m_logits[:, :]), by_seq(m_logits[:, :]), over(m_rank[:, :], [P, CH, ME], 1),
                                      ALU.mult))
            dve.tensor_reduce(m_max[:, :], by_seq(m_logits[:, :]), AX.X, ALU.max).then_inc(s.m_first, 1)
            dve.wait_ge(s.m_first, c + 1)
            dve.tensor_tensor(by_seq(m_hot[:, :]), by_seq(m_logits[:, :]), over(m_max[:, :], [P, CH, ME], 2),
                              ALU.is_equal).then_inc(s.m_onehot, 1)
            dve.wait_ge(s.m_turned, c + 1)
            dve.tensor_copy(m_hotT[:, :], bank[1][0:ME, :]).then_inc(s.m_hot, 1)
            dve.tensor_copy(m_hot16[:, :], bank[1][0:ME, :]).then_inc(s.m_hot, 1)
            for e in range(ME):
                dve.wait_ge(s.m_gelu, c * ME + e + 1)
                dve.tensor_tensor(m_h[e % 2][:, :], m_g[e % 2][:, :], bank[4 + e % 2][:, :], ALU.mult)\
                    .then_inc(s.m_masked, 1)
            dve.wait_ge(s.m_y, c + 1)
            dve.tensor_tensor(XT[:, at], XT[:, at], scores[:, 0, :], ALU.add).then_inc(s.m_added, 1)

        def moe_act(act, c):
            for e in range(ME):
                act.wait_ge(s.m_up, c * ME + e + 1)
                if e >= 2:
                    act.wait_ge(s.m_masked, c * ME + e - 1)
                act.activation(m_g[e % 2][:, :], bank[2 + e % 2][:, :], ACT.Gelu,
                               bias=cols[:, R_MB1 + e:R_MB1 + e + 1]).then_inc(s.m_gelu, 1)

        @block.tensor
        def _(pe):
            pe.wait_ge(s.x_loaded, 32)
            pe.wait_ge(s.const_loaded, 16 * 7)
            for c in range(NCH):
                if c >= 2:
                    pe.wait_ge(s.x_state, c - 1)
                for j in range(CH):
                    mm = pe.transpose(qk_ps[c % 2][:, j * P:(j + 1) * P], xin[:, CH * c + j, :], ident[:, :])
                mm.then_inc(s.x_turned, 1)
            for c in range(2):
                for j in range(4):
                    mm = pe.transpose(scores[:, c, j * P:(j + 1) * P], cond_in[:, 4 * c + j, :], ident[:, :])
                mm.then_inc(s.cond_turned, 1)
            pe.wait_ge(s.small_loaded, 16 * 13)
            pe.transpose(pT_ps[:, 0:ROWS], rows[:, :], ident[0:ROWS, 0:ROWS]).then_inc(s.cond_turned, 1)
            pe.wait_ge(s.cond_state, 4)
            pe.wait_ge(s.x_state, NCH)
            pe.wait_ge(s.wqkv_loaded, 16 * 9)
            pe.wait_ge(s.wo_loaded, 16)
            attention_pass(pe, pe_tick(pe, False), 0, 0)
            pe.wait_ge(a.added, B)
            pe.wait_ge(s.rg_consts, 1)
            pe.wait_ge(a.qkT_moved, TICKS)
            images(pe, pe_image(pe))
            pe.wait_ge(s.rg_moved, B)
            pe.wait_ge(s.rg_consts, 9)
            with pe.Fori(0, DEPTH) as l:
                pe.wait_ge(s.wqkv_loaded, l * 48 + 16 * 12)
                pe.wait_ge(s.wo_loaded, l * 16 + 32)
                attention_pass(pe, pe_tick(pe, True), (l + 1) * TICKS, (l + 1) * B)
                ffn_pe(pe, l)
            pe.wait_ge(s.lf_state, DEPTH * NCH)
            pe.wait_ge(s.x_final, NCH)
            pe.wait_ge(s.g_loaded, 16 * 15)
            with pe.Fori(0, NCH) as c:
                gla_pe(pe, c)
            gate_pe(pe)
            pe.sem_inc(s.e_down, E_DOWN)
            with pe.Fori(0, B // 2) as i:
                experts_pe(pe, i)
            pe.wait_ge(s.m_loaded, 16 * 6)
            with pe.Fori(0, NCH) as c:
                moe_pe(pe, c)
            pe.wait_ge(s.m_added, NCH)
            for c in range(NCH):
                if c >= 2:
                    pe.wait_ge(s.out_ready, c - 1)
                for j in range(CH):
                    mm = pe.transpose(qk_ps[c % 2][:, j * P:(j + 1) * P], XT[:, (CH * c + j) * P:(CH * c + j + 1) * P],
                                      ident[:, :])
                mm.then_inc(s.out_turned, 1)

        @block.vector
        def _(dve):
            dve.memset(rows[:, :], 0.0).then_inc(s.rows_zeroed, 1)
            dve.memset(ones[:, :], 1.0).then_inc(s.rg_consts, 1)
            dve.memset(mean_w[:, :], 1.0 / P).then_inc(s.rg_consts, 1)
            dve.memset(xs[0][HALF:P, 0:1], 0.0).then_inc(s.rg_consts, 1)
            dve.memset(xs[1][HALF:P, 0:1], 0.0).then_inc(s.rg_consts, 1)
            for i in range(2):
                dve.memset(xf[i][HALF:P, :].rearrange("p (b t) -> p b t", b=CH)[:, :, 0:1], 0.0)\
                    .then_inc(s.rg_consts, 1)
            dve.wait_ge(s.const_loaded, 16 * 7)
            dve.tensor_copy(ident16[:, :], ident[:, :]).then_inc(s.rg_consts, 1)
            dve.tensor_copy(local_mask[:, :], mask_wide).then_inc(s.rg_consts, 1)
            dve.tensor_copy(m_pick[:, :], pick_wide).then_inc(s.rg_consts, 1)
            for c in range(NCH):
                dve.wait_ge(s.x_turned, c + 1)
                dve.tensor_copy(XT[:, c * CW:(c + 1) * CW], qk_ps[c % 2][:, :]).then_inc(s.x_state, 1)
            for c in range(2):
                dve.wait_ge(s.cond_turned, c + 1)
                dve.tensor_copy(condT[:, 4 * c:4 * c + 4, 0:P], scores[:, c, :].rearrange("p (s o) -> p s o", s=4))\
                    .then_inc(s.cond_state, 1)
            dve.wait_ge(s.cond_turned, 3)
            dve.tensor_copy(cols[:, :], pT_ps[:, 0:ROWS]).then_inc(s.cond_state, 1)
            dve.wait_ge(s.cond_state, 3)
            dve.tensor_copy(condT[:, :, P:P + 1], cols[:, R_CB:R_CB + SUBJ].unsqueeze(2)).then_inc(s.cond_state, 1)
            dve.wait_ge(s.l0bias_loaded, 16 * 5)
            attention_pass(dve, dve_tick(dve, False), 0, 0)
            dve.wait_ge(s.rg_params, 64)
            small = [0]

            def seq(ins):
                small[0] += 1
                ins.then_inc(s.rg_steps, 1)
                dve.wait_ge(s.rg_steps, small[0])
            seq(dve.tensor_scalar(phase[:, 0, :], angle[:, :], np.pi / 2, None, ALU.add))
            seq(dve.tensor_copy(phase[:, 1, :], angle[:, :]))
            seq(dve.tensor_scalar(turns[:, :, :], phase[:, :, :], 1 / (2 * np.pi), ROUND, ALU.mult, ALU.add))
            seq(dve.tensor_scalar(turns[:, :, :], turns[:, :, :], -ROUND, None, ALU.add))
            for part in TWO_PI:
                seq(dve.scalar_tensor_tensor(phase[:, :, :], turns[:, :, :], -part, phase[:, :, :],
                                             ALU.mult, ALU.add))
            dve.tensor_scalar(phase[:, :, :], phase[:, :, :], PI_BELOW, -PI_BELOW, ALU.min, ALU.max)\
                .then_inc(s.rg_ycolbles, 1)
            dve.wait_ge(s.rg_wave, 1)
            seq(dve.tensor_scalar(step[:, 0:2, :], wave[:, :, :], GRID, None, ALU.mult))
            seq(dve.tensor_scalar(step[:, 2, :], wave[:, 1, :], -GRID, None, ALU.mult))
            seq(dve.tensor_scalar(shift[:, :, :], offset[:, :, :], GRID, CENTRE, ALU.mult, ALU.add))
            with dve.Fori(0, B) as b:
                def per_image(out, k, add):
                    return dve.tensor_scalar(out[:, bass.ds(b * P, P)], grid[:, :], step[:, k, bass.ds(b, 1)],
                                             add, ALU.mult, ALU.add)
                per_image(rg_xcol, 1, negpart[:, 0:1])
                per_image(rg_ycol, 0, negpart[:, 0:1])
                per_image(rg_xrow, 0, shift[:, bass.ds(b, 1), 1])
                per_image(rg_yrow, 2, shift[:, bass.ds(b, 1), 0]).then_inc(s.rg_ycolbles, 1)
            dve.wait_ge(s.rg_ycolbles, B + 1)
            images(dve, dve_image(dve))
            for of_local in (a.summed, a.clamped, a.normed, a.roped_c):
                dve.sem_inc(of_local, TICKS)
            with dve.Fori(0, DEPTH) as l:
                if_scale = qkscale[:, bass.ds(l, 1), :, :].rearrange("p l i e -> p (l i) e")
                dve.tensor_tensor(tabc[:, :, :], ropec[:, :, :], if_scale, ALU.mult).then_inc(s.tables_ready, 1)
                for f in range(2):
                    mine, other = slice(f * HD // 2, (f + 1) * HD // 2), slice((1 - f) * HD // 2, (2 - f) * HD // 2)
                    dve.tensor_tensor(tabs[:, :, mine], ropes[:, :, mine], if_scale[:, :, other], ALU.mult)\
                        .then_inc(s.tables_ready, 1)
                dve.wait_ge(s.tables_ready, l * 3 + 3)
                dve.tensor_copy(gate_b[:, :].unsqueeze(2), cols[:, R_B1 + 3 * DEPTH:ROWS]
                                .rearrange("p (j l) -> p j l", l=DEPTH)[:, :, bass.ds(l, 1)]).then_inc(s.lf_bias, 1)
                attention_pass(dve, dve_tick(dve, True), (l + 1) * TICKS, (l + 1) * B)
                ffn_dve(dve, l)
            for c in range(NCH):
                at = slice(c * CW, (c + 1) * CW)
                dve.wait_ge(s.lf_state, (DEPTH - 1) * NCH + c + 1)
                dve.tensor_tensor(XT[:, at], XT[:, at], ZT[:, at], ALU.add).then_inc(s.x_final, 1)
            dve.wait_ge(s.x_final, NCH)
            dve.wait_ge(s.g_loaded, 16 * 15)
            with dve.Fori(0, NCH) as c:
                gla_dve(dve, c)
            gate_dve(dve)
            dve.wait_ge(s.e_scales, 1)
            dve.sem_inc(s.e_relu, E_FREE)
            dve.sem_inc(s.e_moved, E_FREE)
            with dve.Fori(0, B // 2) as i:
                experts_scale(dve, i)
                experts_relu(dve, i, 1)
            dve.wait_ge(s.e_moved, B + E_FREE)
            dve.wait_ge(s.m_loaded, 16 * 6)
            with dve.Fori(0, NCH) as c:
                moe_dve(dve, c)
            dve.wait_ge(s.m_added, NCH)
            for c in range(NCH):
                dve.wait_ge(s.out_turned, c + 1)
                dve.tensor_copy(ZT[:, c * CW:(c + 1) * CW], qk_ps[c % 2][:, :]).then_inc(s.out_ready, 1)

        @block.scalar
        def _(act):
            attention_pass(act, act_tick(act, False), 0, 0)
            act.wait_ge(s.rg_ycolbles, 1)
            act.activation(wave[:, :, :], phase[:, :, :], ACT.Sin).then_inc(s.rg_wave, 1)
            images(act, act_image(act))
            act.wait_ge(s.rg_moved, B)
            act.sem_inc(a.squared, TICKS)
            with act.Fori(0, DEPTH) as l:
                attention_pass(act, act_tick(act, True), (l + 1) * TICKS, (l + 1) * B)
                ffn_act(act, l)
                act.wait_ge(s.lf_state, l * NCH + NCH)
            with act.Fori(0, NCH) as c:
                gla_act(act, c)
            gate_act(act)
            with act.Fori(0, B // 2) as i:
                experts_relu(act, i, 0)
            with act.Fori(0, NCH) as c:
                moe_act(act, c)

        @block.gpsimd
        def _(pool):
            pool.memset(neg_half[:, :], -0.5).then_inc(s.consts_set, 1)
            pool.wait_ge(s.ids_loaded, 16)
            pool.wait_ge(s.cond_state, 4)
            attention_pass(pool, pool_tick(pool, False), 0, 0)
            pool.wait_ge(s.rg_ycolbles, B + 1)
            images(pool, pool_image(pool))
            for of_local in (a.rs_ready, a.roped_s):
                pool.sem_inc(of_local, TICKS)
            with pool.Fori(0, DEPTH) as l:
                attention_pass(pool, pool_tick(pool, True, l), (l + 1) * TICKS, (l + 1) * B)
                ffn_pool(pool, l)
            with pool.Fori(0, NCH) as c:
                gla_pool(pool, c)
            pool.wait_ge(s.e_loaded, 16 * 9)
            with pool.Fori(0, B // 2) as i:
                experts_pool(pool, i)


def constants():
    f = np.float32
    tok = np.arange(P)
    half = np.arange(0, HD, 2, dtype=np.float64)
    freqs = tok[:, None] / 10000.0 ** (half / HD)[None, :]
    scale = ((half + 0.4 * HD) / (1.4 * HD))[None, :] ** ((tok - P // 2) / (WINDOW // 2))[:, None]
    two = lambda t: np.concatenate([t, t], 1)
    qk = np.stack([8.0 * two(scale), 1.0 / two(scale)], 1)
    sign = np.where(np.arange(HD) < HD // 2, -1.0, 1.0)
    lag = tok[:, None] - tok[None, :]
    lap = np.eye(P, k=1) + np.eye(P, k=-1) - 2 * np.eye(P)
    lap[0, 1] = lap[P - 1, P - 2] = 2.0
    seen = (tok[:, None] <= tok[None, :])
    return {
        "c_lap": lap.T.astype(f).copy(),
        "c_pick": np.repeat(np.eye(ME), P, axis=1).astype(f),
        "c_rank": np.broadcast_to((ME - np.arange(ME)).astype(f), (P, ME)).copy(),
        "c_restart": np.broadcast_to((np.arange(CW) % HALF != 0).astype(f), (P, CW)).copy(),
        "c_gmask": seen.astype(f),
        "c_headmask": (tok[:, None] // GLK == np.arange(GLH)[None, :]).astype(f),
        "c_ident": np.eye(P, dtype=f),
        "c_local_mask": np.where((lag >= 0) & (lag <= WINDOW), 0.0, MASKED).astype(f),
        "c_keep": (lag >= 0).astype(f),
        "c_fill": np.where(lag < 0, f(FILL) * f(HD ** 0.5), 0).astype(f),
        "c_grid": np.broadcast_to((tok - P / 2).astype(f), (P, P)).copy(),
        "c_negpart": -tok[:, None].astype(f),
        "c_ropec": (two(np.cos(freqs))[:, None, :] * qk).astype(f),
        "c_ropes": ((two(np.sin(freqs)) * sign)[:, None, :] * qk).astype(f),
    }


def kernel(**inputs):
    import concourse.bacc as bacc
    from concourse.bass_utils import run_bass_kernel_spmd

    nc = bacc.Bacc("TRN2", target_bir_lowering=False, num_devices=1)
    arrays, drams = {}, {}
    for name, a in {**inputs, **constants()}.items():
        a = np.ascontiguousarray(a)
        arrays[f"in_{name}"] = a
        drams[name] = nc.dram_tensor(f"in_{name}", a.shape, mybir.dt.from_np(a.dtype), kind="ExternalInput").ap()
    out = nc.dram_tensor("out", (B, P, P), F32, kind="ExternalOutput").ap()
    build(nc, drams, out)
    r = run_bass_kernel_spmd(nc, [arrays], core_ids=[0])
    return r.results[0]["out"]
```

```python
from contextlib import ExitStack

import numpy as np

import concourse.bass as bass
from concourse import mybir

F32 = mybir.dt.float32
BF16 = mybir.dt.bfloat16
I32 = mybir.dt.int32
ALU = mybir.AluOpType
ACT = mybir.ActivationFunctionType
AX = mybir.AxisListType

B = 16
P = 128
N = B * P
HALF = P // 2
CH = 4
CW = CH * P
NCH = B // CH
HEADS, HD = 16, 64
GROUPS = 4
GH = HEADS // GROUPS
GV = GH * HD
TICKS = B * GROUPS
BODY = 2 * GROUPS
DEPTH = 6
WINDOW = 32
INNER = int(P * 4 * 2 / 3)
FCH = [(0, P), (P, P), (2 * P, INNER - 2 * P)]
SUBJ = 8
MASKED = -1e30
L2_EPS = 1e-12 ** 2
LN_EPS = 1e-5
FILL = 1e-10

RG_ROWS = 4
RG_CHUNKS = P // RG_ROWS
RG_BODY = 4
RG_BODIES = RG_CHUNKS // RG_BODY
RG_HAT, RG_X, RG_PROD = 1, 1, 3
GRID = (P - 1) / P
CENTRE = (P - 1) / 2
ROUND = 1.5 * 2.0 ** 23
TWO_PI = (6.28125, 0.0019350051879882812, 3.0199159795074593e-07)
PI_BELOW = 3.1415925

GLH, GLK, GLV, RANK = 4, 32, 64, 16
GATE_NORM = 16.0
GLA_STEPS = 6 + 3 + 1 + 2 * CH

TYPES, F, FJ, NEXP = 3, 512, 4, 7
E_FREE, E_DOWN = 2, 10
ME = 8

D_PREP, D_QKV, D_NORM, D_ROPE, D_TURN = 1, 2, 3, 4, 5
D_V, D_SCORE, D_EXP, D_REC, D_PROB, D_OUT, D_PROJ = 6, 6, 7, 8, 9, 10, 11

R_CB, R_LNG, R_LNB, R_B2, R_MB1, R_GK, R_BO = 0, 8, 14, 20, 26, 34, 35
R_B1 = 36
ROWS = R_B1 + 6 * DEPTH


def runs(kind, u, delay):
    t = u - delay
    return kind == "steady" or (kind == "first" and t >= 0) or (kind == "last" and t < 0)


def reused(kind, t, back):
    return kind != "first" or t >= back


def attention_pass(eng, tick, ticks, seqs, ahead=None):
    for u in range(2 * BODY):
        tick("first", u, ticks, seqs, 0)
    with eng.Fori(2, TICKS // BODY) as i:
        for u in range(BODY):
            tick("steady", u, ticks + i * BODY, seqs + i * 2, i)
    for u in range(D_PROJ):
        tick("last", u, ticks + TICKS, seqs + B, TICKS // BODY)
        if ahead:
            ahead(u)


class Semaphores:
    def __init__(self, sem):
        self.const_loaded = sem("const_loaded")
        self.x_loaded = sem("x_loaded")
        self.small_loaded = sem("small_loaded")
        self.rows_zeroed = sem("rows_zeroed")
        self.x_turned = sem("x_turned")
        self.x_state = sem("x_state")
        self.cond_turned = sem("cond_turned")
        self.cond_state = sem("cond_state")
        self.l0bias_loaded = sem("l0bias_loaded")
        self.consts_set = sem("consts_set")
        self.wqkv_loaded = sem("wqkv_loaded")
        self.wo_loaded = sem("wo_loaded")
        self.ids_loaded = sem("ids_loaded")
        self.wsel_ready = sem("wsel_ready")
        self.cond_ready = sem("cond_ready")
        self.ys_ready = sem("ys_ready")
        self.wffn_loaded = sem("wffn_loaded")
        self.tables_ready = sem("tables_ready")
        self.xs_ready = sem("xs_ready")
        self.out_ready = sem("out_ready")
        self.out_stored = sem("out_stored")
        self.out_turned = sem("out_turned")
        self.lf_shifted = sem("lf_shifted")
        self.lf_mean = sem("lf_mean")
        self.lf_centred = sem("lf_centred")
        self.lf_squared = sem("lf_squared")
        self.lf_var = sem("lf_var")
        self.lf_vareps = sem("lf_vareps")
        self.lf_rstd = sem("lf_rstd")
        self.lf_spread = sem("lf_spread")
        self.lf_normed = sem("lf_normed")
        self.lf_xn = sem("lf_xn")
        self.rg_xarg = sem("rg_xarg")
        self.rg_yarg = sem("rg_yarg")
        self.rg_yarg_first = sem("rg_yarg_first")
        self.rg_xabs = sem("rg_xabs")
        self.rg_yabs = sem("rg_yabs")
        self.rg_hat = sem("rg_hat")
        self.rg_xb = sem("rg_xb")
        self.rg_prod = sem("rg_prod")
        self.rg_summed = sem("rg_summed")
        self.rg_consts = sem("rg_consts")
        self.rg_params = sem("rg_params")
        self.rg_wave = sem("rg_wave")
        self.rg_steps = sem("rg_steps")
        self.rg_tables = sem("rg_tables")
        self.lf_bias = sem("lf_bias")
        self.lf_h = sem("lf_h")
        self.lf_gelu = sem("lf_gelu")
        self.lf_gated = sem("lf_gated")
        self.lf_y = sem("lf_y")
        self.lf_state = sem("lf_state")
        self.g_loaded = sem("g_loaded")
        self.g_lapx = sem("g_lapx")
        self.g_src = sem("g_src")
        self.g_qk = sem("g_qk")
        self.g_low = sem("g_low")
        self.g_low_moved = sem("g_low_moved")
        self.g_decay = sem("g_decay")
        self.g_keys = sem("g_keys")
        self.g_vg = sem("g_vg")
        self.g_vg_used = sem("g_vg_used")
        self.g_headed = sem("g_headed")
        self.g_masked = sem("g_masked")
        self.g_a = sem("g_a")
        self.g_o = sem("g_o")
        self.g_o_read = sem("g_o_read")
        self.g_gated = sem("g_gated")
        self.g_oT = sem("g_oT")
        self.g_oT_moved = sem("g_oT_moved")
        self.g_y = sem("g_y")
        self.g_added = sem("g_added")
        self.g_steps = sem("g_steps")
        self.g_edges = sem("g_edges")
        self.g_edge2 = sem("g_edge2")
        self.g_abs = sem("g_abs")
        self.g_soft = sem("g_soft")
        self.g_log = sem("g_log")
        self.g_sum = sem("g_sum")
        self.g_exp = sem("g_exp")
        self.g_sq = sem("g_sq")
        self.g_mean = sem("g_mean")
        self.g_rms = sem("g_rms")
        self.g_sg = sem("g_sg")
        self.g_v_moved = sem("g_v_moved")
        self.x_final = sem("x_final")
        self.e_loaded = sem("e_loaded")
        self.e_first = sem("e_first")
        self.e_gate_h = sem("e_gate_h")
        self.e_gate_relu = sem("e_gate_relu")
        self.e_gate_o = sem("e_gate_o")
        self.e_gate_in = sem("e_gate_in")
        self.e_gate_hid = sem("e_gate_hid")
        self.e_gate_hid_relu = sem("e_gate_hid_relu")
        self.e_gate_logit = sem("e_gate_logit")
        self.e_gate_diag = sem("e_gate_diag")
        self.e_gate_all = sem("e_gate_all")
        self.e_steps = sem("e_steps")
        self.e_type_arg = sem("e_type_arg")
        self.e_type_exp = sem("e_type_exp")
        self.e_gate_arg = sem("e_gate_arg")
        self.e_gate_exp = sem("e_gate_exp")
        self.e_scales = sem("e_scales")
        self.e_chosen = sem("e_chosen")
        self.e_up = sem("e_up")
        self.e_relu = sem("e_relu")
        self.e_moved = sem("e_moved")
        self.e_down = sem("e_down")
        self.e_scaled = sem("e_scaled")
        self.m_loaded = sem("m_loaded")
        self.m_copied = sem("m_copied")
        self.m_logit = sem("m_logit")
        self.m_onehot = sem("m_onehot")
        self.m_turned = sem("m_turned")
        self.m_hot = sem("m_hot")
        self.m_up = sem("m_up")
        self.m_masked = sem("m_masked")
        self.m_y = sem("m_y")
        self.m_steps = sem("m_steps")
        self.m_equal = sem("m_equal")
        self.m_first = sem("m_first")
        self.m_gelu = sem("m_gelu")
        self.m_added = sem("m_added")


class AttentionSemaphores:
    def __init__(self, sem):
        self.qk_ready = sem("attn_qk_ready")
        self.v_ready = sem("attn_v_ready")
        self.squared = sem("attn_squared")
        self.summed = sem("attn_summed")
        self.clamped = sem("attn_clamped")
        self.rs_ready = sem("attn_rs_ready")
        self.normed = sem("attn_normed")
        self.roped_c = sem("attn_roped_c")
        self.roped_s = sem("attn_roped_s")
        self.qr_ready = sem("attn_qr_ready")
        self.qkT_ready = sem("attn_qkT_ready")
        self.qkT_moved = sem("attn_qkT_moved")
        self.sc_ready = sem("attn_sc_ready")
        self.kept = sem("attn_kept")
        self.filled = sem("attn_filled")
        self.maxed = sem("attn_maxed")
        self.negmax_ready = sem("attn_negmax_ready")
        self.exp_ready = sem("attn_exp_ready")
        self.rec_ready = sem("attn_rec_ready")
        self.pT_ready = sem("attn_pT_ready")
        self.pT_moved = sem("attn_pT_moved")
        self.v_moved = sem("attn_v_moved")
        self.o_ready = sem("attn_o_ready")
        self.p_scaled = sem("attn_p_scaled")
        self.oT_moved = sem("attn_oT_moved")
        self.y_ready = sem("attn_y_ready")
        self.added = sem("attn_added")


def build(nc, d, out):
    with ExitStack() as ctx:
        def sb(name, shape, dt=F32):
            return ctx.enter_context(nc.sbuf_tensor(name, shape, dt))

        def sem(name):
            return ctx.enter_context(nc.semaphore(name))

        bank = [ctx.enter_context(nc.psum_tensor(f"bank{i}", [P, 512], F32)) for i in range(6)]
        scores = ctx.enter_context(nc.psum_tensor("scores", [P, 2, 512], F32))
        qk_ps = bank[0:2]
        qkT_ps = bank[2]
        sc_ps = scores[:, :, 0:2 * P]
        cond_ps = scores[:, 0, 2 * P:3 * P]
        pT_ps = bank[3]
        v_ps, y_ps = bank[4][:, 0:GV], bank[4][:, GV:GV + P]
        oT_ps = bank[5][:, 0:GV]

        XT = sb("XT", [P, N])
        ZT = sb("ZT", [P, N])
        ident = sb("ident", [P, P])
        ident16 = sb("ident16", [P, P], BF16)
        local_mask = sb("local_mask", [P, P], BF16)
        keep = sb("keep", [P, P])
        fill = sb("fill", [P, P])
        ropec = sb("ropec", [P, 2, HD])
        ropes = sb("ropes", [P, 2, HD])
        ones = sb("ones", [P, P])
        mean_w = sb("mean_w", [P, P])
        neg_half = sb("neg_half", [P, 8])
        rows = sb("rows", [ROWS, P])
        cols = sb("cols", [P, ROWS])
        wqk = sb("wqk", [P, GROUPS, 2, GV])
        wv = sb("wv", [P, HEADS * HD])
        wo = sb("wo", [P, HEADS * HD // P, P])
        w1 = sb("w1", [P, 2 * INNER])
        w2 = sb("w2", [P, 3, P])
        condT = sb("condT", [P, SUBJ, P + 1])
        wsel = sb("wsel", [P, 2, P + 1])
        subject = sb("subject", [1, B], I32)
        bqk = sb("bqk", [P, GROUPS, 2, GV])
        bv = sb("bv", [P, HEADS * HD])
        qkscale = sb("qkscale", [P, DEPTH, 2, HD])
        tabc = sb("tabc", [P, 2, HD])
        tabs = sb("tabs", [P, 2, HD])
        xs = [sb(f"xs{i}", [P, P]) for i in range(2)]
        ys = [sb(f"ys{i}", [P, P]) for i in range(2)]
        sq = [sb(f"sq{i}", [P, 512]) for i in range(2)]
        ss = [sb(f"ss{i}", [P, 8]) for i in range(2)]
        ssc = [sb(f"ssc{i}", [P, 8]) for i in range(2)]
        rs = [sb(f"rs{i}", [P, 8]) for i in range(2)]
        qn_pair = sb("qn_pair", [P, 2, 512])
        qn = [qn_pair[:, i, :] for i in range(2)]
        t1_pair = sb("t1_pair", [P, 2, 512])
        t1 = [t1_pair[:, i, :] for i in range(2)]
        t2_pair = sb("t2_pair", [P, 2, 512])
        t2 = [t2_pair[:, i, :] for i in range(2)]
        qr_pair = sb("qr_pair", [P, 2, 512])
        qr = [qr_pair[:, i, :] for i in range(2)]
        qkT = [sb(f"qkT{i}", [P, 512]) for i in range(2)]
        vt = [sb(f"vt{i}", [P, GV]) for i in range(GROUPS)]
        negmax = [sb(f"negmax{i}", [P, GH]) for i in range(2)]
        rowmax = [sb(f"rowmax{i}", [P, GH]) for i in range(2)]
        pr = [sb(f"pr{i}", [P, 512]) for i in range(2)]
        sums = [sb(f"sums{i}", [P, GH]) for i in range(2)]
        rec = [sb(f"rec{i}", [P, GH]) for i in range(2)]
        pT = [sb(f"pT{i}", [P, 512]) for i in range(2)]
        on = [sb(f"on{i}", [P, GV]) for i in range(2)]
        oT = [sb(f"oT{i}", [P, HEADS * HD]) for i in range(2)]
        angle = sb("angle", [P, B])
        offset = sb("offset", [P, B, 2])
        phase = sb("phase", [P, 2, B])
        turns = sb("turns", [P, 2, B])
        wave = sb("wave", [P, 2, B])
        step = sb("step", [P, 3, B])
        shift = sb("shift", [P, B, 2])
        grid = sb("grid", [P, P])
        negpart = sb("negpart", [P, 1])
        rg_xcol = sb("rg_xcol", [P, N])
        rg_yrow = sb("rg_yrow", [P, N])
        rg_xrow = sb("rg_xrow", [P, N])
        minus_index = sb("minus_index", [P, P])
        grid_part = sb("grid_part", [P, 1])
        y_of_column = sb("y_of_column", [P, B])
        rg_p = pr[0:2]
        rg_u = [sb(f"rg_u{i}", [P, 2, CW]) for i in range(2)] + [t1_pair, t2_pair]
        rg_w = [sb(f"rg_w{i}", [P, 2, CW]) for i in range(2)] + [qn_pair, qr_pair]
        pr += [rg_u[0][:, i, :] for i in range(2)]
        rg_ux, rg_uy = [u[:, 0, :] for u in rg_u], [u[:, 1, :] for u in rg_u]
        rg_wx, rg_wy = [w[:, 0, :] for w in rg_w], [w[:, 1, :] for w in rg_w]
        gate_b = sb("gate_b", [P, 3])
        xf = [sb(f"xf{i}", [P, CW]) for i in range(2)]
        xc, xq, xn = t1, t2, qr
        xv, xr = ssc[0][:, 0:CH], ssc[1][:, 0:CH]
        gl = qn
        hg = [[sb(f"hg{i}{j}", [P, CW]) for j in range(3)] for i in range(2)]
        xin = ZT[:, :].rearrange("p (b f) -> p b f", b=B)
        cond_in = oT[0][:, :].rearrange("p (s h) -> p s h", s=SUBJ)

        mask_wide, pick_wide = t1[0][:, 0:P], oT[1][0:ME, 0:ME * P]
        diffuse = sb("diffuse", [P, 3, B])
        lap = sb("lap", [P, P])
        gwq, gwk = sb("gwq", [P, P]), sb("gwk", [P, P])
        gwl1, gwl2 = sb("gwl1", [P, RANK]), sb("gwl2", [RANK, P])
        gwvg = sb("gwvg", [P, 2 * GLH * GLV])
        gwo = sb("gwo", [P, 2, P])
        rmsw = sb("rmsw", [P, GLV])
        restart = sb("restart", [P, CW])
        gmask = sb("gmask", [P, P])
        headmask = sb("headmask", [P, GLH])
        gsrc, glow = sq[0], sq[1][0:RANK, :]
        gsum, gep, gen_, gq1 = qn[0], qn[1], qr[0], qr[1]
        gka, gkb, ga, goT = t2[0], t2[1], pr, qkT
        gv, gsg, gout, gss, grs = vt[0:2], vt[2:4], on, negmax, rowmax
        gsq = [rg_u[0][:, i, 0:GLH * GLV] for i in range(2)]
        gon = [rg_u[1][:, i, 0:GLH * GLV] for i in range(2)]
        g_vg_ps, g_o_ps = (bank[4], bank[0]), (bank[5], bank[2])
        gq4 = wqk[:, :, :, :].rearrange("p g i n -> p (g i n)")

        e_up_w, e_down_w, e_sel = sb("e_up_w", [P, 4 * F]), rg_xcol, (rg_yrow, rg_xrow)
        l0_biases = bqk[:, :, :, :].rearrange("p g i n -> p (g i n)")
        share_up = l0_biases[:, 0:3 * F]
        share_down = sb("share_down", [P, 3, FJ, P])
        gw1, gw2 = l0_biases[:, 3 * F:].rearrange("p (k f) -> p k f", k=4), sb("gw2", [P, 4])
        first = sb("first", [P, B])
        gate_h = xf[0][:, 0:NEXP * FJ * B]
        gate_in, gate_hid = sb("gate_in", [P, 4 * B]), sb("gate_hid", [P, B])
        gate_p, gate_max, gate_diag = sb("gate_p", [B, 4]), sb("gate_max", [B, 1]), sb("gate_diag", [B, 4 * B])
        typew, typem = sb("typew", [P, TYPES * 4]), sb("typem", [P, TYPES])
        typei, etype = sb("typei", [P, B], I32), sb("etype", [1, B], I32)
        typef, is_type = sb("typef", [P, B]), sb("is_type", [P, B, TYPES])
        pick, expw = sb("pick", [P, 4 * B]), sb("expw", [P, 4 * B])
        scale5 = sb("scale5", [P, B, 5])
        e_scale = [sb(f"e_scale{i}", [P, 5]) for i in range(2)]
        e_h = t1
        m_w1, m_w2 = wv, wo[:, :, :].rearrange("p c e -> p (c e)")
        m_pick = sb("m_pick", [ME, ME * P], BF16)
        m_b2 = sb("m_b2", [ME, P])
        m_hotT, m_hot16 = qkT[0][0:ME, :], sb("m_hot16", [ME, CW], BF16)
        m_gate, m_gate_b, m_rank = sb("m_gate", [P, ME]), sb("m_gate_b", [P, ME]), sb("m_rank", [P, ME])
        m_logits, m_hot, m_max = sb("m_logits", [P, CH * ME]), sb("m_hot", [P, CH * ME]), sb("m_max", [P, CH])
        m_src, m_g, m_h = sq[0], t2, qn

        def up_of(e):
            return e_up_w[:, e * F:(e + 1) * F] if e < 4 else share_up[:, (e - 4) * F:(e - 3) * F]

        def down_of(e):
            return e_down_w[:, e * F:(e + 1) * F].rearrange("p (j e) -> p j e", j=FJ) if e < 4 \
                else share_down[:, e - 4, :, :]

        s = Semaphores(sem)

        a = AttentionSemaphores(sem)

        block = ctx.enter_context(nc.Block())

        def heads(ap):
            return ap.rearrange("p (h e) -> p h e", e=HD)

        def over(ap, shape, axis):
            return ap.unsqueeze(axis).to_broadcast(shape)

        @block.sync
        def _(sp):
            sp.dma_start(xin, d["x"].rearrange("b t f -> t b f")).then_inc(s.x_loaded, 16)
            sp.dma_start(ident[:, :], d["c_ident"]).then_inc(s.const_loaded, 16)
            sp.dma_start(cond_in, d["L0_cond_weight"].rearrange("s o h -> o s h")).then_inc(s.x_loaded, 16)
            sp.dma_start(mask_wide, d["c_local_mask"]).then_inc(s.const_loaded, 16)
            sp.dma_start(pick_wide, d["c_pick"]).then_inc(s.const_loaded, 16)
            sp.dma_start(keep[:, :], d["c_keep"]).then_inc(s.const_loaded, 16)
            sp.dma_start(fill[:, :], d["c_fill"]).then_inc(s.const_loaded, 16)
            sp.dma_start(ropec[:, :, :], d["c_ropec"]).then_inc(s.const_loaded, 16)
            sp.dma_start(ropes[:, :, :], d["c_ropes"]).then_inc(s.const_loaded, 16)
            sp.wait_ge(s.rows_zeroed, 1)
            small = [(R_CB, "L0_cond_bias"), (R_LNG, "L0_ffn_ln_g"), (R_LNB, "L0_ffn_ln_b"), (R_B2, "L0_ffn_b2"),
                     (R_MB1, "L1_ffn_b1")]
            for r, name in small:
                sp.dma_start(rows[r:r + d[name].shape[0], :], d[name]).then_inc(s.small_loaded, 16)
            sp.dma_start(rows[R_GK:R_GK + 1, :], d["L1_attn_bgk2"].unsqueeze(0)).then_inc(s.small_loaded, 16)
            sp.dma_start(rows[R_BO:R_BO + 1, :], d["L0_attn_Bias_output"].unsqueeze(0)).then_inc(s.small_loaded, 16)
            for half in range(2):
                for j, (o, w) in enumerate(FCH):
                    r = R_B1 + DEPTH * (3 * half + j)
                    sp.dma_start(rows[r:r + DEPTH, 0:w], d["L0_ffn_b1"][:, half * INNER + o:half * INNER + o + w])\
                        .then_inc(s.small_loaded, 16)
            sp.dma_start(subject[:, :], d["itok_B_0_7"].unsqueeze(0)).then_inc(s.ids_loaded, 16)
            for i, w in enumerate(("L0_attn_W_query", "L0_attn_W_key")):
                for g in range(GROUPS):
                    sp.dma_start(heads(wqk[:, g, i, :]), d[w][g * GH:(g + 1) * GH].rearrange("n e h -> e n h"))\
                        .then_inc(s.wqkv_loaded, 16)
            sp.dma_start(heads(wv[:, :]), d["L0_attn_W_values"].rearrange("n e h -> e n h"))\
                .then_inc(s.wqkv_loaded, 16)
            sp.dma_start(wo[:, :, :], d["L0_attn_W_output"].rearrange("n h e -> (n h) e")
                         .rearrange("(c p) e -> p c e", p=P)).then_inc(s.wo_loaded, 16)
            for i, w in enumerate(("L0_attn_Bias_query", "L0_attn_Bias_key")):
                sp.dma_start(bqk[:, :, i, :], d[w].rearrange("(g n) h -> g (n h)", g=GROUPS)
                             .partition_broadcast(P)).then_inc(s.l0bias_loaded, 16)
            sp.dma_start(bv[:, :], d["L0_attn_Bias_values"].rearrange("n h -> (n h)").partition_broadcast(P))\
                .then_inc(s.l0bias_loaded, 16)
            for i, w in enumerate(("L0_ffn_q_scale", "L0_ffn_k_scale")):
                sp.dma_start(qkscale[:, :, i, :], d[w].partition_broadcast(P)).then_inc(s.l0bias_loaded, 16)
            for i, w in enumerate(("condB_angle", "fside_Bx2_0")):
                sp.dma_start((angle, offset)[i][tuple([slice(None)] * (2 + i))], d[w].partition_broadcast(P))\
                    .then_inc(s.rg_params, 16)
            sp.dma_start(grid[:, :], d["c_grid"]).then_inc(s.rg_params, 16)
            sp.dma_start(negpart[:, :], d["c_negpart"]).then_inc(s.rg_params, 16)
            sp.dma_start(minus_index[:, :], d["c_minus_index"]).then_inc(s.rg_params, 16)
            sp.dma_start(grid_part[:, :], d["c_grid_part"]).then_inc(s.rg_params, 16)

            for z, name in enumerate(("condB_zX", "condB_zY", "condB_zR")):
                sp.dma_start(diffuse[:, z, :], d[name].partition_broadcast(P)).then_inc(s.g_loaded, 16)
            for to, name in ((lap, "c_lap"), (gwq, "L1_attn_Wq"), (gwk, "L1_attn_Wk"), (gwl1, "L1_attn_Wgk1"),
                             (gwl2, "L1_attn_Wgk2"), (restart, "c_restart"), (gmask, "c_gmask"),
                             (headmask, "c_headmask")):
                sp.dma_start(to[:, :], d[name]).then_inc(s.g_loaded, 16)
            for i, name in enumerate(("L1_attn_Wv", "L1_attn_Wg")):
                sp.dma_start(gwvg[:, i * GLH * GLV:(i + 1) * GLH * GLV], d[name]).then_inc(s.g_loaded, 16)
            sp.dma_start(gwo[:, :, :], d["L1_attn_Wo"].rearrange("(h p) e -> p h e", p=P)).then_inc(s.g_loaded, 16)
            sp.dma_start(rmsw[:, :], d["L1_attn_rms_w"].partition_broadcast(P)).then_inc(s.g_loaded, 16)

            def load_attention(src_qkv):
                for i in range(2):
                    sp.dma_start(wqk[:, :, i, :], src_qkv[:, i * HEADS * HD:(i + 1) * HEADS * HD]
                                 .rearrange("e (g n) -> e g n", g=GROUPS)).then_inc(s.wqkv_loaded, 16)
                sp.dma_start(wv[:, :], src_qkv[:, 2 * HEADS * HD:3 * HEADS * HD]).then_inc(s.wqkv_loaded, 16)

            def load_wo(src):
                sp.dma_start(wo[:, :, :], src.rearrange("(c p) e -> p c e", p=P)).then_inc(s.wo_loaded, 16)

            def load_ffn(up, dn):
                sp.dma_start(w1[:, :], up).then_inc(s.wffn_loaded, 16)
                sp.dma_start(w2[:, 0:2, :], dn[0:2 * P, :].rearrange("(j p) e -> p j e", p=P))\
                    .then_inc(s.wffn_loaded, 16)
                sp.dma_start(w2[0:FCH[2][1], 2, :], dn[2 * P:INNER, :]).then_inc(s.wffn_loaded, 16)

            load_ffn(d["L0_ffn_W1"][0], d["L0_ffn_W2"][0])
            sp.wait_ge(a.v_ready, TICKS)
            load_attention(d["L0_ffn_Wqkv"][0])
            sp.wait_ge(a.y_ready, B)
            load_wo(d["L0_ffn_Wo"][0])
            sp.wait_ge(s.rg_summed, B * RG_CHUNKS)
            sp.dma_start(e_up_w[:, :].rearrange("p (e f) -> p e f", e=4),
                         d["L1_cond2_expert_wi"].rearrange("e p f -> p e f")).then_inc(s.e_loaded, 16)
            sp.dma_start(e_down_w[:, :].rearrange("p (e j f) -> p e j f", e=4, j=FJ),
                         d["L1_cond2_expert_wo"].rearrange("e (j p) f -> p e j f", p=P)).then_inc(s.e_loaded, 16)
            sp.dma_start(share_up[:, :].rearrange("p (e f) -> p e f", e=3),
                         d["L1_cond2_share_wi"].rearrange("e p f -> p e f")).then_inc(s.e_loaded, 16)
            sp.dma_start(share_down[:, :, :, :],
                         d["L1_cond2_share_wo"].rearrange("e (j p) f -> p e j f", p=P)).then_inc(s.e_loaded, 16)
            sp.dma_start(gw1[:, :, :], d["L1_cond2_gate_w1"].rearrange("(k p) f -> p k f", p=P))\
                .then_inc(s.e_loaded, 16)
            sp.dma_start(gw2[:, :], d["L1_cond2_gate_w2"]).then_inc(s.e_loaded, 16)
            sp.dma_start(typew[:, :], d["L1_cond2_gate_vecs"].rearrange("t e -> (t e)").partition_broadcast(P))\
                .then_inc(s.e_loaded, 16)
            sp.dma_start(typei[:, :], d["itok_B_0_2"].partition_broadcast(P)).then_inc(s.e_loaded, 16)
            sp.dma_start(etype[:, :], d["itok_B_0_2"].unsqueeze(0)).then_inc(s.e_loaded, 16)
            sp.dma_start(m_b2[:, :], d["L1_ffn_b2"]).then_inc(s.m_loaded, 16)
            sp.dma_start(m_gate[:, :], d["L1_ffn_Wg"]).then_inc(s.m_loaded, 16)
            sp.dma_start(m_gate_b[:, :], d["L1_ffn_bg"].partition_broadcast(P)).then_inc(s.m_loaded, 16)
            sp.dma_start(m_rank[:, :], d["c_rank"]).then_inc(s.m_loaded, 16)
            with sp.Fori(1, DEPTH) as l:
                def of_layer(name):
                    return d[name][bass.ds(l, 1)].rearrange("l e n -> (l e) n")
                sp.wait_ge(a.v_ready, (l + 1) * TICKS)
                load_attention(of_layer("L0_ffn_Wqkv"))
                sp.wait_ge(a.y_ready, (l + 1) * B)
                load_wo(of_layer("L0_ffn_Wo"))
                sp.wait_ge(s.lf_y, l * NCH)
                load_ffn(of_layer("L0_ffn_W1"), of_layer("L0_ffn_W2"))
            sp.wait_ge(a.y_ready, (DEPTH + 1) * B)
            sp.dma_start(m_w1[:, :].rearrange("p (e i) -> p e i", e=ME), d["L1_ffn_W1"].rearrange("e p i -> p e i"))\
                .then_inc(s.m_loaded, 16)
            sp.dma_start(m_w2.rearrange("p (e i) -> p e i", e=ME), d["L1_ffn_W2"].rearrange("e p i -> p e i"))\
                .then_inc(s.m_loaded, 16)
            sp.wait_ge(s.out_ready, 4)
            sp.dma_start(out.rearrange("b t f -> t b f"), ZT[:, :].rearrange("p (b f) -> p b f", b=B))\
                .then_inc(s.out_stored, 16)
            sp.wait_ge(s.out_stored, 16)


        def starts(kind, u):
            t = u - D_PREP
            return t // GROUPS if runs(kind, u, D_PREP) and t % GROUPS == 0 else None

        def ends(kind, u):
            t = u - D_PROJ
            return t // GROUPS if runs(kind, u, D_PROJ) and t % GROUPS == GROUPS - 1 else None

        def pe_tick(pe, local):
            src = xs if local else ys

            def tick(kind, u, n, q, i):
                t = u - D_PROB
                if runs(kind, u, D_PROB):
                    pe.wait_ge(a.p_scaled, n + t + 1)
                    if reused(kind, t, 1):
                        pe.wait_ge(a.pT_moved, n + t)
                    for h in range(GH):
                        mm = pe.transpose(pT_ps[:, h * P:(h + 1) * P], pr[t % 4][:, h * P:(h + 1) * P], ident[:, :])
                    mm.then_inc(a.pT_ready, 1)
                b = ends(kind, u)
                if b is not None:
                    pe.wait_ge(a.oT_moved, n + u - D_PROJ + 1)
                    if runs(kind, u - 1, D_V):
                        pe.wait_ge(a.v_moved, n + u - D_V)
                    for c in range(8):
                        mm = pe.matmul(y_ps, wo[:, c, :], oT[b % 2][:, c * P:(c + 1) * P],
                                       start=(c == 0), stop=(c == 7))
                    mm.then_inc(a.y_ready, 1)
                t = u - D_V
                if runs(kind, u, D_V):
                    g = t % GROUPS
                    if reused(kind, t, 1):
                        pe.wait_ge(a.v_moved, n + t)
                    if ends(kind, u) is not None:
                        pe.wait_ge(a.added, q + ends(kind, u) + 1)
                    pe.matmul(v_ps, src[(t // GROUPS) % 2][:, :], wv[:, g * GV:(g + 1) * GV],
                              start=True, stop=True).then_inc(a.v_ready, 1)
                b = starts(kind, u)
                if b is not None and not local:
                    pe.wait_ge(s.wsel_ready, q + b + 1)
                    if runs(kind, u - 1, D_SCORE):
                        pe.wait_ge(a.kept, n + u - D_SCORE)
                    pe.matmul(cond_ps, wsel[:, b % 2, 0:P], XT[:, bass.ds((2 * i + b) * P, P)],
                              start=True, stop=True).then_inc(s.cond_ready, 1)
                t = u - D_SCORE
                if runs(kind, u, D_SCORE):
                    pe.wait_ge(a.qkT_moved, n + t + 1)
                    if reused(kind, t, 1):
                        pe.wait_ge(a.exp_ready if local else a.kept, n + t)
                    if b is not None and not local:
                        pe.wait_ge(s.ys_ready, q + b + 1)
                    st = qkT[t % 2]
                    if local:
                        for r in range(2):
                            pe.matmul(sc_ps[:, r, :].rearrange("p (a k) -> p a k", a=2), ident16[:, :],
                                      over(local_mask[:, :], [P, 2, P], 1), start=True, stop=False,
                                      skip_group_check=True)
                    for pair in range(2):
                        for r in range(2):
                            mm = pe.matmul(sc_ps[:, r, pair * P:(pair + 1) * P],
                                           st[r * HD:(r + 1) * HD, pair * P:(pair + 1) * P],
                                           st[r * HD:(r + 1) * HD, (2 + pair) * P:(3 + pair) * P],
                                           start=not local, stop=True, skip_group_check=True)
                    mm.then_inc(a.sc_ready, 1)
                t = u - D_TURN
                if runs(kind, u, D_TURN):
                    pe.wait_ge(a.qr_ready, n + t + 1)
                    if reused(kind, t, 1):
                        pe.wait_ge(a.qkT_moved, n + t)
                    for c in range(4):
                        mm = pe.transpose(qkT_ps[:, c * P:(c + 1) * P], qr[t % 2][:, c * P:(c + 1) * P], ident[:, :])
                    mm.then_inc(a.qkT_ready, 1)
                t = u - D_QKV
                if runs(kind, u, D_QKV):
                    g = t % GROUPS
                    if g == 0:
                        if local:
                            pe.wait_ge(s.xs_ready, (q - B) * 2 + 2 * (t // GROUPS) + 2)
                        else:
                            pe.wait_ge(s.ys_ready, q + t // GROUPS + 1)
                    if reused(kind, t, 2):
                        pe.wait_ge(a.normed if local else a.qr_ready, n + t - 1)
                    pe.matmul(qk_ps[t % 2][:, :], src[(t // GROUPS) % 2][:, :],
                              wqk[:, g, :, :].rearrange("p i n -> p (i n)"),
                              start=True, stop=True).then_inc(a.qk_ready, 1)
                t = u - D_PROB
                if runs(kind, u, D_PROB):
                    pe.wait_ge(a.pT_moved, n + t + 1)
                    pe.wait_ge(a.v_moved, n + t + 1)
                    if reused(kind, t, 1):
                        pe.wait_ge(a.oT_moved, n + t)
                    for h in range(GH):
                        at, row, col = (h % 2 * 2 + h // 2) * P, h % 2 * HD, h // 2 * P
                        mm = pe.matmul(oT_ps[row:row + HD, col:col + P], vt[t % GROUPS][:, h * HD:(h + 1) * HD],
                                       pT[t % 2][:, at:at + P], start=True, stop=True)
                    mm.then_inc(a.o_ready, 1)
            return tick

        def dve_tick(dve, local):
            def tick(kind, u, n, q, i):
                t = u - D_TURN
                if runs(kind, u, D_TURN) and local:
                    dve.wait_ge(a.roped_c, n + t + 1)
                    dve.wait_ge(a.roped_s, n + t + 1)
                    if reused(kind, t, 2):
                        dve.wait_ge(a.qkT_ready, n + t - 1)
                    dve.tensor_tensor(qr[t % 2][:, :], t1[t % 2][:, :], t2[t % 2][:, :], ALU.add)\
                        .then_inc(a.qr_ready, 1)
                t = u - D_REC
                if runs(kind, u, D_REC):
                    dve.wait_ge(a.exp_ready, n + t + 1)
                    if reused(kind, t, 2):
                        dve.wait_ge(a.p_scaled, n + t - 1)
                    dve.reciprocal(rec[t % 2][:, :], sums[t % 2][:, :]).then_inc(a.rec_ready, 1)
                t = u - D_ROPE
                if runs(kind, u, D_ROPE):
                    if local:
                        dve.wait_ge(a.rs_ready, n + t + 1)
                        if reused(kind, t, 2):
                            dve.wait_ge(a.roped_s, n + t - 1)
                        dve.tensor_tensor(heads(qn[t % 2][:, :]), heads(qk_ps[t % 2][:, :]),
                                          over(rs[t % 2][:, :], [P, 8, HD], 2), ALU.mult).then_inc(a.normed, 1)
                    else:
                        dve.wait_ge(a.qk_ready, n + t + 1)
                        if reused(kind, t, 2):
                            dve.wait_ge(a.qkT_ready, n + t - 1)
                        dve.tensor_tensor(qr[t % 2][:, :], qk_ps[t % 2][:, :],
                                          bqk[:, t % GROUPS, :, :].rearrange("p i n -> p (i n)"),
                                          ALU.add).then_inc(a.qr_ready, 1)
                b = ends(kind, u)
                if b is not None:
                    dve.wait_ge(a.y_ready, q + b + 1)
                    at = bass.ds((2 * i + b) * P, P)
                    if local:
                        dve.tensor_tensor(ZT[:, at], y_ps, ZT[:, at], ALU.add).then_inc(a.added, 1)
                    else:
                        dve.scalar_tensor_tensor(XT[:, at], y_ps, cols[:, R_BO:R_BO + 1], XT[:, at],
                                                 ALU.add, ALU.add).then_inc(a.added, 1)
                t = u - D_NORM
                if runs(kind, u, D_NORM) and local:
                    dve.wait_ge(a.squared, n + t + 1)
                    dve.tensor_reduce(ss[t % 2][:, :], heads(sq[t % 2][:, :]), AX.X, ALU.add).then_inc(a.summed, 1)
                    if reused(kind, t, 2):
                        dve.wait_ge(a.rs_ready, n + t - 1)
                    dve.wait_ge(a.summed, n + t + 1)
                    dve.tensor_scalar(ssc[t % 2][:, :], ss[t % 2][:, :], L2_EPS, None, ALU.max)\
                        .then_inc(a.clamped, 1)
                t = u - D_ROPE
                if runs(kind, u, D_ROPE) and local:
                    dve.wait_ge(a.normed, n + t + 1)
                    dve.tensor_tensor(t1[t % 2][:, :].rearrange("p (i h e) -> p i h e", i=2, h=GH),
                                      qn[t % 2][:, :].rearrange("p (i h e) -> p i h e", i=2, h=GH),
                                      over(tabc[:, :, :], [P, 2, GH, HD], 2), ALU.mult).then_inc(a.roped_c, 1)
                t = u - D_V
                if runs(kind, u, D_V) and not local:
                    dve.wait_ge(a.v_ready, n + t + 1)
                    if reused(kind, t, GROUPS):
                        dve.wait_ge(a.o_ready, n + t - GROUPS + 1)
                    g = t % GROUPS
                    dve.tensor_tensor(vt[g][:, :], v_ps, bv[:, g * GV:(g + 1) * GV], ALU.add).then_inc(a.v_moved, 1)
                t = u - D_SCORE
                if runs(kind, u, D_SCORE):
                    dve.wait_ge(a.sc_ready, n + t + 1)
                    sc = sc_ps.rearrange("p r (a k) -> p r a k", a=2)
                    by_head = [negmax[t % 2][:, :].rearrange("p (r a) -> p r a", r=2),
                               rowmax[t % 2][:, :].rearrange("p (r a) -> p r a", r=2)]
                    if reused(kind, t, 2):
                        dve.wait_ge(a.exp_ready, n + t - 1)
                    if local:
                        dve.tensor_reduce(by_head[0], sc, AX.X, ALU.max, negate=True).then_inc(a.negmax_ready, 1)
                    else:
                        on_all = lambda m: m[:, :].unsqueeze(1).unsqueeze(1).to_broadcast([P, 2, 2, P])
                        masked = t1[t % 2][:, :].rearrange("p (r a k) -> p r a k", r=2, a=2)
                        dve.tensor_tensor(masked, sc, on_all(keep), ALU.mult).then_inc(a.kept, 1)
                        dve.wait_ge(a.kept, n + t + 1)
                        dve.tensor_tensor(masked, masked, on_all(fill), ALU.add).then_inc(a.filled, 1)
                        dve.wait_ge(a.filled, n + t + 1)
                        dve.tensor_reduce(by_head[1], masked, AX.X, ALU.max).then_inc(a.maxed, 1)
                        dve.wait_ge(a.maxed, n + t + 1)
                        dve.tensor_scalar(negmax[t % 2][:, :], rowmax[t % 2][:, :], -HD ** -0.5, None, ALU.mult)\
                            .then_inc(a.negmax_ready, 1)
            return tick

        def act_tick(act, local):
            def tick(kind, u, n, q, i):
                t = u - D_EXP
                if runs(kind, u, D_EXP):
                    act.wait_ge(a.negmax_ready, n + t + 1)
                    if reused(kind, t, 4):
                        act.wait_ge(a.pT_ready, n + t - 3)
                    if reused(kind, t, 2):
                        act.wait_ge(a.rec_ready, n + t - 1)
                    for h in range(GH):
                        its = sc_ps[:, h // 2, h % 2 * P:(h % 2 + 1) * P] if local else t1[t % 2][:, h * P:(h + 1) * P]
                        ex = act.activation(pr[t % 4][:, h * P:(h + 1) * P], its,
                                            ACT.Exp, bias=negmax[t % 2][:, h:h + 1],
                                            scale=1.0 if local else HD ** -0.5, accum_out=sums[t % 2][:, h:h + 1])
                    ex.then_inc(a.exp_ready, 1)
                b = starts(kind, u)
                if b is not None and not local:
                    act.wait_ge(s.cond_ready, q + b + 1)
                    if kind != "first" or b >= 2:
                        act.wait_ge(a.v_ready, n + u - D_PREP - GROUPS)
                    act.activation(ys[b % 2][:, :], cond_ps, ACT.Identity, bias=wsel[:, b % 2, P:P + 1])\
                        .then_inc(s.ys_ready, 1)
                t = u - D_NORM
                if runs(kind, u, D_NORM) and local:
                    act.wait_ge(a.qk_ready, n + t + 1)
                    if reused(kind, t, 2):
                        act.wait_ge(a.summed, n + t - 1)
                    act.activation(sq[t % 2][:, :], qk_ps[t % 2][:, :], ACT.Square).then_inc(a.squared, 1)
                t = u - D_PROB
                if runs(kind, u, D_PROB):
                    act.wait_ge(a.pT_ready, n + t + 1)
                    if reused(kind, t, 2):
                        act.wait_ge(a.o_ready, n + t - 1)
                    act.copy(pT[t % 2][:, :], pT_ps[:, :]).then_inc(a.pT_moved, 1)
                t = u - D_V
                if runs(kind, u, D_V) and local:
                    act.wait_ge(a.v_ready, n + t + 1)
                    if reused(kind, t, GROUPS):
                        act.wait_ge(a.o_ready, n + t - GROUPS + 1)
                    act.copy(vt[t % GROUPS][:, :], v_ps).then_inc(a.v_moved, 1)
                t = u - D_OUT
                if runs(kind, u, D_OUT):
                    act.wait_ge(a.o_ready, n + t + 1)
                    if t % GROUPS == 0 and reused(kind, t, 2 * GROUPS):
                        act.wait_ge(a.y_ready, q + t // GROUPS - 1)
                    g = t % GROUPS
                    act.copy(oT[(t // GROUPS) % 2][:, g * GV:(g + 1) * GV], oT_ps).then_inc(a.oT_moved, 1)
                t = u - D_TURN
                if runs(kind, u, D_TURN):
                    act.wait_ge(a.qkT_ready, n + t + 1)
                    if reused(kind, t, 2):
                        act.wait_ge(a.sc_ready, n + t - 1)
                    act.copy(qkT[t % 2][:, :], qkT_ps[:, :]).then_inc(a.qkT_moved, 1)
                b = starts(kind, u)
                if b is not None and local:
                    if kind != "first" or b >= 2:
                        act.wait_ge(a.v_ready, n + u - D_PREP - GROUPS)
                    at = (2 * i + b) * P
                    act.copy(xs[b % 2][0:HALF, :], ZT[0:HALF, bass.ds(at, P)]).then_inc(s.xs_ready, 1)
                    act.copy(xs[b % 2][HALF:P, 1:P], ZT[HALF:P, bass.ds(at, P - 1)]).then_inc(s.xs_ready, 1)
            return tick

        def pool_tick(pool, local, l=None):
            def tick(kind, u, n, q, i):
                b = starts(kind, u)
                if b is not None and not local:
                    if kind != "first" or b >= 2:
                        pool.wait_ge(s.ys_ready, q + b - 1)
                    who = pool.value_load(subject[0:1, bass.ds(2 * i + b, 1)], min_val=0, max_val=SUBJ - 1)
                    pool.tensor_copy(wsel[:, b % 2, :], condT[:, bass.ds(who, 1), :]).then_inc(s.wsel_ready, 1)
                t = u - D_REC
                if runs(kind, u, D_REC):
                    pool.wait_ge(a.rec_ready, n + t + 1)
                    p = pr[t % 4][:, :].rearrange("p (h k) -> p h k", h=GH)
                    pool.tensor_tensor(p, p, over(rec[t % 2][:, :], [P, GH, P], 2), ALU.mult).then_inc(a.p_scaled, 1)
                t = u - D_ROPE
                if runs(kind, u, D_ROPE) and local:
                    if kind == "first" and t == 0:
                        pool.wait_ge(s.tables_ready, l * 3 + 3)
                    pool.wait_ge(a.normed, n + t + 1)
                    if reused(kind, t, 2):
                        pool.wait_ge(a.qr_ready, n + t - 1)
                    pool.tensor_tensor(t2[t % 2][:, :].rearrange("p (i h f e) -> p i h f e", i=2, h=GH, f=2),
                                       qn[t % 2][:, :].rearrange("p (i h f e) -> p i h f e", i=2, h=GH, f=2)
                                       [:, :, :, ::-1, :],
                                       over(tabs[:, :, :].rearrange("p i (f e) -> p i f e", f=2),
                                            [P, 2, GH, 2, HD // 2], 2), ALU.mult).then_inc(a.roped_s, 1)
                t = u - D_NORM
                if runs(kind, u, D_NORM) and local:
                    pool.wait_ge(a.clamped, n + t + 1)
                    if reused(kind, t, 2):
                        pool.wait_ge(a.normed, n + t - 1)
                    pool.tensor_tensor(rs[t % 2][:, :], ssc[t % 2][:, :], neg_half[:, 0:8], ALU.pow)\
                        .then_inc(a.rs_ready, 1)
            return tick


        def images(eng, tick):
            def chunks_of(b):
                with eng.Fori(1, RG_BODIES) as i:
                    for u in range(RG_BODY):
                        tick("steady", u, b * RG_BODIES + i, b)
            for u in range(RG_BODY):
                tick("first", u, 0, 0)
            chunks_of(0)
            with eng.Fori(1, B) as b:
                for u in range(RG_BODY):
                    tick("turn", u, b * RG_BODIES, b)
                chunks_of(b)
            for u in range(RG_PROD):
                tick("last", u, B * RG_BODIES, B)

        def in_turn(kind, u, delay):
            return kind in ("steady", "turn") or runs(kind, u, delay)

        def by_row(ap):
            return ap.rearrange("p (r w) -> p r w", r=RG_ROWS)

        def y_arguments(eng, kind, u, n):
            if kind != "first":
                eng.wait_ge(s.rg_hat, n + u - RG_BODY + 1)
            done = s.rg_yarg_first if u == 0 else s.rg_yarg
            eng.tensor_tensor(by_row(rg_uy[u]), over(minus_index[:, :], [P, RG_ROWS, P], 1),
                              over(rg_yrow[:, bass.ds((n + u) * RG_ROWS, RG_ROWS)], [P, RG_ROWS, P], 2), ALU.add)\
                .then_inc(done, 1)

        def pe_image(pe):
            def tick(kind, u, m, b):
                n = m * RG_BODY
                t = u - RG_X
                if in_turn(kind, u, RG_X):
                    pe.wait_ge(s.rg_hat, n + t + 1)
                    if kind != "first" or t >= RG_BODY:
                        pe.wait_ge(s.rg_prod, n + t - RG_BODY + 1)
                    at = b * P if t >= 0 or kind == "steady" else b * P - P
                    for r in range(RG_ROWS):
                        mm = pe.matmul(bank[t % RG_BODY][:, r * P:(r + 1) * P], rg_wx[t % RG_BODY][:, r * P:(r + 1) * P],
                                       XT[:, bass.ds(at, P)], start=True, stop=True)
                    mm.then_inc(s.rg_xb, 1)
            return tick

        def dve_image(dve):
            def tick(kind, u, m, b):
                n = m * RG_BODY
                t = u - RG_PROD
                if in_turn(kind, u, RG_PROD):
                    dve.wait_ge(s.rg_xb, n + t + 1)
                    dve.wait_ge(s.rg_hat, n + t + 1)
                    if kind != "first" or t >= 2:
                        dve.wait_ge(s.rg_summed, n + t - 1)
                    dve.tensor_tensor(rg_p[t % 2][:, :], bank[t % RG_BODY][:, :], rg_wy[t % RG_BODY][:, :], ALU.mult)\
                        .then_inc(s.rg_prod, 1)
                if kind != "last":
                    dve.wait_ge(s.rg_xarg, n + u + 1)
                    bits = rg_ux[u][:, :].bitcast(I32)
                    dve.tensor_scalar(bits, bits, 0x7FFFFFFF, None, ALU.bitwise_and).then_inc(s.rg_xabs, 1)
                    if u == 0:
                        y_arguments(dve, kind, u, n)
                if in_turn(kind, u, RG_PROD):
                    dve.wait_ge(s.rg_prod, n + t + 1)
                    dve.tensor_reduce(ZT[:, bass.ds((n + t) * RG_ROWS, RG_ROWS)], by_row(rg_p[t % 2][:, :]),
                                      AX.X, ALU.add).then_inc(s.rg_summed, 1)
            return tick

        def act_image(act):
            def tick(kind, u, m, b):
                n = m * RG_BODY
                t = u - RG_HAT
                if in_turn(kind, u, RG_HAT):
                    act.wait_ge(s.rg_xabs, n + t + 1)
                    act.wait_ge(s.rg_yabs, n + t + 1)
                    if kind != "first" or t >= RG_BODY:
                        act.wait_ge(s.rg_xb, n + t - RG_BODY + 1)
                        act.wait_ge(s.rg_prod, n + t - RG_BODY + 1)
                    act.activation(rg_w[t % RG_BODY][:, :, :], rg_u[t % RG_BODY][:, :, :], ACT.Relu, bias=1.0, scale=-1.0)\
                        .then_inc(s.rg_hat, 1)
                if kind != "last":
                    if u == 0:
                        act.wait_ge(s.rg_yarg_first, m + 1)
                    else:
                        act.wait_ge(s.rg_yarg, m * (RG_BODY - 1) + u)
                    act.activation(rg_uy[u][:, :], rg_uy[u][:, :], ACT.Abs).then_inc(s.rg_yabs, 1)
            return tick

        def pool_image(pool):
            def tick(kind, u, m, b):
                n = m * RG_BODY
                if kind != "last":
                    if u != 0:
                        y_arguments(pool, kind, u, n)
                    if kind != "first":
                        pool.wait_ge(s.rg_hat, n + u - RG_BODY + 1)
                    pool.tensor_tensor(by_row(rg_ux[u]), over(rg_xcol[:, bass.ds(b * P, P)], [P, RG_ROWS, P], 1),
                                       over(rg_xrow[:, bass.ds((n + u) * RG_ROWS, RG_ROWS)], [P, RG_ROWS, P], 2),
                                       ALU.add).then_inc(s.rg_xarg, 1)
            return tick

        def shift_in(act, c, l):
            act.wait_ge(a.added, l * B + B + CH * (c + 1))
            lo = ZT[0:HALF, c * CW:(c + 1) * CW]
            hi = ZT[HALF:P, c * CW:(c + 1) * CW].rearrange("p (b t) -> p b t", b=CH)
            if c >= 2:
                act.wait_ge(s.lf_centred, l * NCH + c - 1)
            act.copy(xf[c % 2][0:HALF, :], lo).then_inc(s.lf_shifted, 1)
            act.copy(xf[c % 2][HALF:P, :].rearrange("p (b t) -> p b t", b=CH)[:, :, 1:P], hi[:, :, 0:P - 1])\
                .then_inc(s.lf_shifted, 1)

        def ffn_pe(pe, l):
            def mean(c):
                pe.wait_ge(s.lf_shifted, l * (2 * NCH) + 2 * (c + 1))
                if c >= 1:
                    pe.wait_ge(s.lf_centred, l * NCH + c)
                pe.matmul(qk_ps[0][:, :], mean_w[:, :], xf[c % 2][:, :], start=True, stop=True)\
                    .then_inc(s.lf_mean, 1)

            def var(c):
                pe.wait_ge(s.lf_squared, l * NCH + c + 1)
                if c >= 1:
                    pe.wait_ge(s.lf_normed, l * NCH + c)
                for j in range(CH):
                    mm = pe.matmul(qk_ps[1][:, j:j + 1], xq[c % 2][:, j * P:(j + 1) * P], mean_w[:, 0:1],
                                   start=True, stop=True)
                mm.then_inc(s.lf_var, 1)

            def spread(c):
                pe.wait_ge(s.lf_rstd, l * NCH + c + 1)
                for j in range(CH):
                    mm = pe.transpose(qk_ps[1][:, j * P:(j + 1) * P], xr[:, j:j + 1].to_broadcast([P, P]), ident[:, :])
                mm.then_inc(s.lf_spread, 1)

            def hidden(c, j):
                k = 3 * c + j
                o, w = FCH[j]
                if j == 0:
                    pe.wait_ge(s.lf_xn, l * NCH + c + 1)
                if k >= 2:
                    pe.wait_ge(s.lf_gated, l * 12 + k - 1)
                pe.matmul(bank[2 + k % 2][0:w, :], w1[:, o:o + w], xn[c % 2][:, :], start=True, stop=True)
                pe.matmul(bank[4 + k % 2][0:w, :], w1[:, INNER + o:INNER + o + w], xn[c % 2][:, :],
                          start=True, stop=True).then_inc(s.lf_h, 1)

            def down(c):
                if c >= 1:
                    pe.wait_ge(s.lf_state, l * NCH + c)
                for j, (o, w) in enumerate(FCH):
                    pe.wait_ge(s.lf_gated, l * 12 + 3 * c + j + 1)
                    mm = pe.matmul(scores[:, 0, :], w2[0:w, j, :], hg[c % 2][j][0:w, :], start=(j == 0), stop=(j == 2))
                mm.then_inc(s.lf_y, 1)

            def ahead(u):
                if u == 5:
                    mean(0)
                if u == 7:
                    var(0)
                if u == 8:
                    spread(0)

            def rest():
                pe.wait_ge(s.wffn_loaded, l * 48 + 48)
                pe.wait_ge(a.added, (l + 2) * B)
                for c in range(NCH):
                    if c + 1 < NCH:
                        mean(c + 1)
                    hidden(c, 0)
                    hidden(c, 1)
                    if c + 1 < NCH:
                        var(c + 1)
                    hidden(c, 2)
                    if c + 1 < NCH:
                        spread(c + 1)
                    down(c)
            return ahead, rest

        def ffn_dve(dve, l):
            def centre(c):
                dve.wait_ge(s.lf_mean, l * NCH + c + 1)
                if c >= 2:
                    dve.wait_ge(s.lf_squared, l * NCH + c - 1)
                    dve.wait_ge(s.lf_normed, l * NCH + c - 1)
                dve.tensor_tensor(xc[c % 2][:, :], xf[c % 2][:, :], qk_ps[0][:, :], ALU.subtract)\
                    .then_inc(s.lf_centred, 1)

            def vareps(c):
                dve.wait_ge(s.lf_var, l * NCH + c + 1)
                if c >= 1:
                    dve.wait_ge(s.lf_rstd, l * NCH + c)
                dve.tensor_scalar(xv, qk_ps[1][:, 0:CH], LN_EPS, None, ALU.add).then_inc(s.lf_vareps, 1)

            def norm(c):
                dve.wait_ge(s.lf_spread, l * NCH + c + 1)
                dve.wait_ge(s.lf_centred, l * NCH + c + 1)
                dve.tensor_tensor(xc[c % 2][:, :], xc[c % 2][:, :], qk_ps[1][:, :], ALU.mult).then_inc(s.lf_normed, 1)
                dve.wait_ge(s.lf_normed, l * NCH + c + 1)
                if c >= 2:
                    dve.wait_ge(s.lf_h, l * 12 + 3 * (c - 1))
                dve.tensor_scalar(xn[c % 2][:, :], xc[c % 2][:, :], cols[:, bass.ds(l + R_LNG, 1)],
                                  cols[:, bass.ds(l + R_LNB, 1)], ALU.mult, ALU.add).then_inc(s.lf_xn, 1)

            def gate(c, j):
                k = 3 * c + j
                w = FCH[j][1]
                dve.wait_ge(s.lf_gelu, l * 12 + k + 1)
                if c >= 2 and j == 0:
                    dve.wait_ge(s.lf_y, l * NCH + c - 1)
                dve.scalar_tensor_tensor(hg[c % 2][j][0:w, :], bank[2 + k % 2][0:w, :],
                                         cols[0:w, bass.ds(l + R_B1 + DEPTH * j, 1)], gl[k % 2][0:w, :],
                                         ALU.add, ALU.mult).then_inc(s.lf_gated, 1)

            def state(c):
                dve.wait_ge(s.lf_y, l * NCH + c + 1)
                dve.scalar_tensor_tensor(ZT[:, c * CW:(c + 1) * CW], scores[:, 0, :], cols[:, bass.ds(l + R_B2, 1)],
                                         ZT[:, c * CW:(c + 1) * CW], ALU.add, ALU.add).then_inc(s.lf_state, 1)

            def ahead(u):
                if u == 5:
                    centre(0)
                if u == 7:
                    vareps(0)
                if u == 8:
                    norm(0)

            def rest():
                for c in range(NCH):
                    if c + 1 < NCH:
                        centre(c + 1)
                    gate(c, 0)
                    gate(c, 1)
                    if c + 1 < NCH:
                        vareps(c + 1)
                    gate(c, 2)
                    if c + 1 < NCH:
                        norm(c + 1)
                    state(c)
            return ahead, rest

        def ffn_act(act, l):
            def square(c):
                act.wait_ge(s.lf_centred, l * NCH + c + 1)
                if c >= 2:
                    act.wait_ge(s.lf_var, l * NCH + c - 1)
                act.activation(xq[c % 2][:, :], xc[c % 2][:, :], ACT.Square).then_inc(s.lf_squared, 1)

            def gelu(c, j):
                k = 3 * c + j
                w = FCH[j][1]
                act.wait_ge(s.lf_h, l * 12 + k + 1)
                if k >= 2:
                    act.wait_ge(s.lf_gated, l * 12 + k - 1)
                act.activation(gl[k % 2][0:w, :], bank[4 + k % 2][0:w, :], ACT.Gelu,
                               bias=gate_b[0:w, j:j + 1]).then_inc(s.lf_gelu, 1)

            def ahead(u):
                if u == 4:
                    shift_in(act, 0, l)
                if u == 6:
                    square(0)

            def rest():
                act.wait_ge(s.lf_bias, l + 1)
                for c in range(NCH):
                    if c + 1 < NCH:
                        shift_in(act, c + 1, l)
                    gelu(c, 0)
                    if c + 1 < NCH:
                        square(c + 1)
                    gelu(c, 1)
                    gelu(c, 2)
            return ahead, rest

        def ffn_pool(pool, l):
            def rstd(c):
                pool.wait_ge(s.lf_vareps, l * NCH + c + 1)
                if c >= 1:
                    pool.wait_ge(s.lf_spread, l * NCH + c)
                pool.tensor_tensor(xr, xv, neg_half[:, 0:CH], ALU.pow).then_inc(s.lf_rstd, 1)

            def ahead(u):
                if u == 7:
                    rstd(0)

            def rest():
                for c in range(1, NCH):
                    rstd(c)
            return ahead, rest


        def sections(ap):
            return ap.rearrange("p (b c t) -> p b c t", b=CH, c=2)

        def seqs_of(ap):
            return ap.rearrange("p (b t) -> p b t", b=CH)

        def gla_pe(pe, c):
            at = bass.ds(c * CW, CW)
            pe.matmul(bank[0][:, :], lap[:, :], XT[:, at], start=True, stop=True).then_inc(s.g_lapx, 1)
            pe.wait_ge(s.g_src, c + 1)
            pe.matmul(bank[1][:, :], gwq[:, :], gsrc[:, :], start=True, stop=True).then_inc(s.g_qk, 1)
            pe.matmul(bank[2][:, :], gwk[:, :], gsrc[:, :], start=True, stop=True).then_inc(s.g_qk, 1)
            pe.matmul(bank[3][0:RANK, :], gwl1[:, :], gsrc[:, :], start=True, stop=True).then_inc(s.g_low, 1)
            pe.wait_ge(s.g_low_moved, c + 1)
            pe.matmul(bank[0][:, :], gwl2[:, :], glow[:, :], start=True, stop=True).then_inc(s.g_decay, 1)

            def products(j):
                k = c * CH + j
                if j == 0:
                    pe.wait_ge(s.g_keys, 3 * c + 3)
                if j >= 2:
                    pe.wait_ge(s.g_vg_used, k - 1)
                pe.matmul(g_vg_ps[j % 2][:, :], gsrc[:, j * P:(j + 1) * P], gwvg[:, :], start=True, stop=True)\
                    .then_inc(s.g_vg, 1)
                if j == 0:
                    pe.wait_ge(s.g_headed, c * GLH + GLH)
                if j >= 2:
                    pe.wait_ge(s.g_masked, k - 1)
                for h, keys in enumerate((gka, gkb)):
                    mm = pe.matmul(scores[:, j % 2, h * 2 * P:(h + 1) * 2 * P], keys[:, j * P:(j + 1) * P],
                                   gq4[:, j * 4 * P + h * 2 * P:j * 4 * P + (h + 1) * 2 * P], start=True, stop=True)
                mm.then_inc(s.g_a, 1)

            def outputs(j):
                k = c * CH + j
                pe.wait_ge(s.g_masked, k + 1)
                pe.wait_ge(s.g_v_moved, k + 1)
                if j >= 2:
                    pe.wait_ge(s.g_o_read, k - 1)
                for h in range(GLH):
                    mm = pe.matmul(g_o_ps[j % 2][:, h * GLV:(h + 1) * GLV], ga[j % 2][:, h * P:(h + 1) * P],
                                   gv[j % 2][:, h * GLV:(h + 1) * GLV], start=True, stop=True)
                mm.then_inc(s.g_o, 1)

            def turned(j):
                k = c * CH + j
                pe.wait_ge(s.g_gated, k + 1)
                if j:
                    pe.wait_ge(s.g_oT_moved, k)
                for h in range(2):
                    mm = pe.transpose(bank[3][:, h * P:(h + 1) * P], gout[j % 2][:, h * P:(h + 1) * P], ident[:, :])
                mm.then_inc(s.g_oT, 1)
            products(0)
            for j in range(CH):
                if j + 1 < CH:
                    products(j + 1)
                outputs(j)
                if j:
                    turned(j - 1)
            turned(CH - 1)
            pe.wait_ge(s.g_oT_moved, c * CH + CH)
            for h in range(2):
                mm = pe.matmul(bank[1][:, :], gwo[:, h, :], goT[h][:, :], start=(h == 0), stop=(h == 1))
            mm.then_inc(s.g_y, 1)
            pe.wait_ge(s.g_added, c + 1)

        def gla_dve(dve, c):
            at = bass.ds(c * CW, CW)
            seqs = bass.ds(c * CH, CH)
            step_no = [0]

            def ordered(ins):
                step_no[0] += 1
                ins.then_inc(s.g_steps, 1)
                dve.wait_ge(s.g_steps, c * GLA_STEPS + step_no[0])
            x = XT[:, at]
            ge, gn, gl_, gy = xf[0], xf[1], t1[0], t1[1]
            dve.tensor_tensor(seqs_of(ge[:, :])[:, :, 1:P - 1], seqs_of(x)[:, :, 0:P - 2], seqs_of(x)[:, :, 2:P],
                              ALU.add).then_inc(s.g_edges, 1)
            dve.tensor_scalar(seqs_of(ge[:, :])[:, :, 0::P - 1], seqs_of(x)[:, :, 1::P - 3], 2.0, None, ALU.mult)\
                .then_inc(s.g_edges, 1)
            dve.tensor_scalar(gn[:, :], x, -1.0, 1.0, ALU.mult, ALU.add).then_inc(s.g_edges, 1)
            dve.wait_ge(s.g_edges, c * 3 + 3)
            ordered(dve.scalar_tensor_tensor(ge[:, :], x, -2.0, ge[:, :], ALU.mult, ALU.add))
            ordered(dve.tensor_tensor(seqs_of(gy[:, :]), seqs_of(x), over(diffuse[:, 2, seqs], [P, CH, P], 2), ALU.mult))
            ordered(dve.tensor_tensor(gy[:, :], gy[:, :], gn[:, :], ALU.mult))
            ordered(dve.tensor_tensor(seqs_of(ge[:, :]), seqs_of(ge[:, :]), over(diffuse[:, 1, seqs], [P, CH, P], 2),
                                      ALU.mult))
            dve.wait_ge(s.g_lapx, c + 1)
            ordered(dve.tensor_tensor(seqs_of(gl_[:, :]), seqs_of(bank[0][:, :]), over(diffuse[:, 0, seqs], [P, CH, P], 2),
                                      ALU.mult))
            ordered(dve.tensor_tensor(gl_[:, :], gl_[:, :], ge[:, :], ALU.add))
            dve.tensor_tensor(gsrc[:, :], gl_[:, :], gy[:, :], ALU.add).then_inc(s.g_src, 1)
            pre, low = gn, gy
            dve.wait_ge(s.g_src, c + 1)
            dve.wait_ge(s.g_decay, c + 1)
            ordered(dve.tensor_scalar(pre[:, :], bank[0][:, :], cols[:, R_GK:R_GK + 1], None, ALU.add))
            dve.tensor_scalar(low[:, :], pre[:, :], 0.0, None, ALU.min).then_inc(s.g_edge2, 1)
            dve.tensor_scalar(gl_[:, :].bitcast(I32), pre[:, :].bitcast(I32), 0x7FFFFFFF, None, ALU.bitwise_and)\
                .then_inc(s.g_abs, 1)
            dve.wait_ge(s.g_log, c + 1)
            dve.wait_ge(s.g_edge2, c + 1)
            ordered(dve.tensor_tensor(low[:, :], low[:, :], ge[:, :], ALU.subtract))
            ordered(dve.tensor_tensor_scan(gsum[:, :], restart[:, :], low[:, :], 0.0, ALU.mult, ALU.add))
            dve.tensor_tensor(seqs_of(gn[:, :])[:, :, 0:HALF],
                              sections(gsum[:, :])[:, :, 0, HALF - 1:HALF].to_broadcast([P, CH, HALF]),
                              sections(gsum[:, :])[:, :, 0, :], ALU.subtract).then_inc(s.g_sum, 1)
            dve.wait_ge(s.g_exp, c * 3 + 3)
            dve.wait_ge(s.g_qk, c * 2 + 2)
            dve.tensor_tensor(gka[:, :], bank[2][:, :], gen_[:, :], ALU.mult).then_inc(s.g_keys, 1)
            dve.tensor_tensor(sections(gkb[:, :])[:, :, 0, :], sections(bank[2][:, :])[:, :, 0, :],
                              seqs_of(ge[:, :])[:, :, 0:HALF], ALU.mult).then_inc(s.g_keys, 1)
            dve.tensor_tensor(sections(gkb[:, :])[:, :, 1, :], sections(bank[2][:, :])[:, :, 1, :],
                              sections(gen_[:, :])[:, :, 1, :], ALU.mult).then_inc(s.g_keys, 1)
            ordered(dve.scalar_tensor_tensor(gq1[:, :], gep[:, :], GLK ** -0.5, bank[1][:, :], ALU.mult, ALU.mult))
            for h in range(GLH):
                dve.tensor_scalar(gq4[:, :].rearrange("p (b c h t) -> p b c h t", b=CH, c=2, h=GLH)[:, :, :, h, :],
                                  sections(gq1[:, :]), headmask[:, h:h + 1], None, ALU.mult).then_inc(s.g_headed, 1)

            def masked(j):
                k = c * CH + j
                dve.wait_ge(s.g_a, k + 1)
                if j >= 2:
                    dve.wait_ge(s.g_o, k - 1)
                dve.tensor_tensor(ga[j % 2][:, :].rearrange("p (h c t) -> p h c t", h=GLH, c=2),
                                  scores[:, j % 2, :].rearrange("p (c h t) -> p h c t", h=GLH, c=2),
                                  over(gmask[:, :].rearrange("p (c t) -> p c t", c=2), [P, GLH, 2, HALF], 1),
                                  ALU.mult).then_inc(s.g_masked, 1)

            by_head = lambda ap: ap.rearrange("p (h e) -> p h e", h=GLH)
            masked(0)
            for j in range(CH):
                k = c * CH + j
                dve.wait_ge(s.g_sq, k + 1)
                ordered(dve.tensor_reduce(gss[j % 2][:, :], by_head(gsq[j % 2]), AX.X, ALU.add))
                dve.tensor_scalar(gss[j % 2][:, :], gss[j % 2][:, :], 1.0 / GLV, LN_EPS, ALU.mult, ALU.add)\
                    .then_inc(s.g_mean, 1)
                if j + 1 < CH:
                    masked(j + 1)
                dve.wait_ge(s.g_rms, k + 1)
                dve.wait_ge(s.g_sg, k + 1)
                dve.tensor_tensor(by_head(gon[j % 2]), by_head(g_o_ps[j % 2][:, 0:GLH * GLV]),
                                  over(grs[j % 2][:, :], [P, GLH, GLV], 2), ALU.mult).then_inc(s.g_o_read, 1)
                dve.wait_ge(s.g_o_read, k + 1)
                ordered(dve.tensor_tensor(gon[j % 2], gon[j % 2], gsg[j % 2][:, :], ALU.mult))
                if j >= 2:
                    dve.wait_ge(s.g_oT, k - 1)
                dve.tensor_tensor(by_head(gout[j % 2][:, :]), by_head(gon[j % 2]),
                                  over(rmsw[:, :], [P, GLH, GLV], 1), ALU.mult).then_inc(s.g_gated, 1)
            dve.wait_ge(s.g_y, c + 1)
            dve.tensor_tensor(XT[:, at], bank[1][:, :], XT[:, at], ALU.add).then_inc(s.g_added, 1)
            dve.wait_ge(s.g_added, c + 1)

        def gla_act(act, c):
            ge, gn, gl_ = xf[0], xf[1], t1[0]
            act.wait_ge(s.g_low, c + 1)
            act.copy(glow[:, :], bank[3][0:RANK, :]).then_inc(s.g_low_moved, 1)
            act.wait_ge(s.g_abs, c + 1)
            act.activation(ge[:, :], gl_[:, :], ACT.Exp, scale=-1.0).then_inc(s.g_soft, 1)
            act.wait_ge(s.g_soft, c + 1)
            act.activation(ge[:, :], ge[:, :], ACT.Ln, bias=1.0).then_inc(s.g_log, 1)
            act.wait_ge(s.g_sum, c + 1)
            act.activation(gep[:, :], gsum[:, :], ACT.Exp, scale=1.0 / GATE_NORM).then_inc(s.g_exp, 1)
            act.activation(gen_[:, :], gsum[:, :], ACT.Exp, scale=-1.0 / GATE_NORM).then_inc(s.g_exp, 1)
            act.activation(seqs_of(ge[:, :])[:, :, 0:HALF], seqs_of(gn[:, :])[:, :, 0:HALF], ACT.Exp,
                           scale=1.0 / GATE_NORM).then_inc(s.g_exp, 1)

            def values(j):
                k = c * CH + j
                act.wait_ge(s.g_vg, k + 1)
                if j >= 2:
                    act.wait_ge(s.g_gated, k - 1)
                    act.wait_ge(s.g_o, k - 1)
                act.copy(gv[j % 2][:, :], g_vg_ps[j % 2][:, 0:GLH * GLV]).then_inc(s.g_v_moved, 1)
                act.activation(gsg[j % 2][:, :], g_vg_ps[j % 2][:, GLH * GLV:2 * GLH * GLV], ACT.Silu)\
                    .then_inc(s.g_sg, 1)
                act.wait_ge(s.g_sg, k + 1)
                act.wait_ge(s.g_v_moved, k + 1)
                act.sem_inc(s.g_vg_used, 1)

            def move(j):
                act.wait_ge(s.g_oT, c * CH + j + 1)
                for h in range(2):
                    cp = act.copy(goT[h][:, j * P:(j + 1) * P], bank[3][:, h * P:(h + 1) * P])
                cp.then_inc(s.g_oT_moved, 1)
            values(0)
            for j in range(CH):
                if j + 1 < CH:
                    values(j + 1)
                act.wait_ge(s.g_o, c * CH + j + 1)
                act.activation(gsq[j % 2], g_o_ps[j % 2][:, 0:GLH * GLV], ACT.Square).then_inc(s.g_sq, 1)
                if j:
                    move(j - 1)
            move(CH - 1)
            act.wait_ge(s.g_y, c + 1)

        def gla_pool(pool, c):
            for j in range(CH):
                k = c * CH + j
                pool.wait_ge(s.g_mean, k + 1)
                pool.tensor_tensor(grs[j % 2][:, :], gss[j % 2][:, :], neg_half[:, 0:GLH], ALU.pow).then_inc(s.g_rms, 1)


        def gate_pe(pe):
            pe.wait_ge(s.e_loaded, 16 * 9)
            pe.wait_ge(s.e_first, 1)
            for e in range(NEXP):
                for j in range(FJ):
                    at = (e * FJ + j) * B
                    mm = pe.matmul(bank[0][:, at:at + B], up_of(e)[:, j * P:(j + 1) * P], first[:, :],
                                   start=True, stop=True)
            mm.then_inc(s.e_gate_h, 1)
            pe.wait_ge(s.e_gate_relu, 1)
            for e in range(NEXP):
                for j in range(FJ):
                    at = (e * FJ + j) * B
                    mm = pe.matmul(bank[1][:, e * B:(e + 1) * B], down_of(e)[:, j, :], gate_h[:, at:at + B],
                                   start=(j == 0), stop=(j == FJ - 1))
            mm.then_inc(s.e_gate_o, 1)
            pe.wait_ge(s.e_gate_in, 2)
            for k in range(4):
                mm = pe.matmul(bank[2][:, 0:B], gw1[:, k, :], gate_in[:, k * B:(k + 1) * B], start=(k == 0),
                               stop=(k == 3))
            mm.then_inc(s.e_gate_hid, 1)
            pe.wait_ge(s.e_gate_hid_relu, 1)
            pe.matmul(bank[3][0:B, 0:4], gate_hid[:, :], gw2[:, :], start=True, stop=True).then_inc(s.e_gate_logit, 1)
            pe.wait_ge(s.e_gate_diag, 1)
            pe.matmul(bank[4][:, 0:4 * B], ones[0:B, :], gate_diag[:, :], start=True, stop=True)\
                .then_inc(s.e_gate_all, 1)

        def gate_dve(dve):
            step_no = [0]

            def ordered(ins):
                step_no[0] += 1
                ins.then_inc(s.e_steps, 1)
                dve.wait_ge(s.e_steps, step_no[0])
            dve.wait_ge(s.g_added, NCH)
            dve.tensor_copy(first[:, :].unsqueeze(2), XT[:, :].rearrange("p (b t) -> p b t", b=B)[:, :, 0:1])\
                .then_inc(s.e_first, 1)
            dve.wait_ge(s.e_loaded, 16 * 9)
            tw = typew[:, :].rearrange("p (t e) -> p t e", t=TYPES)
            ordered(dve.tensor_reduce(typem[:, :], tw, AX.X, ALU.max))
            ordered(dve.tensor_tensor(tw, tw, over(typem[:, :], [P, TYPES, 4], 2), ALU.subtract))
            ordered(dve.tensor_scalar(typew[:, :], typew[:, :], 10.0, None, ALU.mult))
            dve.sem_inc(s.e_type_arg, 1)
            dve.wait_ge(s.e_type_exp, 1)
            ordered(dve.tensor_reduce(typem[:, :], tw, AX.X, ALU.add))
            ordered(dve.reciprocal(typem[:, :], typem[:, :]))
            ordered(dve.tensor_tensor(tw, tw, over(typem[:, :], [P, TYPES, 4], 2), ALU.mult))
            ordered(dve.tensor_copy(typef[:, :], typei[:, :]))
            for t in range(TYPES):
                ins = dve.tensor_scalar(is_type[:, :, t], typef[:, :], float(t), None, ALU.is_equal)
                ordered(ins)
            for i in range(2):
                ordered(dve.tensor_tensor(pick[:, 0:B * TYPES].rearrange("p (b t) -> p b t", b=B), is_type[:, :, :],
                                          over(typew[:, i:i + 11:5], [P, B, TYPES], 1), ALU.mult))
                ordered(dve.tensor_reduce(scale5[:, :, i], pick[:, 0:B * TYPES].rearrange("p (b t) -> p b t", b=B),
                                          AX.X, ALU.add))
            ordered(dve.memset(expw[:, :], 0.0))
            ew = expw[:, :].rearrange("p (e b) -> p e b", e=4)
            for t in range(TYPES):
                for i in range(2):
                    ordered(dve.scalar_tensor_tensor(ew[:, t + i, :], is_type[:, :, t], typew[:, 5 * t + i:5 * t + i + 1],
                                                     ew[:, t + i, :], ALU.mult, ALU.add))
            dve.wait_ge(s.e_gate_h, 1)
            dve.tensor_scalar(gate_h[:, :], bank[0][:, 0:NEXP * FJ * B], 0.0, None, ALU.max).then_inc(s.e_gate_relu, 1)
            dve.wait_ge(s.e_gate_o, 1)
            ordered(dve.tensor_tensor(pick[:, 0:4 * B], bank[1][:, 0:4 * B], expw[:, :], ALU.mult))
            dve.tensor_reduce(gate_in[:, 0:B], pick[:, 0:4 * B].rearrange("p (e b) -> p b e", e=4), AX.X, ALU.add)\
                .then_inc(s.e_gate_in, 1)
            dve.tensor_copy(gate_in[:, B:4 * B], bank[1][:, 4 * B:7 * B]).then_inc(s.e_gate_in, 1)
            dve.wait_ge(s.e_gate_hid, 1)
            dve.tensor_scalar(gate_hid[:, :], bank[2][:, 0:B], 0.0, None, ALU.max).then_inc(s.e_gate_hid_relu, 1)
            dve.wait_ge(s.e_gate_logit, 1)
            ordered(dve.tensor_reduce(gate_max[:, :], bank[3][0:B, 0:4], AX.X, ALU.max))
            ordered(dve.tensor_scalar(gate_p[:, :], bank[3][0:B, 0:4], gate_max[:, :], None, ALU.subtract))
            dve.sem_inc(s.e_gate_arg, 1)
            dve.wait_ge(s.e_gate_exp, 1)
            ordered(dve.tensor_reduce(gate_max[:, :], gate_p[:, :], AX.X, ALU.add))
            ordered(dve.reciprocal(gate_max[:, :], gate_max[:, :]))
            ordered(dve.tensor_scalar(gate_p[:, :], gate_p[:, :], gate_max[:, :], None, ALU.mult))
            dve.tensor_tensor(gate_diag[:, :].rearrange("p (b k) -> p b k", b=B), over(gate_p[:, :], [B, B, 4], 1),
                              over(ident[0:B, 0:B], [B, B, 4], 2), ALU.mult).then_inc(s.e_gate_diag, 1)
            dve.wait_ge(s.e_gate_all, 1)
            ga_ = bank[4][:, 0:4 * B].rearrange("p (b k) -> p b k", b=B)
            ordered(dve.tensor_copy(scale5[:, :, 2:5], ga_[:, :, 1:4]))
            dve.tensor_tensor(scale5[:, :, 0:2], scale5[:, :, 0:2], ga_[:, :, 0:1].to_broadcast([P, B, 2]), ALU.mult)\
                .then_inc(s.e_scales, 1)

        def gate_act(act):
            act.wait_ge(s.e_type_arg, 1)
            act.activation(typew[:, :], typew[:, :], ACT.Exp).then_inc(s.e_type_exp, 1)
            act.wait_ge(s.e_gate_arg, 1)
            act.activation(gate_p[:, :], gate_p[:, :], ACT.Exp).then_inc(s.e_gate_exp, 1)


        def experts_pe(pe, i):
            def up(u, x):
                job = i * 10 + u * 5 + x
                parity = (u * 5 + x) % 2
                if x == 0:
                    pe.wait_ge(s.e_chosen, i * 4 + u * 2 + 2)
                pe.wait_ge(s.e_relu, job - 1 + E_FREE)
                w = e_sel[u][:, x * F:(x + 1) * F] if x < 2 else up_of(2 + x)
                for j in range(FJ):
                    mm = pe.matmul(bank[parity][:, j * P:(j + 1) * P], w[:, j * P:(j + 1) * P],
                                   XT[:, bass.ds((i * 2 + u) * P, P)], start=True, stop=True)
                mm.then_inc(s.e_up, 1)

            def down(u, x):
                job = i * 10 + u * 5 + x
                parity = (u * 5 + x) % 2
                pe.wait_ge(s.e_relu, job + 1 + E_FREE)
                if x == 0:
                    pe.wait_ge(s.e_moved, i * 2 + u - 1 + E_FREE)
                w = e_sel[u][:, (2 + x) * F:(3 + x) * F].rearrange("p (j e) -> p j e", j=FJ) if x < 2 else down_of(2 + x)
                for j in range(FJ):
                    mm = pe.matmul(bank[2 + u][:, 0:P], w[:, j, :], e_h[parity][:, j * P:(j + 1) * P],
                                   start=(x == 0 and j == 0), stop=(x == 4 and j == FJ - 1))
                mm.then_inc(s.e_down, 1)
            jobs = [(u, x) for u in range(2) for x in range(5)]
            up(*jobs[0])
            for n, job in enumerate(jobs):
                if n + 1 < len(jobs):
                    up(*jobs[n + 1])
                down(*job)

        def experts_relu(eng, i, mine):
            for u in range(2):
                for x in range(5):
                    job, parity = i * 10 + u * 5 + x, (u * 5 + x) % 2
                    if parity != mine:
                        continue
                    eng.wait_ge(s.e_up, job + 1)
                    eng.wait_ge(s.e_relu, job + E_FREE)
                    eng.wait_ge(s.e_down, job - 1 + E_DOWN)
                    if x <= 1:
                        eng.wait_ge(s.e_scaled, i * 2 + u + 1)
                    if mine:
                        eng.tensor_scalar(e_h[parity][:, :], bank[parity][:, :], e_scale[u][:, x:x + 1], 0.0,
                                          ALU.mult, ALU.max).then_inc(s.e_relu, 1)
                    else:
                        eng.activation(e_h[parity][:, :], bank[parity][:, :], ACT.Relu,
                                       scale=e_scale[u][:, x:x + 1]).then_inc(s.e_relu, 1)
                if mine:
                    eng.wait_ge(s.e_down, i * 10 + u * 5 + 5 + E_DOWN)
                    eng.tensor_copy(ZT[:, bass.ds((i * 2 + u) * P, P)], bank[2 + u][:, 0:P]).then_inc(s.e_moved, 1)

        def experts_scale(dve, i):
            for u in range(2):
                dve.tensor_copy(e_scale[u][:, :].unsqueeze(1), scale5[:, bass.ds(i * 2 + u, 1), :])\
                    .then_inc(s.e_scaled, 1)

        def experts_pool(pool, i):
            for u in range(2):
                b = i * 2 + u
                pool.wait_ge(s.e_down, b * 5 - 8 + E_DOWN)
                who = pool.value_load(etype[0:1, bass.ds(b, 1)], min_val=0, max_val=TYPES - 1)
                pool.tensor_copy(e_sel[u][:, 0:2 * F], e_up_w[:, bass.ds(who * F, 2 * F)]).then_inc(s.e_chosen, 1)
                pool.tensor_copy(e_sel[u][:, 2 * F:4 * F], e_down_w[:, bass.ds(who * F, 2 * F)]).then_inc(s.e_chosen, 1)


        def moe_pe(pe, c):
            pe.wait_ge(s.m_copied, c + 1)
            for j in range(CH):
                mm = pe.matmul(bank[0][:, j * ME:(j + 1) * ME], m_src[:, j * P:(j + 1) * P], m_gate[:, :],
                               start=True, stop=True)
            mm.then_inc(s.m_logit, 1)
            pe.wait_ge(s.m_onehot, c + 1)
            for j in range(CH):
                mm = pe.transpose(bank[1][0:ME, j * P:(j + 1) * P], m_hot[:, j * ME:(j + 1) * ME], ident[:, :])
            mm.then_inc(s.m_turned, 1)
            pe.wait_ge(s.m_hot, 2 * c + 2)
            y = scores[:, 0, :]
            pe.matmul(y, m_b2[:, :], m_hotT[:, :], start=True, stop=False)

            def up(e):
                if e >= 2:
                    pe.wait_ge(s.m_masked, c * ME + e - 1)
                pe.matmul(bank[2 + e % 2][:, :], m_w1[:, e * P:(e + 1) * P], m_src[:, :], start=True, stop=True)
                pe.matmul(bank[4 + e % 2][:, :], m_pick[:, e * P:(e + 1) * P], m_hot16[:, :], start=True, stop=True)\
                    .then_inc(s.m_up, 1)
            up(0)
            for e in range(ME):
                if e + 1 < ME:
                    up(e + 1)
                pe.wait_ge(s.m_masked, c * ME + e + 1)
                mm = pe.matmul(y, m_w2[:, e * P:(e + 1) * P], m_h[e % 2][:, :], start=False, stop=(e == ME - 1))
            mm.then_inc(s.m_y, 1)

        def moe_dve(dve, c):
            at = bass.ds(c * CW, CW)
            step_no = [0]

            def ordered(ins):
                step_no[0] += 1
                ins.then_inc(s.m_steps, 1)
                dve.wait_ge(s.m_steps, c * 3 + step_no[0])
            by_seq = lambda ap: ap.rearrange("p (b e) -> p b e", b=CH)
            dve.tensor_copy(m_src[:, :], ZT[:, at]).then_inc(s.m_copied, 1)
            dve.wait_ge(s.m_logit, c + 1)
            ordered(dve.tensor_tensor(by_seq(m_logits[:, :]), by_seq(bank[0][:, 0:CH * ME]),
                                      over(m_gate_b[:, :], [P, CH, ME], 1), ALU.add))
            ordered(dve.tensor_reduce(m_max[:, :], by_seq(m_logits[:, :]), AX.X, ALU.max))
            dve.tensor_tensor(by_seq(m_logits[:, :]), by_seq(m_logits[:, :]), over(m_max[:, :], [P, CH, ME], 2),
                              ALU.is_equal).then_inc(s.m_equal, 1)
            dve.wait_ge(s.m_equal, c + 1)
            ordered(dve.tensor_tensor(by_seq(m_logits[:, :]), by_seq(m_logits[:, :]), over(m_rank[:, :], [P, CH, ME], 1),
                                      ALU.mult))
            dve.tensor_reduce(m_max[:, :], by_seq(m_logits[:, :]), AX.X, ALU.max).then_inc(s.m_first, 1)
            dve.wait_ge(s.m_first, c + 1)
            dve.tensor_tensor(by_seq(m_hot[:, :]), by_seq(m_logits[:, :]), over(m_max[:, :], [P, CH, ME], 2),
                              ALU.is_equal).then_inc(s.m_onehot, 1)
            dve.wait_ge(s.m_turned, c + 1)
            dve.tensor_copy(m_hotT[:, :], bank[1][0:ME, :]).then_inc(s.m_hot, 1)
            dve.tensor_copy(m_hot16[:, :], bank[1][0:ME, :]).then_inc(s.m_hot, 1)
            for e in range(ME):
                dve.wait_ge(s.m_gelu, c * ME + e + 1)
                dve.tensor_tensor(m_h[e % 2][:, :], m_g[e % 2][:, :], bank[4 + e % 2][:, :], ALU.mult)\
                    .then_inc(s.m_masked, 1)
            dve.wait_ge(s.m_y, c + 1)
            dve.tensor_tensor(XT[:, at], XT[:, at], scores[:, 0, :], ALU.add).then_inc(s.m_added, 1)

        def moe_act(act, c):
            for e in range(ME):
                act.wait_ge(s.m_up, c * ME + e + 1)
                if e >= 2:
                    act.wait_ge(s.m_masked, c * ME + e - 1)
                act.activation(m_g[e % 2][:, :], bank[2 + e % 2][:, :], ACT.Gelu,
                               bias=cols[:, R_MB1 + e:R_MB1 + e + 1]).then_inc(s.m_gelu, 1)

        @block.tensor
        def _(pe):
            pe.wait_ge(s.x_loaded, 32)
            pe.wait_ge(s.const_loaded, 16 * 7)
            for c in range(NCH):
                if c >= 2:
                    pe.wait_ge(s.x_state, c - 1)
                for j in range(CH):
                    mm = pe.transpose(qk_ps[c % 2][:, j * P:(j + 1) * P], xin[:, CH * c + j, :], ident[:, :])
                mm.then_inc(s.x_turned, 1)
            for c in range(2):
                for j in range(4):
                    mm = pe.transpose(scores[:, c, j * P:(j + 1) * P], cond_in[:, 4 * c + j, :], ident[:, :])
                mm.then_inc(s.cond_turned, 1)
            pe.wait_ge(s.small_loaded, 16 * 13)
            pe.transpose(pT_ps[:, 0:ROWS], rows[:, :], ident[0:ROWS, 0:ROWS]).then_inc(s.cond_turned, 1)
            pe.wait_ge(s.cond_state, 4)
            pe.wait_ge(s.x_state, NCH)
            pe.wait_ge(s.wqkv_loaded, 16 * 9)
            pe.wait_ge(s.wo_loaded, 16)
            attention_pass(pe, pe_tick(pe, False), 0, 0)
            pe.wait_ge(a.added, B)
            pe.wait_ge(s.rg_consts, 1)
            pe.wait_ge(a.qkT_moved, TICKS)
            images(pe, pe_image(pe))
            pe.wait_ge(s.rg_summed, B * RG_CHUNKS)
            pe.wait_ge(s.rg_consts, 9)
            with pe.Fori(0, DEPTH) as l:
                pe.wait_ge(s.wqkv_loaded, l * 48 + 16 * 12)
                pe.wait_ge(s.wo_loaded, l * 16 + 32)
                ahead, rest = ffn_pe(pe, l)
                attention_pass(pe, pe_tick(pe, True), (l + 1) * TICKS, (l + 1) * B, ahead)
                rest()
            pe.wait_ge(s.lf_state, DEPTH * NCH)
            pe.wait_ge(s.x_final, NCH)
            pe.wait_ge(s.g_loaded, 16 * 15)
            with pe.Fori(0, NCH) as c:
                gla_pe(pe, c)
            gate_pe(pe)
            pe.sem_inc(s.e_down, E_DOWN)
            with pe.Fori(0, B // 2) as i:
                experts_pe(pe, i)
            pe.wait_ge(s.m_loaded, 16 * 6)
            with pe.Fori(0, NCH) as c:
                moe_pe(pe, c)
            pe.wait_ge(s.m_added, NCH)
            for c in range(NCH):
                if c >= 2:
                    pe.wait_ge(s.out_ready, c - 1)
                for j in range(CH):
                    mm = pe.transpose(qk_ps[c % 2][:, j * P:(j + 1) * P], XT[:, (CH * c + j) * P:(CH * c + j + 1) * P],
                                      ident[:, :])
                mm.then_inc(s.out_turned, 1)

        @block.vector
        def _(dve):
            dve.memset(rows[:, :], 0.0).then_inc(s.rows_zeroed, 1)
            dve.memset(ones[:, :], 1.0).then_inc(s.rg_consts, 1)
            dve.memset(mean_w[:, :], 1.0 / P).then_inc(s.rg_consts, 1)
            dve.memset(xs[0][HALF:P, 0:1], 0.0).then_inc(s.rg_consts, 1)
            dve.memset(xs[1][HALF:P, 0:1], 0.0).then_inc(s.rg_consts, 1)
            for i in range(2):
                dve.memset(xf[i][HALF:P, :].rearrange("p (b t) -> p b t", b=CH)[:, :, 0:1], 0.0)\
                    .then_inc(s.rg_consts, 1)
            dve.wait_ge(s.const_loaded, 16 * 7)
            dve.tensor_copy(ident16[:, :], ident[:, :]).then_inc(s.rg_consts, 1)
            dve.tensor_copy(local_mask[:, :], mask_wide).then_inc(s.rg_consts, 1)
            dve.tensor_copy(m_pick[:, :], pick_wide).then_inc(s.rg_consts, 1)
            for c in range(NCH):
                dve.wait_ge(s.x_turned, c + 1)
                dve.tensor_copy(XT[:, c * CW:(c + 1) * CW], qk_ps[c % 2][:, :]).then_inc(s.x_state, 1)
            for c in range(2):
                dve.wait_ge(s.cond_turned, c + 1)
                dve.tensor_copy(condT[:, 4 * c:4 * c + 4, 0:P], scores[:, c, :].rearrange("p (s o) -> p s o", s=4))\
                    .then_inc(s.cond_state, 1)
            dve.wait_ge(s.cond_turned, 3)
            dve.tensor_copy(cols[:, :], pT_ps[:, 0:ROWS]).then_inc(s.cond_state, 1)
            dve.wait_ge(s.cond_state, 3)
            dve.tensor_copy(condT[:, :, P:P + 1], cols[:, R_CB:R_CB + SUBJ].unsqueeze(2)).then_inc(s.cond_state, 1)
            dve.wait_ge(s.l0bias_loaded, 16 * 5)
            attention_pass(dve, dve_tick(dve, False), 0, 0)
            dve.wait_ge(s.rg_params, 96)
            small = [0]

            def seq(ins):
                small[0] += 1
                ins.then_inc(s.rg_steps, 1)
                dve.wait_ge(s.rg_steps, small[0])
            seq(dve.tensor_scalar(phase[:, 0, :], angle[:, :], np.pi / 2, None, ALU.add))
            seq(dve.tensor_copy(phase[:, 1, :], angle[:, :]))
            seq(dve.tensor_scalar(turns[:, :, :], phase[:, :, :], 1 / (2 * np.pi), ROUND, ALU.mult, ALU.add))
            seq(dve.tensor_scalar(turns[:, :, :], turns[:, :, :], -ROUND, None, ALU.add))
            for part in TWO_PI:
                seq(dve.scalar_tensor_tensor(phase[:, :, :], turns[:, :, :], -part, phase[:, :, :],
                                             ALU.mult, ALU.add))
            dve.tensor_scalar(phase[:, :, :], phase[:, :, :], PI_BELOW, -PI_BELOW, ALU.min, ALU.max)\
                .then_inc(s.rg_tables, 1)
            dve.wait_ge(s.rg_wave, 1)
            seq(dve.tensor_scalar(step[:, 0:2, :], wave[:, :, :], GRID, None, ALU.mult))
            seq(dve.tensor_scalar(step[:, 2, :], wave[:, 1, :], -GRID, None, ALU.mult))
            seq(dve.tensor_scalar(shift[:, :, :], offset[:, :, :], GRID, CENTRE, ALU.mult, ALU.add))
            seq(dve.tensor_scalar(y_of_column[:, :], step[:, 0, :], grid_part[:, :], None, ALU.mult))
            seq(dve.tensor_tensor(y_of_column[:, :], y_of_column[:, :], shift[:, :, 0], ALU.add))
            with dve.Fori(0, B) as b:
                def per_image(out, k, add):
                    return dve.tensor_scalar(out[:, bass.ds(b * P, P)], grid[:, :], step[:, k, bass.ds(b, 1)],
                                             add, ALU.mult, ALU.add)
                per_image(rg_xcol, 1, negpart[:, 0:1])
                per_image(rg_xrow, 0, shift[:, bass.ds(b, 1), 1])
                per_image(rg_yrow, 2, y_of_column[:, bass.ds(b, 1)]).then_inc(s.rg_tables, 1)
            dve.wait_ge(s.rg_tables, B + 1)
            images(dve, dve_image(dve))
            for of_local in (a.summed, a.clamped, a.normed, a.roped_c):
                dve.sem_inc(of_local, TICKS)
            with dve.Fori(0, DEPTH) as l:
                if_scale = qkscale[:, bass.ds(l, 1), :, :].rearrange("p l i e -> p (l i) e")
                dve.tensor_tensor(tabc[:, :, :], ropec[:, :, :], if_scale, ALU.mult).then_inc(s.tables_ready, 1)
                for f in range(2):
                    mine, other = slice(f * HD // 2, (f + 1) * HD // 2), slice((1 - f) * HD // 2, (2 - f) * HD // 2)
                    dve.tensor_tensor(tabs[:, :, mine], ropes[:, :, mine], if_scale[:, :, other], ALU.mult)\
                        .then_inc(s.tables_ready, 1)
                dve.wait_ge(s.tables_ready, l * 3 + 3)
                dve.tensor_copy(gate_b[:, :].unsqueeze(2), cols[:, R_B1 + 3 * DEPTH:ROWS]
                                .rearrange("p (j l) -> p j l", l=DEPTH)[:, :, bass.ds(l, 1)]).then_inc(s.lf_bias, 1)
                ahead, rest = ffn_dve(dve, l)
                attention_pass(dve, dve_tick(dve, True), (l + 1) * TICKS, (l + 1) * B, ahead)
                rest()
            for c in range(NCH):
                at = slice(c * CW, (c + 1) * CW)
                dve.wait_ge(s.lf_state, (DEPTH - 1) * NCH + c + 1)
                dve.tensor_tensor(XT[:, at], XT[:, at], ZT[:, at], ALU.add).then_inc(s.x_final, 1)
            dve.wait_ge(s.x_final, NCH)
            dve.wait_ge(s.g_loaded, 16 * 15)
            with dve.Fori(0, NCH) as c:
                gla_dve(dve, c)
            gate_dve(dve)
            dve.wait_ge(s.e_scales, 1)
            dve.sem_inc(s.e_relu, E_FREE)
            dve.sem_inc(s.e_moved, E_FREE)
            with dve.Fori(0, B // 2) as i:
                experts_scale(dve, i)
                experts_relu(dve, i, 1)
            dve.wait_ge(s.e_moved, B + E_FREE)
            dve.wait_ge(s.m_loaded, 16 * 6)
            with dve.Fori(0, NCH) as c:
                moe_dve(dve, c)
            dve.wait_ge(s.m_added, NCH)
            for c in range(NCH):
                dve.wait_ge(s.out_turned, c + 1)
                dve.tensor_copy(ZT[:, c * CW:(c + 1) * CW], qk_ps[c % 2][:, :]).then_inc(s.out_ready, 1)

        @block.scalar
        def _(act):
            attention_pass(act, act_tick(act, False), 0, 0)
            act.wait_ge(s.rg_tables, 1)
            act.activation(wave[:, :, :], phase[:, :, :], ACT.Sin).then_inc(s.rg_wave, 1)
            images(act, act_image(act))
            act.wait_ge(s.rg_summed, B * RG_CHUNKS)
            act.sem_inc(a.squared, TICKS)
            with act.Fori(0, DEPTH) as l:
                ahead, rest = ffn_act(act, l)
                attention_pass(act, act_tick(act, True), (l + 1) * TICKS, (l + 1) * B, ahead)
                rest()
                act.wait_ge(s.lf_state, l * NCH + NCH)
            with act.Fori(0, NCH) as c:
                gla_act(act, c)
            gate_act(act)
            with act.Fori(0, B // 2) as i:
                experts_relu(act, i, 0)
            with act.Fori(0, NCH) as c:
                moe_act(act, c)

        @block.gpsimd
        def _(pool):
            pool.memset(neg_half[:, :], -0.5).then_inc(s.consts_set, 1)
            pool.wait_ge(s.ids_loaded, 16)
            pool.wait_ge(s.cond_state, 4)
            attention_pass(pool, pool_tick(pool, False), 0, 0)
            pool.wait_ge(s.rg_tables, B + 1)
            images(pool, pool_image(pool))
            for of_local in (a.rs_ready, a.roped_s):
                pool.sem_inc(of_local, TICKS)
            with pool.Fori(0, DEPTH) as l:
                ahead, rest = ffn_pool(pool, l)
                attention_pass(pool, pool_tick(pool, True, l), (l + 1) * TICKS, (l + 1) * B, ahead)
                rest()
            with pool.Fori(0, NCH) as c:
                gla_pool(pool, c)
            pool.wait_ge(s.e_loaded, 16 * 9)
            with pool.Fori(0, B // 2) as i:
                experts_pool(pool, i)


def constants():
    f = np.float32
    tok = np.arange(P)
    half = np.arange(0, HD, 2, dtype=np.float64)
    freqs = tok[:, None] / 10000.0 ** (half / HD)[None, :]
    scale = ((half + 0.4 * HD) / (1.4 * HD))[None, :] ** ((tok - P // 2) / (WINDOW // 2))[:, None]
    two = lambda t: np.concatenate([t, t], 1)
    qk = np.stack([8.0 * two(scale), 1.0 / two(scale)], 1)
    sign = np.where(np.arange(HD) < HD // 2, -1.0, 1.0)
    lag = tok[:, None] - tok[None, :]
    lap = np.eye(P, k=1) + np.eye(P, k=-1) - 2 * np.eye(P)
    lap[0, 1] = lap[P - 1, P - 2] = 2.0
    seen = (tok[:, None] <= tok[None, :])
    return {
        "c_lap": lap.T.astype(f).copy(),
        "c_pick": np.repeat(np.eye(ME), P, axis=1).astype(f),
        "c_rank": np.broadcast_to((ME - np.arange(ME)).astype(f), (P, ME)).copy(),
        "c_restart": np.broadcast_to((np.arange(CW) % HALF != 0).astype(f), (P, CW)).copy(),
        "c_gmask": seen.astype(f),
        "c_headmask": (tok[:, None] // GLK == np.arange(GLH)[None, :]).astype(f),
        "c_ident": np.eye(P, dtype=f),
        "c_local_mask": np.where((lag >= 0) & (lag <= WINDOW), 0.0, MASKED).astype(f),
        "c_keep": (lag >= 0).astype(f),
        "c_fill": np.where(lag < 0, f(FILL) * f(HD ** 0.5), 0).astype(f),
        "c_grid": np.broadcast_to((tok - P / 2).astype(f), (P, P)).copy(),
        "c_minus_index": np.broadcast_to(-tok.astype(f), (P, P)).copy(),
        "c_grid_part": (tok[:, None] - P / 2).astype(f),
        "c_negpart": -tok[:, None].astype(f),
        "c_ropec": (two(np.cos(freqs))[:, None, :] * qk).astype(f),
        "c_ropes": ((two(np.sin(freqs)) * sign)[:, None, :] * qk).astype(f),
    }


def kernel(**inputs):
    import concourse.bacc as bacc
    from concourse.bass_utils import run_bass_kernel_spmd

    nc = bacc.Bacc("TRN2", target_bir_lowering=False, num_devices=1)
    arrays, drams = {}, {}
    for name, a in {**inputs, **constants()}.items():
        a = np.ascontiguousarray(a)
        arrays[f"in_{name}"] = a
        drams[name] = nc.dram_tensor(f"in_{name}", a.shape, mybir.dt.from_np(a.dtype), kind="ExternalInput").ap()
    out = nc.dram_tensor("out", (B, P, P), F32, kind="ExternalOutput").ap()
    build(nc, drams, out)
    r = run_bass_kernel_spmd(nc, [arrays], core_ids=[0])
    return r.results[0]["out"]
```
